# Optimizing a Trainium2 kernel written in Bass

```python
import numpy as np
import jax
import jax.numpy as jnp

def _softmax(x, axis=-1):
    return jax.nn.softmax(x, axis=axis)

def _gelu(x):
    return jax.nn.gelu(x, approximate=True)

def _silu(x):
    return jax.nn.silu(x)

def _sigmoid(x):
    return jax.nn.sigmoid(x)

def _layernorm(x, axis=-1, eps=1e-05):
    m = jnp.mean(x, axis=axis, keepdims=True)
    v = jnp.var(x, axis=axis, keepdims=True)
    return (x - m) / jnp.sqrt(v + eps)

def _scatter_add(tgt, idx, src, axis=0):
    return tgt.at[idx].add(src)

def _segment_sum(src, seg, n):
    return jax.ops.segment_sum(src, seg, n)
kernel_name = 'mk_gps_d1_gnn_r64_7f28a4'

def setup_inputs(seed: int=0):
    np.random.seed(seed)
    _w = jnp.asarray

    def _rec_inputs():
        import jax
        import jax.numpy as jnp
        _gk = jax.random.key(seed)
        x = -8.776e-05 + 1 * jax.random.normal(jax.random.fold_in(_gk, 1), (10000, 512), jnp.float32)
        _s = jax.random.randint(jax.random.fold_in(_gk, 2), (1250,), 0, 10000, jnp.int32)
        _d = jax.random.randint(jax.random.fold_in(_gk, 3), (1250,), 0, 10000, jnp.int32)
        _loop = jnp.arange(10000, dtype=jnp.int32)
        src = jnp.concatenate([_s, _d, _loop])
        dst = jnp.concatenate([_d, _s, _loop])
        _o = jnp.argsort(dst, stable=True)
        src = src[_o]
        dst = dst[_o]
        return (x, src, dst)
    x, src, dst = _rec_inputs()

    def _L0_gnn_setup():
        import jax, jax.numpy as jnp
        import numpy as np
        N = 10000
        E = 2500
        H = 4
        C = 256
        D_IN = 512
        D_OUT = 512
        NEG_SLOPE = 0.2

        def gat_conv(x, src, dst, W, a_src, a_dst, bias):
            n = x.shape[0]
            h = (x @ W).reshape(n, H, C)
            al_s = jnp.einsum('nhc,hc->nh', h, a_src)
            al_d = jnp.einsum('nhc,hc->nh', h, a_dst)
            e = jax.nn.leaky_relu(al_s[src] + al_d[dst], NEG_SLOPE)
            emax = jax.ops.segment_max(e, dst, num_segments=n)
            w = jnp.exp(e - emax[dst])
            denom = jax.ops.segment_sum(w, dst, num_segments=n)
            alpha = w / denom[dst]
            out = jax.ops.segment_sum(h[src] * alpha[:, :, None], dst, num_segments=n)
            return out.reshape(n, H * C) + bias
        key = jax.random.key(seed)
        ks = jax.random.split(key, 13)
        s = 0.05
        return {'x': jax.random.normal(ks[0], (N, D_IN), jnp.float32), 'edge_index': jax.random.randint(ks[1], (2, E), 0, N, dtype=jnp.int32), 'W1': jax.random.normal(ks[2], (D_IN, H * C), jnp.float32) * s, 'a_src1': jax.random.normal(ks[3], (H, C), jnp.float32) * s, 'a_dst1': jax.random.normal(ks[4], (H, C), jnp.float32) * s, 'b1': jnp.zeros((H * C,), jnp.float32), 'W2': jax.random.normal(ks[5], (H * C, H * C), jnp.float32) * s, 'a_src2': jax.random.normal(ks[6], (H, C), jnp.float32) * s, 'a_dst2': jax.random.normal(ks[7], (H, C), jnp.float32) * s, 'b2': jnp.zeros((H * C,), jnp.float32), 'Wfc': jax.random.normal(ks[8], (H * C, D_OUT), jnp.float32) * s, 'bfc': jnp.zeros((D_OUT,), jnp.float32)}
    _L0_gnn_all = _L0_gnn_setup()
    _L0_gnn_in = {k: v for k, v in _L0_gnn_all.items() if k in ('W1', 'a_src1', 'a_dst1', 'b1', 'W2', 'a_src2', 'a_dst2', 'b2', 'Wfc', 'bfc')}
    del _L0_gnn_all

    def _L0_mix_setup():
        import jax, jax.numpy as jnp
        import numpy as np
        HEADS = 8
        EPS_LN = 1e-05
        EPS_NORM = 1e-08
        key = jax.random.key(seed)
        ks = jax.random.split(key, 3)
        B, N, C = (4, 128, 512)
        x = jax.random.normal(ks[0], (B, N, C), dtype=jnp.float32)
        qkv_w = jax.random.normal(ks[1], (3 * C, C), dtype=jnp.float32) / np.sqrt(C)
        qkv_b = jnp.zeros((3 * C,), dtype=jnp.float32)
        out_w = jax.random.normal(ks[2], (C, C), dtype=jnp.float32) / np.sqrt(C)
        out_b = jnp.zeros((C,), dtype=jnp.float32)
        ln_gamma = jnp.ones((C,), dtype=jnp.float32)
        ln_beta = jnp.zeros((C,), dtype=jnp.float32)
        return {'x': x, 'qkv_w': qkv_w, 'qkv_b': qkv_b, 'out_w': out_w, 'out_b': out_b, 'ln_gamma': ln_gamma, 'ln_beta': ln_beta}
    _L0_mix_all = _L0_mix_setup()
    _L0_mix_in = {k: v for k, v in _L0_mix_all.items() if k in ('qkv_w', 'qkv_b', 'out_w', 'out_b', 'ln_gamma', 'ln_beta')}
    del _L0_mix_all

    def _L0_ffn_setup():
        import jax, jax.numpy as jnp
        import numpy as np
        import math
        E, K, CAPF = (8, 2, 1.25)
        D, DFF = (512, 32)

        def _moe(x, Wr, br, W1, b1, W2, b2):
            orig = x.shape
            d = orig[-1]
            xf = x.reshape(-1, d)
            N = xf.shape[0]
            logits = xf @ Wr + br
            probs = jax.nn.softmax(logits, axis=-1)
            topk_p, topk_i = jax.lax.top_k(probs, K)
            topk_w = topk_p / (jnp.sum(topk_p, axis=-1, keepdims=True) + 1e-09)
            cap = max(1, int(math.ceil(CAPF * float(N * K) / float(E))))
            flat_e = topk_i.reshape(-1)
            flat_w = topk_w.reshape(-1)
            tok = jnp.repeat(jnp.arange(N), K)
            one_hot = jax.nn.one_hot(flat_e, E, dtype=xf.dtype)
            pos = (jnp.cumsum(one_hot, axis=0) - one_hot)[jnp.arange(N * K), flat_e]
            pos = pos.astype(jnp.int32)
            keep = pos < cap
            w_k = jnp.where(keep, flat_w, 0.0)
            sum_w = jnp.zeros((N,), xf.dtype).at[tok].add(w_k)
            w_norm = w_k / (sum_w[tok] + 1e-09)
            slot = flat_e * cap + pos
            slot_safe = jnp.where(keep, slot, E * cap)
            expert_in = jnp.zeros((E * cap, d), xf.dtype).at[slot_safe].set(xf[tok], mode='drop').reshape(E, cap, d)
            h = jax.nn.gelu(jnp.einsum('ecd,edf->ecf', expert_in, W1) + b1[:, None, :], approximate=False)
            expert_out = (jnp.einsum('ecf,efd->ecd', h, W2) + b2[:, None, :]).reshape(E * cap, d)
            contrib = expert_out[jnp.where(keep, slot, 0)]
            y = jnp.zeros((N, d), xf.dtype).at[tok].add(contrib * w_norm[:, None])
            return y.reshape(orig)
        key = jax.random.key(seed)
        ks = jax.random.split(key, 5)
        s = lambda k, sh, sc: jax.random.normal(k, sh, jnp.float32) * sc
        return {'x': jax.random.normal(ks[0], (8, 64, D), jnp.float32), 'Wr': s(ks[1], (D, E), 1.0 / math.sqrt(D)), 'br': jnp.zeros((E,), jnp.float32), 'W1': s(ks[2], (E, D, DFF), 1.0 / math.sqrt(D)), 'b1': jnp.zeros((E, DFF), jnp.float32), 'W2': s(ks[3], (E, DFF, D), 1.0 / math.sqrt(DFF)), 'b2': jnp.zeros((E, D), jnp.float32)}
    _L0_ffn_all = _L0_ffn_setup()
    _L0_ffn_in = {k: v for k, v in _L0_ffn_all.items() if k in ('Wr', 'br', 'W1', 'b1', 'W2', 'b2')}
    del _L0_ffn_all
    return {'x': x, 'src': src, 'dst': dst, 'L0_gnn_W1': _L0_gnn_in['W1'], 'L0_gnn_a_src1': _L0_gnn_in['a_src1'], 'L0_gnn_a_dst1': _L0_gnn_in['a_dst1'], 'L0_gnn_b1': _L0_gnn_in['b1'], 'L0_gnn_W2': _L0_gnn_in['W2'], 'L0_gnn_a_src2': _L0_gnn_in['a_src2'], 'L0_gnn_a_dst2': _L0_gnn_in['a_dst2'], 'L0_gnn_b2': _L0_gnn_in['b2'], 'L0_gnn_Wfc': _L0_gnn_in['Wfc'], 'L0_gnn_bfc': _L0_gnn_in['bfc'], 'L0_mix_qkv_w': _L0_mix_in['qkv_w'], 'L0_mix_qkv_b': _L0_mix_in['qkv_b'], 'L0_mix_out_w': _L0_mix_in['out_w'], 'L0_mix_out_b': _L0_mix_in['out_b'], 'L0_mix_ln_gamma': _L0_mix_in['ln_gamma'], 'L0_mix_ln_beta': _L0_mix_in['ln_beta'], 'L0_ffn_Wr': _L0_ffn_in['Wr'], 'L0_ffn_br': _L0_ffn_in['br'], 'L0_ffn_W1': _L0_ffn_in['W1'], 'L0_ffn_b1': _L0_ffn_in['b1'], 'L0_ffn_W2': _L0_ffn_in['W2'], 'L0_ffn_b2': _L0_ffn_in['b2']}

def reference(x, src, dst, L0_gnn_W1, L0_gnn_a_src1, L0_gnn_a_dst1, L0_gnn_b1, L0_gnn_W2, L0_gnn_a_src2, L0_gnn_a_dst2, L0_gnn_b2, L0_gnn_Wfc, L0_gnn_bfc, L0_mix_qkv_w, L0_mix_qkv_b, L0_mix_out_w, L0_mix_out_b, L0_mix_ln_gamma, L0_mix_ln_beta, L0_ffn_Wr, L0_ffn_br, L0_ffn_W1, L0_ffn_b1, L0_ffn_W2, L0_ffn_b2):
    import jax
    import jax.numpy as jnp

    def _L0_gnn_ref(x, edge_index, W1, a_src1, a_dst1, b1, W2, a_src2, a_dst2, b2, Wfc, bfc):
        import jax, jax.numpy as jnp
        import numpy as np
        N = 10000
        E = 2500
        H = 4
        C = 256
        D_IN = 512
        D_OUT = 512
        NEG_SLOPE = 0.2

        def gat_conv(x, src, dst, W, a_src, a_dst, bias):
            n = x.shape[0]
            h = (x @ W).reshape(n, H, C)
            al_s = jnp.einsum('nhc,hc->nh', h, a_src)
            al_d = jnp.einsum('nhc,hc->nh', h, a_dst)
            e = jax.nn.leaky_relu(al_s[src] + al_d[dst], NEG_SLOPE)
            emax = jax.ops.segment_max(e, dst, num_segments=n)
            w = jnp.exp(e - emax[dst])
            denom = jax.ops.segment_sum(w, dst, num_segments=n)
            alpha = w / denom[dst]
            out = jax.ops.segment_sum(h[src] * alpha[:, :, None], dst, num_segments=n)
            return out.reshape(n, H * C) + bias
        loop = jnp.arange(N, dtype=edge_index.dtype)
        src = jnp.concatenate([edge_index[0], loop])
        dst = jnp.concatenate([edge_index[1], loop])
        h = jax.nn.relu(gat_conv(x, src, dst, W1, a_src1, a_dst1, b1))
        h = jax.nn.relu(gat_conv(h, src, dst, W2, a_src2, a_dst2, b2))
        return h @ Wfc + bfc

    def _L0_mix_ref(x, qkv_w, qkv_b, out_w, out_b, ln_gamma, ln_beta):
        import jax, jax.numpy as jnp
        import numpy as np
        HEADS = 8
        EPS_LN = 1e-05
        EPS_NORM = 1e-08
        B, N, C = x.shape
        h = HEADS
        d = C // h
        residual = x
        mu = jnp.mean(x, axis=-1, keepdims=True)
        var = jnp.var(x, axis=-1, keepdims=True)
        xn = (x - mu) / jnp.sqrt(var + EPS_LN) * ln_gamma + ln_beta
        qkv = xn @ qkv_w.T + qkv_b
        qkv = qkv.reshape(B, N, 3, h, d).transpose(2, 0, 3, 1, 4)
        q, k, v = (qkv[0], qkv[1], qkv[2])
        q = jax.nn.elu(q) + 1.0
        k = jax.nn.elu(k) + 1.0
        kv = jnp.einsum('bhnd,bhne->bhde', k, v)
        k_sum = jnp.sum(k, axis=2)
        out = jnp.einsum('bhnd,bhde->bhne', q, kv)
        normalizer = jnp.einsum('bhnd,bhd->bhn', q, k_sum)
        out = out / (normalizer[..., None] + EPS_NORM)
        out = out.transpose(0, 2, 1, 3).reshape(B, N, C)
        out = out @ out_w.T + out_b
        return out + residual

    def _L0_ffn_ref(x, Wr, br, W1, b1, W2, b2):
        import jax, jax.numpy as jnp
        import numpy as np
        import math
        E, K, CAPF = (8, 2, 1.25)
        D, DFF = (512, 32)

        def _moe(x, Wr, br, W1, b1, W2, b2):
            orig = x.shape
            d = orig[-1]
            xf = x.reshape(-1, d)
            N = xf.shape[0]
            logits = xf @ Wr + br
            probs = jax.nn.softmax(logits, axis=-1)
            topk_p, topk_i = jax.lax.top_k(probs, K)
            topk_w = topk_p / (jnp.sum(topk_p, axis=-1, keepdims=True) + 1e-09)
            cap = max(1, int(math.ceil(CAPF * float(N * K) / float(E))))
            flat_e = topk_i.reshape(-1)
            flat_w = topk_w.reshape(-1)
            tok = jnp.repeat(jnp.arange(N), K)
            one_hot = jax.nn.one_hot(flat_e, E, dtype=xf.dtype)
            pos = (jnp.cumsum(one_hot, axis=0) - one_hot)[jnp.arange(N * K), flat_e]
            pos = pos.astype(jnp.int32)
            keep = pos < cap
            w_k = jnp.where(keep, flat_w, 0.0)
            sum_w = jnp.zeros((N,), xf.dtype).at[tok].add(w_k)
            w_norm = w_k / (sum_w[tok] + 1e-09)
            slot = flat_e * cap + pos
            slot_safe = jnp.where(keep, slot, E * cap)
            expert_in = jnp.zeros((E * cap, d), xf.dtype).at[slot_safe].set(xf[tok], mode='drop').reshape(E, cap, d)
            h = jax.nn.gelu(jnp.einsum('ecd,edf->ecf', expert_in, W1) + b1[:, None, :], approximate=False)
            expert_out = (jnp.einsum('ecf,efd->ecd', h, W2) + b2[:, None, :]).reshape(E * cap, d)
            contrib = expert_out[jnp.where(keep, slot, 0)]
            y = jnp.zeros((N, d), xf.dtype).at[tok].add(contrib * w_norm[:, None])
            return y.reshape(orig)
        return _moe(x, Wr, br, W1, b1, W2, b2)
    edge_index = jnp.stack([src, dst])
    xn = _layernorm(x, axis=-1)
    x = x + _L0_gnn_ref(xn, edge_index, L0_gnn_W1, L0_gnn_a_src1, L0_gnn_a_dst1, L0_gnn_b1, L0_gnn_W2, L0_gnn_a_src2, L0_gnn_a_dst2, L0_gnn_b2, L0_gnn_Wfc, L0_gnn_bfc) + _L0_mix_ref(xn[None], L0_mix_qkv_w, L0_mix_qkv_b, L0_mix_out_w, L0_mix_out_b, L0_mix_ln_gamma, L0_mix_ln_beta)[0]
    x = x + _L0_ffn_ref(_layernorm(x, axis=-1)[None], L0_ffn_Wr, L0_ffn_br, L0_ffn_W1, L0_ffn_b1, L0_ffn_W2, L0_ffn_b2)[0]
    return x

_drawn_inputs = setup_inputs


def setup_inputs(seed=0):
    import zlib

    import numpy as np

    out = dict(_drawn_inputs(seed))
    spreads = {'L0_gnn_b1': (0.0, 0.1),
     'L0_gnn_b2': (0.0, 0.1),
     'L0_gnn_bfc': (0.0, 0.1),
     'L0_mix_qkv_b': (0.0, 0.1),
     'L0_mix_out_b': (0.0, 0.1),
     'L0_mix_ln_gamma': (1.0, 0.6),
     'L0_mix_ln_beta': (0.0, 0.1),
     'L0_ffn_br': (0.0, 0.1),
     'L0_ffn_b1': (0.0, 0.396),
     'L0_ffn_b2': (0.0, 0.1)}
    factors = {'L0_gnn_a_dst1': 2.723, 'L0_gnn_a_src2': 3.779, 'L0_gnn_a_dst2': 6.76}
    for name, (base, spread) in spreads.items():
        noise = np.random.default_rng([zlib.crc32(name.encode()), seed]).standard_normal(out[name].shape)
        drawn = base * np.exp(spread * noise) if base else spread * noise
        out[name] = jnp.asarray(drawn.astype(out[name].dtype))
    for name, factor in factors.items():
        out[name] = (out[name] * factor).astype(out[name].dtype)
    return out
```

```python
import concourse.bass as bass
from concourse import mybir
from contextlib import ExitStack

f32 = mybir.dt.float32
f32r = mybir.dt.float32r
bf16 = mybir.dt.bfloat16
i32 = mybir.dt.int32
ALU = mybir.AluOpType
ACT = mybir.ActivationFunctionType
AX = mybir.AxisListType

P = 128
N = 10000
D = 512
HC = 1024
HEADS = 4
C = HC // HEADS
NT = -(-N // P)
LAST = N - (NT - 1) * P
NPAD = NT * P
ALS, ALD, DEN = HC, HC + HEADS, HC + 2 * HEADS
ROW = HC + 3 * HEADS
WEXT = HC + 2 * HEADS
EP, EK = 125, 100
SLOTS = 64
NITEMS = -(-(NT + (EP * EK) // SLOTS + 4) // 4) * 4
IG = NITEMS // 4
PADSLOT = 16384 * 256 + 255
NEG = -1.0e30
LN_EPS = 1e-5
NE = 8
CAP = 3125
KD = D // P
KH = HC // P
GT = 4
NG = -(-NT // GT)
assert NITEMS % 4 == 0 and IG <= P


class Chain:

    def __init__(self, eng, sem):
        self.eng, self.sem, self.n, self.base = eng, sem, 0, 0

    def mark(self, ins):
        ins.then_inc(self.sem, 1)
        self.n += 1

    def sync(self):
        self.eng.wait_ge(self.sem, self.base + self.n)

    def link(self, ins):
        self.mark(ins)
        self.sync()


def semaphores(nc, stack, suffix=""):
    taken = []

    def clear():
        nc.clear_and_free_semaphores(taken)
        nc.all_engine_barrier()

    def sem(name):
        taken.append(nc.alloc_semaphore(name + suffix))
        return taken[-1]

    stack.callback(clear)
    return sem


def wait_apart(e, sem, value, carrier):
    e.wait_ge(sem, value)
    e.sem_inc(carrier, 1)


def build(nc, x, src, dst, W1, as1, ad1, b1, W2, as2, ad2, b2, Wfc, bfc, qkv_w, qkv_b, out_w, out_b,
          gamma, beta, Wr, br, fW1, fb1, fW2, fb2, out, stop_after=99, dbg=None):
    h1t = nc.dram_tensor("h1_table", (NPAD, ROW), f32)
    h2t = nc.dram_tensor("h2_table", (NPAD, ROW), f32)
    yt = nc.dram_tensor("gnn_out", (NPAD, D), f32)
    slots = nc.dram_tensor("slot_table", (NITEMS * SLOTS, 1), i32)
    keep = ExitStack()
    with keep:
        def ksb(name, shape, dt=f32):
            return keep.enter_context(nc.sbuf_tensor(name, shape, dt))

        K = {}
        K["ident"] = ksb("ident", [P, P])
        K["stat"] = ksb("stat", [P, NG * GT, 3])
        K["den0"] = ksb("den0", [P, NT])
        K["pos"] = ksb("pos", [P, EK], i32)
        K["val"] = ksb("val", [P, EK], i32)
        K["items"] = ksb("items", [1, 2 * NITEMS], i32)
        K["nitems"] = ksb("nitems", [1, 2], i32)
        K["iota"] = ksb("iota_node", [P, P])
        K["slot_src"] = ksb("slot_src", [SLOTS, NITEMS], i32)
        K["slot_dst"] = ksb("slot_dst", [SLOTS, NITEMS])
        K["bq"] = ksb("bq", [P, KD])
        K["kvT"] = ksb("kvT", [P, D])
        K["ksum"] = ksb("ksum", [P, KD])
        K["incl"] = ksb("incl", [P, P])
        dram = dict(h1t=h1t, h2t=h2t, yt=yt, slots=slots)
        edges(nc, K, src, dst, dram)
        if stop_after >= 1:
            with ExitStack() as st:
                wq = st.enter_context(nc.sbuf_tensor("wq", [P, 2, KD, D], f32r))
                dense_in(nc, K, wq, x, W1, as1, ad1, qkv_w, qkv_b, gamma, beta, dram)
                if stop_after >= 2:
                    gat(nc, K, 1, b1, W2, as2, ad2, dram["h1t"], dram["h2t"], dram)
                if stop_after >= 3:
                    gat(nc, K, 2, b2, Wfc, None, None, dram["h2t"], dram["yt"], dram)
                if stop_after >= 4:
                    tail(nc, K, wq, x, bfc, out_w, out_b, Wr, br, fW1, fb1, fW2, fb2, out, dram)
        if dbg:
            dbg(nc, K, dram)


def edges(nc, K, src, dst, dram):
    with ExitStack() as st:
        def sb(name, shape, dt=f32):
            return st.enter_context(nc.sbuf_tensor(name, shape, dt))

        sem = semaphores(nc, st)

        se = sb("src_i", [EP, EK], i32)
        de = sb("dst_i", [EP, EK], i32)
        ti = sb("tile_i", [EP, EK], i32)
        li = sb("local_i", [EP, EK], i32)
        sf, tf, lf, ed, te, tl, vf, pf = (sb(n, [EP, EK]) for n in (
            "src_f", "tile_f", "local_f", "is_edge", "tile_edge", "tile_loop", "val_f", "pos_f"))
        iot = sb("iota_tile", [P, NT])
        iop = K["iota"]
        oh = sb("edge_in_tile", [EP, NT, EK], bf16)
        ol = sb("loop_in_tile", [EP, NT, EK], bf16)
        on = sb("at_node", [EP, EK, P], bf16)
        rk = sb("rank", [P, NT, EK])
        low = sb("earlier", [P, P], bf16)
        one = sb("ones_b", [P, P], bf16)
        wrap = sb("not_first_col", [P, 5, EK])
        cnt = sb("tile_count", [P, NT])
        cnti = sb("tile_count_i", [P, NT], i32)
        end = sb("tile_end", [P, NT])
        base = sb("tile_base", [P, NT])
        itp = sb("item_number", [P, 4])
        tlt = sb("item_tile", [P, 4])
        cmp_ = sb("item_after", [P, NT])
        row = sb("item_row", [1, NITEMS])
        first = sb("item_first", [1, NITEMS])
        par = sb("item_parity", [1, NITEMS])
        offl = sb("item_base", [1, NITEMS])
        nn = sb("n_items_f", [1, 2])
        ni = sb("n_items_i", [1, 2], i32)
        pad = sb("pad_slots", [P, NITEMS * SLOTS // P], i32)
        zr = sb("zero_row", [P, NT])
        psa = st.enter_context(nc.psum_tensor("ps_rank", [P, 5 * EK], f32))
        psb = st.enter_context(nc.psum_tensor("ps_total", [P, 5 * EK], f32))
        psl = st.enter_context(nc.psum_tensor("ps_loops", [P, NT], f32))
        psi = st.enter_context(nc.psum_tensor("ps_items", [1, NITEMS], f32))

        loaded, consts, onehots, mm_done, evac, dv, loops_done, items_in, items_row, pads, padded = (sem(n) for n in (
            "edges_loaded", "edge_consts", "onehots_ready", "ranks_ready", "ranks_taken", "edges_dve", "loops_counted",
            "item_tiles_ready", "item_rows_ready", "pads_ready", "pads_stored"))
        pool = sem("edges_pool")
        chunks = [(a, min(a + 5, NT)) for a in range(0, NT, 5)]
        block = st.enter_context(nc.Block())

        @block.sync
        def _(e):
            e.dma_start(se[:, :], src.rearrange("(p k) -> p k", p=EP)).then_inc(loaded, 16)
            e.dma_start(de[:, :], dst.rearrange("(p k) -> p k", p=EP)).then_inc(loaded, 16)
            e.wait_ge(pads, 1)
            e.dma_start(dram["slots"].ap().rearrange("(p n) o -> p (n o)", p=P), pad[:, :]).then_inc(padded, 16)
            e.wait_ge(padded, 16)

        @block.gpsimd
        def _(e):
            pc = Chain(e, pool)
            e.memset(pad[:, :], PADSLOT).then_inc(pads, 1)
            pc.mark(e.memset(K["ident"][:, :], 0.0))
            pc.mark(e.memset(K["incl"][:, :], 1.0))
            pc.mark(e.memset(low[:, :], 0.0))
            pc.mark(e.memset(wrap[:, :, :], 1.0))
            pc.mark(e.memset(K["stat"][:, :, :], 0.0))
            pc.sync()
            pc.mark(e.affine_select(out=K["ident"][:, :], in_=K["ident"][:, :], compare_op=ALU.not_equal,
                                    fill=1.0, base=0, pattern=[[-1, P]], channel_multiplier=1))
            pc.mark(e.affine_select(out=K["incl"][:, :], in_=K["incl"][:, :], compare_op=ALU.is_gt,
                                    fill=0.0, base=0, pattern=[[1, P]], channel_multiplier=-1))
            pc.mark(e.affine_select(out=low[:, :], in_=low[:, :], compare_op=ALU.is_gt,
                                    fill=-1.0, base=0, pattern=[[1, P]], channel_multiplier=-1))
            pc.mark(e.memset(wrap[:, :, 0:1], 0.0))
            pc.mark(e.memset(one[:, :], 1.0))
            pc.mark(e.memset(zr[:, :], 1.0))
            pc.mark(e.iota(iot[:, :], pattern=[[1, NT]], base=0, channel_multiplier=0,
                           allow_small_or_imprecise_dtypes=True))
            pc.mark(e.iota(iop[:, :], pattern=[[1, P]], base=0, channel_multiplier=0,
                           allow_small_or_imprecise_dtypes=True))
            pc.mark(e.iota(itp[:, :], pattern=[[IG, 4]], base=0, channel_multiplier=1,
                           allow_small_or_imprecise_dtypes=True))
            pc.mark(e.iota(par[:, :].rearrange("p (a b) -> p a b", b=2), pattern=[[0, NITEMS // 2], [1, 2]],
                           base=0, channel_multiplier=0, allow_small_or_imprecise_dtypes=True))
            pc.sync()
            e.engine_nop().then_inc(consts, 1)

        @block.vector
        def _(e):
            c = Chain(e, dv)
            e.wait_ge(loaded, 32)
            e.wait_ge(consts, 1)
            c.mark(e.tensor_scalar(ti[:, :], de[:, :], 7, None, ALU.arith_shift_right))
            c.mark(e.tensor_scalar(li[:, :], de[:, :], 127, None, ALU.bitwise_and))
            c.mark(e.tensor_copy(sf[:, :], se[:, :]))
            c.mark(e.tensor_tensor(ed[:, :], se[:, :], de[:, :], ALU.not_equal))
            c.sync()
            c.mark(e.tensor_copy(tf[:, :], ti[:, :]))
            c.mark(e.tensor_copy(lf[:, :], li[:, :]))
            c.sync()
            c.mark(e.scalar_tensor_tensor(vf[:, :], sf[:, :], 256.0, lf[:, :], ALU.mult, ALU.add))
            c.mark(e.scalar_tensor_tensor(tl[:, :], ed[:, :], 1000.0, tf[:, :], ALU.mult, ALU.add))
            c.mark(e.tensor_scalar(te[:, :], ed[:, :], -1000.0, 1000.0, ALU.mult, ALU.add))
            c.sync()
            c.mark(e.tensor_copy(K["val"][0:EP, :], vf[:, :]))
            c.mark(e.tensor_tensor(te[:, :], te[:, :], tf[:, :], ALU.add))
            c.sync()
            e.tensor_tensor(oh[:, :, :], iot[0:EP, :].unsqueeze(2).to_broadcast([EP, NT, EK]),
                            te[:, :].unsqueeze(1).to_broadcast([EP, NT, EK]), ALU.is_equal).then_inc(onehots, 1)
            e.tensor_tensor(ol[:, :, :], iot[0:EP, :].unsqueeze(2).to_broadcast([EP, NT, EK]),
                            tl[:, :].unsqueeze(1).to_broadcast([EP, NT, EK]), ALU.is_equal).then_inc(onehots, 1)
            e.tensor_tensor(on[:, :, :], iop[0:EP, :].unsqueeze(1).to_broadcast([EP, EK, P]),
                            lf[:, :].unsqueeze(2).to_broadcast([EP, EK, P]), ALU.is_equal).then_inc(onehots, 1)
            for j, (a, b) in enumerate(chunks):
                w = (b - a) * EK
                e.wait_ge(mm_done, j + 1)
                c.link(e.tensor_tensor_scan(rk[:, a:b, :].rearrange("p a b -> p (a b)"),
                                            wrap[:, 0:b - a, :].rearrange("p a b -> p (a b)"),
                                            psb[:, 0:w], 0.0, ALU.mult, ALU.add))
                c.link(e.tensor_copy(cnt[:, a:b], rk[:, a:b, EK - 1:EK].rearrange("p a b -> p (a b)")))
                e.tensor_tensor(rk[0:EP, a:b, :].rearrange("p a b -> p (a b)"),
                                rk[0:EP, a:b, :].rearrange("p a b -> p (a b)"),
                                psa[0:EP, 0:w], ALU.add).then_inc(evac, 1)
            e.wait_ge(evac, len(chunks))
            c.link(e.tensor_scalar(cnt[:, :], cnt[:, :], float(SLOTS - 1), None, ALU.add))
            c.link(e.tensor_copy(cnti[:, :], cnt[:, :]))
            c.link(e.tensor_scalar(cnti[:, :], cnti[:, :], 6, None, ALU.arith_shift_right))
            c.link(e.tensor_copy(cnt[:, :], cnti[:, :]))
            c.link(e.tensor_scalar(cnt[:, :], cnt[:, :], 1.0, None, ALU.max))
            c.link(e.tensor_tensor_scan(end[:, :], zr[:, :], cnt[:, :], 0.0, ALU.mult, ALU.add))
            c.link(e.tensor_tensor(base[:, :], end[:, :], cnt[:, :], ALU.subtract))
            c.link(e.tensor_scalar(base[:, :], base[:, :], float(SLOTS), None, ALU.mult))
            c.link(e.tensor_tensor(rk[0:EP, :, :], rk[0:EP, :, :],
                                   base[0:EP, :].unsqueeze(2).to_broadcast([EP, NT, EK]), ALU.add))
            c.link(e.tensor_tensor(rk[0:EP, :, :], rk[0:EP, :, :], oh[:, :, :], ALU.mult))
            c.link(e.tensor_reduce(pf[:, :], rk[0:EP, :, :].rearrange("p t k -> p k t"), axis=AX.X, op=ALU.add))
            c.link(e.tensor_scalar(vf[:, :], ed[:, :], -1048576.0, 1048576.0, ALU.mult, ALU.add))
            c.link(e.tensor_tensor(pf[:, :], pf[:, :], vf[:, :], ALU.add))
            c.link(e.tensor_copy(K["pos"][0:EP, :], pf[:, :]))
            for g in range(4):
                c.link(e.tensor_scalar(cmp_[:, :], end[:, :], itp[:, g:g + 1], None, ALU.is_le))
                c.link(e.reduce_sum(tlt[:, g:g + 1], cmp_[:, :], axis=AX.X))
            e.tensor_scalar(tlt[:, :], tlt[:, :], float(NT - 1), None, ALU.min).then_inc(items_in, 1)
            e.wait_ge(items_row, 1)
            c.link(e.tensor_copy(row[:, :], psi[:, :]))
            c.mark(e.tensor_copy(K["items"][:, 0:NITEMS], row[:, :]))
            c.link(e.memset(first[:, :], 1.0))
            c.link(e.tensor_tensor(first[:, 1:NITEMS], row[:, 1:NITEMS], row[:, 0:NITEMS - 1], ALU.not_equal))
            c.link(e.tensor_scalar(offl[:, :], par[:, :], 2.0, -3.0, ALU.mult, ALU.add))
            c.link(e.tensor_tensor(offl[:, :], offl[:, :], first[:, :], ALU.mult))
            c.link(e.tensor_tensor(offl[:, :], offl[:, :], par[:, :], ALU.subtract))
            c.link(e.tensor_scalar(offl[:, :], offl[:, :], 3.0, float(ROW), ALU.add, ALU.mult))
            c.link(e.tensor_copy(K["items"][:, NITEMS:2 * NITEMS], offl[:, :]))
            c.link(e.tensor_scalar(nn[:, 0:1], end[0:1, NT - 1:NT], 1.0, None, ALU.add))
            c.link(e.tensor_copy(ni[:, 0:1], nn[:, 0:1]))
            c.link(e.tensor_scalar(K["nitems"][:, 0:1], ni[:, 0:1], 1, None, ALU.arith_shift_right))
            e.wait_ge(loops_done, 1)
            c.link(e.tensor_scalar(K["den0"][:, :], psl[:, :], 1.0, None, ALU.add))

        @block.tensor
        def _(e):
            e.wait_ge(consts, 1)
            e.wait_ge(onehots, 1)
            for j, (a, b) in enumerate(chunks):
                w = (b - a) * EK
                if j:
                    e.wait_ge(evac, j)
                m = oh[:, a:b, :].rearrange("p a b -> p (a b)")
                e.matmul(psb[:, 0:w], one[0:EP, :], m, start=True, stop=True)
                e.matmul(psa[:, 0:w], low[0:EP, :], m, start=True, stop=True).then_inc(mm_done, 1)
            e.wait_ge(onehots, 3)
            for k in range(EK):
                last = e.matmul(psl[:, :], on[:, k, :], ol[:, :, k], start=(k == 0), stop=(k == EK - 1))
            last.then_inc(loops_done, 1)
            e.wait_ge(items_in, 1)
            for g in range(4):
                last = e.matmul(psi[:, g * IG:(g + 1) * IG], tlt[0:IG, g:g + 1], K["ident"][0:IG, 0:IG],
                                start=True, stop=True)
            last.then_inc(items_row, 1)


def dense_in(nc, K, wq, x, W1, as1, ad1, qkv_w, qkv_b, gamma, beta, dram):
    with ExitStack() as st:
        def sb(name, shape, dt=f32):
            return st.enter_context(nc.sbuf_tensor(name, shape, dt))

        w1 = sb("w1", [P, 2, KD, WEXT], f32r)
        wkv = sb("wkv", [P, 2, KD, 2 * D], f32r)
        bkv = sb("bkv", [P, 2 * D])
        with ExitStack() as prep:
            weights_in(nc, K, prep, w1, wkv, bkv, wq, W1, as1, ad1, qkv_w, qkv_b, gamma, beta)
        tiles_in(nc, K, st, w1, wkv, bkv, x, dram)


def weights_in(nc, K, st, w1, wkv, bkv, wq, W1, as1, ad1, qkv_w, qkv_b, gamma, beta):
    def sb(name, shape, dt=f32):
        return st.enter_context(nc.sbuf_tensor(name, shape, dt))

    sem = semaphores(nc, st)

    w1s = sb("w1_stage", [P, KD, WEXT])
    qs = sb("qkv_stage", [P, 12, D])
    raw = sb("qkv_t", [P, KD, 3 * D])
    arep = sb("att_rep", [P, 2, HC])
    tmp = sb("att_prod", [P, HC])
    gc, bc, qb = sb("gamma_c", [P, KD]), sb("beta_c", [P, KD]), sb("qb_c", [P, KD])
    brep = sb("beta_rep", [P, KD, P])
    kvb = sb("kv_bias_rep", [P, 2 * D])
    pst = [st.enter_context(nc.psum_tensor(f"ps_wt{i}", [P, D], f32)) for i in range(2)]
    psb = [st.enter_context(nc.psum_tensor(f"ps_wb{i}", [P, D], f32)) for i in range(2)]
    psq = st.enter_context(nc.psum_tensor("ps_qb", [P, KD], f32))
    w1_in, q_in, small_in, turned, taken, raw_ready, rep_ready, bias_mm, dv, ac = (sem(n) for n in (
        "w1_loaded", "qkv_loaded", "small_loaded", "qkv_turned", "qkv_taken", "qkv_t_ready", "beta_rep_ready",
        "bias_products", "weights_dve", "weights_act"))
    block = st.enter_context(nc.Block())

    @block.sync
    def _(e):
        e.dma_start(qs[:, :, :], qkv_w.rearrange("(b p) c -> p b c", p=P)).then_inc(q_in, 16)
        e.dma_start(w1s[:, :, 0:HC], W1.rearrange("(k p) n -> p k n", p=P)).then_inc(w1_in, 16)
        for j, a in enumerate((as1, ad1)):
            e.dma_start(arep[:, j, :], a.rearrange("(o h) c -> o (h c)", o=1).to_broadcast([P, HC])).then_inc(w1_in, 16)
        e.wait_ge(w1_in, 48)

    @block.scalar
    def _(e):
        for t, s in ((gc, gamma), (bc, beta), (qb, qkv_b[0:D])):
            e.dma_start(t[:, :], s.rearrange("(k p) -> p k", p=P), allow_slow_non_contiguous=True).then_inc(small_in, 16)
        e.dma_start(kvb[:, :], qkv_b[D:3 * D].rearrange("(o c) -> o c", o=1).to_broadcast([P, 2 * D])).then_inc(small_in, 16)
        for n in range(12):
            k, b = n // 3, n % 3
            e.wait_ge(turned, n + 1)
            e.activation(raw[:, k, b * D:(b + 1) * D], pst[n % 2][:, :], ACT.Copy).then_inc(taken, 1)

    @block.tensor
    def _(e):
        e.wait_ge(q_in, 16)
        for n in range(12):
            k, b = n // 3, n % 3
            if n >= 2:
                e.wait_ge(taken, n - 1)
            for j in range(4):
                last = e.transpose(pst[n % 2][:, j * P:(j + 1) * P], qs[:, 4 * b + j, k * P:(k + 1) * P], K["ident"][:, :])
            last.then_inc(turned, 1)
        e.wait_ge(taken, 12)
        e.wait_ge(rep_ready, 1)
        for b in range(2):
            for k in range(KD):
                e.matmul(psb[b][:, :], brep[:, k, :], raw[:, k, (b + 1) * D:(b + 2) * D], start=(k == 0), stop=(k == KD - 1))
        for b in range(KD):
            for k in range(KD):
                last = e.matmul(psq[:, b:b + 1], raw[:, k, b * P:(b + 1) * P], bc[:, k:k + 1], start=(k == 0), stop=(k == KD - 1))
        last.then_inc(bias_mm, 1)

    @block.vector
    def _(e):
        c = Chain(e, dv)
        e.wait_ge(small_in, 64)
        e.tensor_copy(brep[:, :, :], bc[:, :].unsqueeze(2).to_broadcast([P, KD, P])).then_inc(rep_ready, 1)
        e.wait_ge(w1_in, 48)
        for k in range(KD):
            for j in range(2):
                c.link(e.tensor_tensor(tmp[:, :], w1s[:, k, 0:HC], arep[:, j, :], ALU.mult))
                c.link(e.reduce_sum(w1s[:, k, HC + 4 * j:HC + 4 * j + 4], tmp[:, :].rearrange("p (h c) -> p h c", h=HEADS), axis=AX.X))
        for k in range(KD):
            c.mark(e.tensor_copy(w1[:, 0, k, :], w1s[:, k, :]))
        c.sync()
        for k in range(KD):
            c.mark(e.tensor_tensor(w1[:, 1, k, :], w1s[:, k, :], w1[:, 0, k, :].bitcast(f32), ALU.subtract))
        for k in range(KD):
            e.wait_ge(taken, 3 * k + 3)
            g = gc[:, k:k + 1]
            for w, a, b in ((wq, 0, D), (wkv, D, 3 * D)):
                c.link(e.tensor_scalar(w[:, 0, k, :], raw[:, k, a:b], g, None, ALU.mult))
                c.mark(e.scalar_tensor_tensor(w[:, 1, k, :], raw[:, k, a:b], g, w[:, 0, k, :].bitcast(f32), ALU.mult, ALU.subtract))
        e.wait_ge(bias_mm, 1)
        for b in range(2):
            c.mark(e.tensor_tensor(bkv[:, b * D:(b + 1) * D], kvb[:, b * D:(b + 1) * D], psb[b][:, :], ALU.add))
        c.link(e.tensor_tensor(K["bq"][:, :], qb[:, :], psq[:, :], ALU.add))


def tiles_in(nc, K, st, w1, wkv, bkv, x, dram):
    def sb(name, shape, dt=f32):
        return st.enter_context(nc.sbuf_tensor(name, shape, dt))

    sem = semaphores(nc, st)

    ps = lambda name, w=D: st.enter_context(nc.psum_tensor(name, [P, w], f32))
    xb = sb("x_rows", [P, 2, D])
    bn = sb("bn", [P, 6])
    mv = sb("mean_var", [P, 2])
    sc = sb("norm_vars", [P, 3])
    sq = sb("norm_roots", [P, 2])
    xn = sb("x_norm", [P, D])
    xt = sb("x_norm_t", [P, 2, 2, D], f32r)
    ho = sb("h_rows", [P, 2, ROW])
    kz, km, ke = sb("k_pre", [P, D]), sb("k_min", [P, D]), sb("k_exp", [P, D])
    kf = sb("k_feat", [P, 2, D])
    vf = sb("v_rows", [P, 2, D])
    ones = sb("ones_c", [P, 2])
    idx = sb("slot_of", [EP, 2, 2], i32)
    pst, psh0, psh1, psk, psv, pss, pskv, psks = (
        ps(n, w) for n, w in (("ps_t", D), ("ps_h0", D), ("ps_h1", D), ("ps_k", D), ("ps_v", D), ("ps_al", D),
                              ("ps_kv", D), ("ps_ks", D)))
    x_in = [sem("x_in0"), sem("x_in1")]
    h_out = [sem("h_out0"), sem("h_out1")]
    names = ("var_ready roots_ready scales_ready xn_ready x_turned hi_ready lo_ready h_done h_taken al_taken "
             "k_done v_done k_taken v_taken kmin_ready kexp_ready kv_ready kvt_done kvt_taken x_free ho_free "
             "a_dve bn_seen slot_free slot_copied").split()
    S = {n: sem(n) for n in names}
    slotdma = [sem(f"slot_dma{i}") for i in range(2)]
    TRIPS = NT // 2
    assert NT == 2 * TRIPS + 1
    block = st.enter_context(nc.Block())

    @block.sync
    def _(e):
        with e.Fori(0, TRIPS) as t:
            it = e.snap(t)
            for p in range(2):
                i = it * 2 + p
                e.wait_ge(S["xn_ready"], i + 1)
                e.dma_start(xb[:, p, :], x[bass.ds(i * P, P), :]).then_inc(x_in[p], 16)
        e.wait_ge(S["xn_ready"], NT)
        e.dma_start(xb[0:LAST, 0, :], x[(NT - 1) * P:N, :]).then_inc(x_in[0], 16)
        e.wait_ge(x_in[0], 16 * (TRIPS + 1))

    @block.gpsimd
    def _(e):
        with e.Fori(0, EK // 2) as t:
            it = e.snap(t)
            for p in range(2):
                k = it * 2 + p
                e.tensor_copy(idx[:, p, 0:1], K["pos"][0:EP, bass.ds(k, 1)]).then_inc(S["slot_copied"], 1)
                e.tensor_copy(idx[:, p, 1:2], K["val"][0:EP, bass.ds(k, 1)]).then_inc(S["slot_copied"], 1)
                wait_apart(e, S["slot_copied"], k * 2 + 2, S["slot_free"])
                e.indirect_dma_start(out=dram["slots"].ap(), out_offset=bass.IndirectOffsetOnAxis(ap=idx[:, p, 0:1], axis=0),
                                     in_=idx[:, p, 1:2], in_offset=None, bounds_check=NITEMS * SLOTS - 1,
                                     oob_is_err=False).then_inc(slotdma[p], 16)
                wait_apart(e, slotdma[p], it * 16 + 16, S["slot_free"])

    @block.scalar
    def _(e):
        e.sem_inc(S["xn_ready"], 2)
        e.sem_inc(S["h_taken"], 1)
        for p in range(2):
            e.sem_inc(h_out[p], 16)

        def normalise(i, p):
            e.wait_ge(S["var_ready"], i + 1)
            e.activation(sq[:, :], sc[:, 0:2], ACT.Sqrt).then_inc(S["roots_ready"], 1)
            e.wait_ge(S["x_turned"], i + 1)
            e.wait_ge(S["scales_ready"], i + 1)
            e.activation(xn[:, :], xb[:, p, :], ACT.Identity, bias=K["stat"][:, bass.ds(i, 1), 1],
                         scale=K["stat"][:, bass.ds(i, 1), 0]).then_inc(S["xn_ready"], 1)

        def high(i, p):
            e.wait_ge(S["x_turned"], i + 2)
            e.wait_ge(S["v_done"], i + 1)
            e.activation(xt[:, p, 0, :], pst[:, :], ACT.Copy).then_inc(S["hi_ready"], 1)

        def body(i, it, p, ahead=True):
            if ahead:
                normalise(i + 1, 1 - p)
            e.wait_ge(S["h_done"], i + 1)
            e.wait_ge(h_out[p], it * 16 + 16)
            q = K["stat"][:, bass.ds(i, 1), 2]
            e.activation(ho[:, p, 0:D], psh0[:, :], ACT.Copy, scale=q)
            e.activation(ho[:, p, D:HC], psh1[:, :], ACT.Copy, scale=q).then_inc(S["h_taken"], 1)
            if ahead:
                high(i + 1, 1 - p)
            e.wait_ge(S["kmin_ready"], i + 1)
            e.activation(ke[:, :], km[:, :], ACT.Exp).then_inc(S["kexp_ready"], 1)
            e.wait_ge(S["h_taken"], i + 2)
            e.wait_ge(S["al_taken"], i + 2)
            e.dma_start(dram["h1t"].ap()[bass.ds(i * P, P), :], ho[:, p, :]).then_inc(h_out[p], 16)

        normalise(0, 0)
        high(0, 0)
        with e.Fori(0, TRIPS) as t:
            it = e.snap(t)
            for p in range(2):
                body(e.snap(it * 2 + p), it, p)
        body(NT - 1, TRIPS, 0, ahead=False)
        e.wait_ge(h_out[0], 16 * (TRIPS + 2))
        e.wait_ge(h_out[1], 16 * (TRIPS + 1))

    @block.vector
    def _(e):
        c = Chain(e, S["a_dve"])

        def stats(i, it, p):
            e.wait_ge(x_in[p], it * 16 + 16)
            c.link(e.bn_stats(bn[:, :], xb[:, p, :]))
            e.sem_inc(S["bn_seen"], 1)
            c.link(e.bn_aggr(mv[:, :], bn[:, :]))
            c.mark(e.tensor_scalar(sc[:, 2:3], mv[:, 1:2], LN_EPS, None, ALU.add))
            c.link(e.tensor_scalar(sc[:, 0:1], mv[:, 1:2], 1.0 + LN_EPS, LN_EPS * LN_EPS, ALU.mult, ALU.add))
            c.link(e.reciprocal(sc[:, 2:3], sc[:, 2:3]))
            e.tensor_tensor(sc[:, 1:2], sc[:, 0:1], sc[:, 2:3], ALU.mult).then_inc(S["var_ready"], 1)
            e.wait_ge(S["roots_ready"], i + 1)
            s = K["stat"][:, bass.ds(i, 1), :]
            c.mark(e.tensor_copy(K["stat"][:, bass.ds(i, 1), 2], sq[:, 1:2]))
            c.link(e.reciprocal(K["stat"][:, bass.ds(i, 1), 0], sq[:, 0:1]))
            e.scalar_tensor_tensor(K["stat"][:, bass.ds(i, 1), 1], mv[:, 0:1], -1.0, K["stat"][:, bass.ds(i, 1), 0],
                                   ALU.mult, ALU.mult).then_inc(S["scales_ready"], 1)

        def low(i, p):
            e.wait_ge(S["hi_ready"], i + 1)
            e.tensor_tensor(xt[:, p, 1, :], pst[:, :], xt[:, p, 0, :].bitcast(f32), ALU.subtract).then_inc(S["lo_ready"], 1)

        def body(i, it, p, ahead=True):
            if ahead:
                stats(i + 1, it if p == 0 else it + 1, 1 - p)
            e.wait_ge(S["h_done"], i + 1)
            e.wait_ge(h_out[p], it * 16 + 16)
            c.mark(e.tensor_scalar(ho[:, p, HC:DEN], pss[:, 0:8], K["stat"][:, bass.ds(i, 1), 2], None, ALU.mult))
            e.tensor_copy(ho[:, p, DEN:ROW], K["den0"][:, bass.ds(i, 1)].to_broadcast([P, HEADS])).then_inc(S["al_taken"], 1)
            if ahead:
                low(i + 1, 1 - p)
            accumulate(i)
            e.wait_ge(S["k_done"], i + 1)
            e.tensor_tensor(kz[:, :], psk[:, :], bkv[:, 0:D], ALU.add).then_inc(S["k_taken"], 1)
            e.wait_ge(S["k_taken"], i + 2)
            e.tensor_scalar(km[:, :], kz[:, :], 0.0, None, ALU.min).then_inc(S["kmin_ready"], 1)
            e.wait_ge(S["v_done"], i + 3)
            e.wait_ge(S["kvt_done"], i + 1)
            e.tensor_tensor(vf[:, p, :], psv[:, :], bkv[:, D:2 * D], ALU.add).then_inc(S["v_taken"], 1)
            e.wait_ge(S["kexp_ready"], i + 1)
            e.scalar_tensor_tensor(kf[:, p, :], kz[:, :], 0.0, ke[:, :], ALU.max, ALU.add).then_inc(S["kv_ready"], 1)

        def accumulate(n):
            e.wait_ge(S["kvt_done"], n + 2)
            c.mark(e.tensor_tensor(K["ksum"][:, :], K["ksum"][:, :], psks[:, 0:KD], ALU.add))
            e.tensor_tensor(K["kvT"][:, :], K["kvT"][:, :], pskv[:, :], ALU.add).then_inc(S["kvt_taken"], 1)

        e.sem_inc(S["al_taken"], 1)
        e.sem_inc(S["lo_ready"], 1)
        e.sem_inc(S["k_taken"], 1)
        e.sem_inc(S["v_taken"], 1)
        e.sem_inc(S["kvt_taken"], 1)
        c.mark(e.memset(kf[:, 1, :], 0.0))
        c.mark(e.memset(vf[:, 1, :], 0.0))
        c.mark(e.memset(K["kvT"][:, :], 0.0))
        c.mark(e.memset(K["ksum"][:, :], 0.0))
        c.mark(e.memset(ones[:, :], 1.0))
        c.sync()
        e.engine_nop().then_inc(S["kv_ready"], 1)
        stats(0, 0, 0)
        low(0, 0)
        assert c.n == A_START, c.n
        with e.Fori(0, TRIPS) as t:
            it = e.snap(t)
            c.base, c.n = e.snap(it * A_STEPS + A_START), 0
            for p in range(2):
                body(e.snap(it * 2 + p), it, p)
            assert c.n == A_STEPS, c.n
        c.base, c.n = 0, A_STEPS * TRIPS + A_START
        body(NT - 1, TRIPS, 0, ahead=False)
        accumulate(NT)

    @block.tensor
    def _(e):
        e.sem_inc(S["x_turned"], 1)
        e.sem_inc(S["v_done"], 2)
        e.sem_inc(S["kvt_done"], 1)

        def turn(i):
            e.wait_ge(S["xn_ready"], i + 3)
            e.wait_ge(S["lo_ready"], i + 1)
            for k in range(KD):
                last = e.transpose(pst[:, k * P:(k + 1) * P], xn[:, k * P:(k + 1) * P], K["ident"][:, :])
            last.then_inc(S["x_turned"], 1)

        def product(p, w, outs):
            for k in range(KD):
                for n, (a, b) in enumerate(((0, 0), (0, 1), (1, 0))):
                    for o, c0, c1 in outs:
                        last = e.matmul(o, xt[:, p, a, k * P:(k + 1) * P], w[:, b, k, c0:c1],
                                        start=(k == 0 and n == 0), stop=(k == KD - 1 and n == 2))
            return last

        def kv(n, p, rows=P):
            e.wait_ge(S["kv_ready"], n + 1)
            e.wait_ge(S["kvt_taken"], n + 1)
            for b in range(KD):
                s = slice(b * P, (b + 1) * P)
                e.matmul(pskv[:, s], vf[0:rows, p, s], kf[0:rows, p, s], start=True, stop=True)
                last = e.matmul(psks[:, b:b + 1], kf[0:rows, p, s], ones[0:rows, 0:1], start=True, stop=True)
            last.then_inc(S["kvt_done"], 1)

        def body(i, p, ahead=True):
            e.wait_ge(S["lo_ready"], i + 2)
            e.wait_ge(S["h_taken"], i + 1)
            e.wait_ge(S["al_taken"], i + 1)
            product(p, w1, ((psh0[:, :], 0, D), (psh1[:, :], D, HC), (pss[:, 0:8], HC, WEXT))).then_inc(S["h_done"], 1)
            if ahead:
                turn(i + 1)
            kv(i, 1 - p)
            e.wait_ge(S["k_taken"], i + 1)
            product(p, wkv, ((psk[:, :], 0, D),)).then_inc(S["k_done"], 1)
            e.wait_ge(S["v_taken"], i + 1)
            product(p, wkv, ((psv[:, :], D, 2 * D),)).then_inc(S["v_done"], 1)

        turn(0)
        with e.Fori(0, TRIPS) as t:
            it = e.snap(t)
            for p in range(2):
                body(e.snap(it * 2 + p), p)
        body(NT - 1, 0, ahead=False)
        kv(NT, 0, LAST)


A_STEPS = 18
A_START = 12


def gat(nc, K, layer, bias, W, att_s, att_d, table, result, dram):
    WO = WEXT if layer == 1 else D
    with ExitStack() as st:
        w = st.enter_context(nc.sbuf_tensor(f"w_next{layer}", [P, 2, KH, WO], f32r))
        bcol = st.enter_context(nc.sbuf_tensor(f"bias_c{layer}", [P, KH], f32))
        with ExitStack() as prep:
            gat_weights(nc, K, prep, layer, w, bcol, bias, W, att_s, att_d, dram)
        gat_items(nc, K, st, layer, w, bcol, table, result)


def gat_weights(nc, K, st, layer, w, bcol, bias, W, att_s, att_d, dram):
    def sb(name, shape, dt=f32):
        return st.enter_context(nc.sbuf_tensor(f"{name}{layer}", shape, dt))

    sem = semaphores(nc, st, str(layer))

    WO = WEXT if layer == 1 else D
    ws = sb("w_stage", [P, KH, WO])
    arep = sb("att_rep", [P, 2, HC])
    tmp = sb("att_prod", [P, HC])
    raw = sb("slots_raw", [IG, 4, SLOTS], i32)
    si, di = sb("slots_src_i", [IG, 4, SLOTS], i32), sb("slots_dst_i", [IG, 4, SLOTS], i32)
    sf = sb("slots_f", [IG, 2, 4, SLOTS])
    ps = [st.enter_context(nc.psum_tensor(f"ps_slots{layer}{i}", [SLOTS, NITEMS], f32)) for i in range(2)]
    w_in, s_in, b_in, parts, turned, dv = (sem(n) for n in (
        "gw_loaded", "slots_loaded", "bias_loaded", "slots_parts", "slots_turned", "gw_dve"))
    block = st.enter_context(nc.Block())

    @block.sync
    def _(e):
        e.dma_start(ws[:, :, 0:min(WO, HC)], W.rearrange("(k p) n -> p k n", p=P)).then_inc(w_in, 16)
        if layer == 1:
            for j, a in enumerate((att_s, att_d)):
                e.dma_start(arep[:, j, :], a.rearrange("(o h) c -> o (h c)", o=1).to_broadcast([P, HC])).then_inc(w_in, 16)
            e.dma_start(raw[:, :, :], dram["slots"].ap().rearrange("(g i s) o -> i g (s o)", i=IG, s=SLOTS)).then_inc(s_in, 16)
        e.dma_start(bcol[:, :], bias.rearrange("(k p) -> p k", p=P), allow_slow_non_contiguous=True).then_inc(b_in, 16)
        e.wait_ge(b_in, 16)

    @block.vector
    def _(e):
        c = Chain(e, dv)
        if layer == 1:
            e.wait_ge(s_in, 16)
            c.mark(e.tensor_scalar(si[:, :, :], raw[:, :, :], 8, None, ALU.arith_shift_right))
            c.mark(e.tensor_scalar(di[:, :, :], raw[:, :, :], 255, None, ALU.bitwise_and))
            c.sync()
            c.mark(e.tensor_copy(sf[:, 0, :, :], si[:, :, :]))
            e.tensor_copy(sf[:, 1, :, :], di[:, :, :]).then_inc(parts, 1)
            e.wait_ge(turned, 1)
            c.mark(e.tensor_copy(K["slot_src"][:, :], ps[0][:, :]))
            c.mark(e.tensor_copy(K["slot_dst"][:, :], ps[1][:, :]))
            e.wait_ge(w_in, 48)
            for k in range(KH):
                for j in range(2):
                    c.link(e.tensor_tensor(tmp[:, :], ws[:, k, 0:HC], arep[:, j, :], ALU.mult))
                    c.link(e.reduce_sum(ws[:, k, HC + 4 * j:HC + 4 * j + 4], tmp[:, :].rearrange("p (h c) -> p h c", h=HEADS), axis=AX.X))
        else:
            e.wait_ge(w_in, 16)
        for k in range(KH):
            c.mark(e.tensor_copy(w[:, 0, k, :], ws[:, k, :]))
        c.sync()
        for k in range(KH):
            c.mark(e.tensor_tensor(w[:, 1, k, :], ws[:, k, :], w[:, 0, k, :].bitcast(f32), ALU.subtract))
        c.sync()

    @block.tensor
    def _(e):
        if layer == 1:
            e.wait_ge(parts, 1)
            for j in range(2):
                for g in range(4):
                    last = e.matmul(ps[j][:, g * IG:(g + 1) * IG], sf[:, j, g, :], K["ident"][0:IG, 0:IG], start=True, stop=True)
            last.then_inc(turned, 1)


def gat_items(nc, K, st, layer, w, bcol, table, result):
    def sb(name, shape, dt=f32):
        return st.enter_context(nc.sbuf_tensor(f"{name}{layer}", shape, dt))

    sem = semaphores(nc, st, str(layer))

    def ps(name, rows=P):
        return st.enter_context(nc.psum_tensor(f"{name}{layer}", [rows, D], f32))

    first = layer == 1
    OW = ROW if first else D
    SH = HEADS * SLOTS
    state = sb("state", [P, 4, ROW])
    flat = state[:, :, :].rearrange("p a b -> p (a b)")
    gr = sb("edge_rows", [SLOTS, 2, ROW])
    ix = sb("edge_index", [SLOTS, 2], i32)
    dm = sb("edge_node", [SLOTS, P])
    y = sb("edge_logit_diag", [SLOTS, 5, SLOTS])
    pen = sb("mask", [P, SLOTS])
    s = sb("logits", [P, HEADS, SLOTS])
    mx = sb("edge_max", [P, HEADS])
    z2 = sb("new_old_max", [P, 2 * HEADS])
    ee = sb("exponents", [P, SH + HEADS])
    ex = sb("weights", [P, SH + HEADS])
    dn = sb("den_part", [P, 3, HEADS])
    cs = sb("base_scale", [P, HEADS])
    pr = sb("alpha", [P, HEADS, SLOTS])
    pt = sb("alpha_t", [SLOTS, HEADS * P])
    ff = sb("features_t", [P, 2, D])
    ft = sb("features_t_parts", [P, 2, 2, HC], f32r)
    ho = sb("next_rows", [P, 2, OW])
    lt = sb("next_logits_t", [2 * HEADS, P])
    psb, psp, psa0, psa1, pst, psal, psh0, psh1 = (ps("ps_b"), ps("ps_p", SLOTS), ps("ps_a0"), ps("ps_a1"), ps("ps_t"), ps("ps_al"),
                                                  ps("ps_h0"), ps("ps_h1"))
    names = ("d_ready a_done s_taken e_ready x_ready p_ready b_done pt_ready c_done combined turned f_ready part_hi "
             "parts_ready h0_done h1_done h0_taken h1_taken al_done lt_ready alt_done al_taken index_ready b_dve ended pool_apart pe_apart").split()
    S = {n: sem(n) for n in names}
    last_done = S["h1_done" if first else "h0_done"]
    gathered, loaded, h_out = ([sem(f"{n}{p}_") for p in range(2)] for n in ("gathered", "loaded", "rows_out"))
    tab, res = table.ap(), result.ap()
    block = st.enter_context(nc.Block())

    def pairs(e):
        return e.value_load(K["nitems"][0:1, 0:1], min_val=1, max_val=NITEMS // 2 - 2)

    def base_of(e, i):
        return e.value_load(K["items"][0:1, bass.ds(i + NITEMS, 1)], min_val=0, max_val=3 * ROW)

    def tile_of(e, i):
        return e.value_load(K["items"][0:1, bass.ds(i, 1)], min_val=0, max_val=NT - 1)

    @block.sync
    def _(e):
        for p in range(2):
            e.sem_inc(h_out[p], 16)

        def load(i, p):
            t = tile_of(e, i)
            e.dma_start(state[:, p, :], tab[bass.ds(t * P, P), :]).then_inc(loaded[p], 16)

        load(0, 0)
        load(1, 1)
        e.wait_ge(S["combined"], 2)
        load(2, 0)
        n = pairs(e)
        with e.Fori(0, n) as tt:
            it = e.snap(tt)
            for p in range(2):
                i = e.snap(it * 2 + p)
                e.wait_ge(S["combined"], i + 3)
                load(i + 3, 1 - p)
                t = tile_of(e, i)
                if first:
                    e.wait_ge(S["h1_taken"], i + 2)
                    e.wait_ge(S["al_taken"], i + 2)
                else:
                    e.wait_ge(S["h0_taken"], i + 3)
                e.sem_inc(S["ended"], 1)
                wait_apart(e, h_out[1 - p], it * 16 + (16, 32)[p], S["ended"])
                e.dma_start(res[bass.ds(t * P, P), :], ho[:, p, :]).then_inc(h_out[p], 16)
        for p in range(2):
            wait_apart(e, h_out[p], n * 16 + 16, S["ended"])
            wait_apart(e, loaded[p], n * 16 + (32, 16)[p], S["ended"])

    @block.gpsimd
    def _(e):
        e.sem_inc(S["parts_ready"], 2)

        def index(i, p):
            e.tensor_copy(ix[:, p:p + 1], K["slot_src"][:, bass.ds(i, 1)]).then_inc(S["index_ready"], 1)

        def gather(i, p):
            wait_apart(e, S["index_ready"], i + 1, S["pool_apart"])
            e.indirect_dma_start(out=gr[:, p, :], out_offset=None, in_=tab,
                                 in_offset=bass.IndirectOffsetOnAxis(ap=ix[:, p:p + 1], axis=0),
                                 bounds_check=N - 1, oob_is_err=False).then_inc(gathered[p], 16)

        def parts(i, p):
            for j in range(2):
                n = i * 2 + j
                h = slice(j * D, (j + 1) * D)
                e.wait_ge(S["part_hi"], n + 1)
                e.tensor_tensor(ft[:, p, 1, h], ff[:, j, :], ft[:, p, 0, h].bitcast(f32), ALU.subtract)\
                 .then_inc(S["parts_ready"], 1)

        e.memset(gr[:, :, :], 0.0)
        index(0, 0)
        index(1, 1)
        gather(0, 0)
        gather(1, 1)
        e.wait_ge(S["c_done"], 1)
        index(2, 0)
        gather(2, 0)
        parts(0, 0)
        n = pairs(e)
        with e.Fori(0, n) as tt:
            it = e.snap(tt)
            for p in range(2):
                i = e.snap(it * 2 + p)
                wait_apart(e, S["c_done"], i + 2, S["pool_apart"])
                index(i + 3, 1 - p)
                gather(i + 3, 1 - p)
                parts(i + 1, 1 - p)
        for p in range(2):
            wait_apart(e, gathered[p], n * 16 + (32, 16)[p], S["pool_apart"])

    @block.scalar
    def _(e):
        e.sem_inc(S["pt_ready"], 1)
        e.sem_inc(S["f_ready"], 1)
        e.sem_inc(S["h0_taken"], 1 if first else 2)
        e.sem_inc(S["h1_taken"], 1)

        def exps(i):
            e.wait_ge(S["e_ready"], i + 1)
            e.activation(ex[:, :], ee[:, :], ACT.Exp).then_inc(S["x_ready"], 1)

        def alphas(i):
            e.wait_ge(S["b_done"], i + 2)
            e.activation(pt[:, :], psp[:, :], ACT.Copy).then_inc(S["pt_ready"], 1)

        def features(i, p, j):
            n = i * 2 + j
            e.wait_ge(S["turned"], n + 1)
            e.wait_ge(S["parts_ready"], n + 1)
            for b in range(4):
                last = e.activation(ff[:, j, b * P:(b + 1) * P], pst[:, b * P:(b + 1) * P], ACT.Relu,
                                    bias=bcol[:, 4 * j + b:4 * j + b + 1])
            last.then_inc(S["f_ready"], 1)
            e.wait_ge(S["f_ready"], n + 2)
            e.wait_ge(last_done, i + 1)
            e.activation(ft[:, p, 0, j * D:(j + 1) * D], ff[:, j, :], ACT.Copy).then_inc(S["part_hi"], 1)

        exps(0)
        alphas(0)
        exps(1)
        features(0, 0, 0)
        features(0, 0, 1)
        n = pairs(e)
        with e.Fori(0, n) as tt:
            it = e.snap(tt)
            for p in range(2):
                i = e.snap(it * 2 + p)
                alphas(i + 1)
                exps(i + 2)
                if first:
                    e.wait_ge(S["h0_done"], i + 1)
                    e.wait_ge(h_out[p], it * 16 + 16)
                    e.activation(ho[:, p, 0:D], psh0[:, :], ACT.Copy).then_inc(S["h0_taken"], 1)
                    e.wait_ge(S["alt_done"], i + 1)
                    e.activation(lt[:, :], psal[0:2 * HEADS, 0:P], ACT.Copy).then_inc(S["lt_ready"], 1)
                features(i + 1, 1 - p, 0)
                features(i + 1, 1 - p, 1)
                if first:
                    e.wait_ge(S["h1_done"], i + 3)
                    e.activation(ho[:, p, D:HC], psh1[:, :], ACT.Copy).then_inc(S["h1_taken"], 1)
                else:
                    e.wait_ge(S["h0_done"], i + 3)
                    e.wait_ge(h_out[p], it * 16 + 16)
                    e.activation(ho[:, p, :], (psh0, psh1)[p][:, :], ACT.Copy).then_inc(S["h0_taken"], 1)

    @block.vector
    def _(e):
        c = Chain(e, S["b_dve"])
        e.sem_inc(S["s_taken"], 1)
        e.sem_inc(S["combined"], 1)
        e.sem_inc(S["al_taken"], 1)
        e.tensor_copy(y[:, 4, :], K["ident"][0:SLOTS, 0:SLOTS])

        def prepare(i, it, p):
            e.wait_ge(gathered[p], it * 16 + 16)
            e.wait_ge(S["a_done"], i + 1)
            e.tensor_scalar(dm[:, :], K["iota"][0:SLOTS, :], K["slot_dst"][:, bass.ds(i, 1)], None, ALU.is_equal)
            e.tensor_tensor(y[:, 0:HEADS, :], K["ident"][0:SLOTS, 0:SLOTS].unsqueeze(1).to_broadcast([SLOTS, HEADS, SLOTS]),
                            gr[:, p, ALS:ALD].unsqueeze(2).to_broadcast([SLOTS, HEADS, SLOTS]), ALU.mult)\
             .then_inc(S["d_ready"], 1)

        def softmax_exponents(i, it, p):
            new = state[:, 2 + p, :]
            e.wait_ge(S["a_done"], i + 2)
            c.link(e.tensor_scalar(pen[:, :], psb[:, SH:SH + SLOTS], -1.0, -NEG, ALU.add, ALU.mult))
            e.tensor_tensor(s[:, :, :], psb[:, 0:SH].rearrange("p (h s) -> p h s", h=HEADS),
                            pen[:, :].unsqueeze(1).to_broadcast([P, HEADS, SLOTS]), ALU.add).then_inc(S["s_taken"], 1)
            e.wait_ge(S["s_taken"], i + 2)
            c.link(e.tensor_reduce(mx[:, :], s[:, :, :], axis=AX.X, op=ALU.max))
            e.wait_ge(loaded[p], it * 16 + 16)
            o = base_of(e, i)
            bm, ba = (flat[:, bass.ds(o + k, HEADS)] for k in (ALS, ALD))
            c.mark(e.tensor_copy(new[:, ALD:DEN], ba))
            c.link(e.tensor_tensor(new[:, ALS:ALD], mx[:, :], bm, ALU.max))
            c.mark(e.tensor_tensor(z2[:, HEADS:2 * HEADS], bm, new[:, ALD:DEN], ALU.add))
            c.mark(e.tensor_tensor(z2[:, 0:HEADS], new[:, ALS:ALD], new[:, ALD:DEN], ALU.add))
            c.link(e.tensor_tensor(s[:, :, :], s[:, :, :], new[:, ALD:DEN].unsqueeze(2).to_broadcast([P, HEADS, SLOTS]), ALU.add))
            c.mark(e.scalar_tensor_tensor(z2[:, :], z2[:, :], 0.2, z2[:, :], ALU.mult, ALU.max))
            c.link(e.scalar_tensor_tensor(s[:, :, :], s[:, :, :], 0.2, s[:, :, :], ALU.mult, ALU.max))
            e.tensor_tensor(ee[:, SH:SH + HEADS], z2[:, HEADS:2 * HEADS], z2[:, 0:HEADS], ALU.subtract)
            e.tensor_tensor(ee[:, 0:SH].rearrange("p (h s) -> p h s", h=HEADS), s[:, :, :],
                            z2[:, 0:HEADS].unsqueeze(2).to_broadcast([P, HEADS, SLOTS]), ALU.subtract).then_inc(S["e_ready"], 1)

        def softmax_weights(i, p):
            new = state[:, 2 + p, :]
            bd = flat[:, bass.ds(base_of(e, i) + DEN, HEADS)]
            e.wait_ge(S["x_ready"], i + 1)
            xe = ex[:, 0:SH].rearrange("p (h s) -> p h s", h=HEADS)
            c.mark(e.tensor_tensor(dn[:, 1, :], ex[:, SH:SH + HEADS], bd, ALU.mult))
            c.link(e.reduce_sum(dn[:, 0, :], xe, axis=AX.X))
            c.link(e.tensor_tensor(new[:, DEN:ROW], dn[:, 0, :], dn[:, 1, :], ALU.add))
            c.link(e.reciprocal(dn[:, 2, :], new[:, DEN:ROW]))
            e.wait_ge(S["combined"], i + 1)
            e.wait_ge(S["b_done"], i + 1)
            c.mark(e.tensor_tensor(cs[:, :], dn[:, 1, :], dn[:, 2, :], ALU.mult))
            e.tensor_tensor(pr[:, :, :], xe, dn[:, 2, :].unsqueeze(2).to_broadcast([P, HEADS, SLOTS]), ALU.mult)\
             .then_inc(S["p_ready"], 1)

        def combine(i, p):
            o = base_of(e, i)
            e.wait_ge(S["c_done"], i + 1)
            e.wait_ge(S["p_ready"], i + 1)
            e.wait_ge(S["combined"], i + 1)
            for h in range(HEADS):
                a = (psa0, psa1)[h // 2][:, (h % 2) * C:(h % 2 + 1) * C]
                last = e.scalar_tensor_tensor(state[:, 2 + p, h * C:(h + 1) * C], flat[:, bass.ds(o + h * C, C)],
                                              cs[:, h:h + 1], a, ALU.mult, ALU.add)
            last.then_inc(S["combined"], 1)

        prepare(0, 0, 0)
        softmax_exponents(0, 0, 0)
        softmax_weights(0, 0)
        prepare(1, 0, 1)
        softmax_exponents(1, 0, 1)
        combine(0, 0)
        softmax_weights(1, 1)
        start = c.n
        n = pairs(e)
        with e.Fori(0, n) as tt:
            it = e.snap(tt)
            c.base, c.n = e.snap(it * start + start), 0
            for p in range(2):
                i = e.snap(it * 2 + p)
                prepare(i + 2, it + 1, p)
                softmax_exponents(i + 2, it + 1, p)
                combine(i + 1, 1 - p)
                softmax_weights(i + 2, p)
                if first:
                    t = tile_of(e, i)
                    e.wait_ge(S["al_done"], i + 1)
                    e.wait_ge(h_out[p], it * 16 + 16)
                    e.tensor_copy(ho[:, p, DEN:ROW], K["den0"][:, bass.ds(t, 1)].to_broadcast([P, HEADS]))
                    e.tensor_copy(ho[:, p, HC:DEN], psal[:, P:P + 2 * HEADS]).then_inc(S["al_taken"], 1)
            assert c.n == start, (c.n, start)

    @block.tensor
    def _(e):
        e.sem_inc(S["a_done"], 1)
        e.sem_inc(S["b_done"], 1)
        e.sem_inc(last_done, 2)

        def spread(i):
            e.wait_ge(S["d_ready"], i + 1)
            e.wait_ge(S["s_taken"], i + 1)
            e.matmul(psb[:, 0:SH + SLOTS], dm[:, :], y[:, :, :].rearrange("p a b -> p (a b)"), start=True, stop=True)\
             .then_inc(S["a_done"], 1)

        def turn_alpha(i):
            e.wait_ge(S["p_ready"], i + 1)
            wait_apart(e, S["pt_ready"], i + 1, S["pe_apart"])
            for h in range(HEADS):
                last = e.transpose(psp[:, h * P:(h + 1) * P], pr[:, h, :], K["ident"][:, :])
            last.then_inc(S["b_done"], 1)

        def aggregate(i, p):
            e.wait_ge(S["pt_ready"], i + 2)
            e.wait_ge(S["combined"], i + 1)
            for h in range(HEADS):
                a = (psa0, psa1)[h // 2][:, (h % 2) * C:(h % 2 + 1) * C]
                last = e.matmul(a, pt[:, h * P:(h + 1) * P], gr[:, p, h * C:(h + 1) * C], start=True, stop=True)
            last.then_inc(S["c_done"], 1)

        def turn(i, p, j):
            e.wait_ge(S["combined"], i + 2)
            e.wait_ge(S["f_ready"], i * 2 + j + 1)
            for b in range(4):
                k = 4 * j + b
                last = e.transpose(pst[:, b * P:(b + 1) * P], state[:, 2 + p, k * P:(k + 1) * P], K["ident"][:, :])
            last.then_inc(S["turned"], 1)

        def product(out, p, ks, c0, c1):
            for k in ks:
                for n, (a, b) in enumerate(((0, 0), (0, 1), (1, 0))):
                    last = e.matmul(out, ft[:, p, a, k * P:(k + 1) * P], w[:, b, k, c0:c1],
                                    start=(k == 0 and n == 0), stop=(k == KH - 1 and n == 2))
            return last

        def next_logits(i, p):
            e.wait_ge(S["al_taken"], i + 1)
            for k in range(KH):
                for n, (a, b) in enumerate(((0, 0), (0, 1), (1, 0))):
                    last = e.matmul(psal[0:2 * HEADS, 0:P], w[:, b, k, HC:WEXT], ft[:, p, a, k * P:(k + 1) * P],
                                    start=(k == 0 and n == 0), stop=(k == KH - 1 and n == 2))
            last.then_inc(S["alt_done"], 1)

        def turn_logits(i):
            wait_apart(e, S["lt_ready"], i + 1, S["pe_apart"])
            e.transpose(psal[:, P:P + 2 * HEADS], lt[:, :], K["ident"][0:2 * HEADS, 0:2 * HEADS]).then_inc(S["al_done"], 1)

        spread(0)
        turn_alpha(0)
        spread(1)
        aggregate(0, 0)
        turn(0, 0, 0)
        turn(0, 0, 1)
        n = pairs(e)
        with e.Fori(0, n) as tt:
            it = e.snap(tt)
            for p in range(2):
                i = e.snap(it * 2 + p)
                h0 = psh0 if first or p == 0 else psh1
                turn_alpha(i + 1)
                spread(i + 2)
                e.wait_ge(S["parts_ready"], i * 2 + 3)
                e.wait_ge(S["h0_taken"], i + 1)
                product(h0[:, :], p, (0, 1), 0, D)
                aggregate(i + 1, 1 - p)
                product(h0[:, :], p, (2, 3), 0, D)
                e.wait_ge(S["parts_ready"], i * 2 + 4)
                if first:
                    product(h0[:, :], p, (4, 5, 6, 7), 0, D).then_inc(S["h0_done"], 1)
                    next_logits(i, p)
                    turn(i + 1, 1 - p, 0)
                    e.wait_ge(S["h1_taken"], i + 1)
                    product(psh1[:, :], p, (0, 1, 2, 3), D, HC)
                    turn_logits(i)
                    turn(i + 1, 1 - p, 1)
                    product(psh1[:, :], p, (4, 5, 6, 7), D, HC).then_inc(S["h1_done"], 1)
                else:
                    product(h0[:, :], p, (4, 5), 0, D)
                    turn(i + 1, 1 - p, 0)
                    product(h0[:, :], p, (6, 7), 0, D).then_inc(S["h0_done"], 1)
                    turn(i + 1, 1 - p, 1)


def tail(nc, K, wq, x, bfc, out_w, out_b, Wr, br, fW1, fb1, fW2, fb2, out, dram):
    with ExitStack() as st:
        def sb(name, shape, dt=f32):
            return st.enter_context(nc.sbuf_tensor(name, shape, dt))

        T = dict(mw=sb("mix_out_w", [P, 2, KD, D], f32r), w1=sb("expert_w1", [P, 2, KD, 2 * P], f32r),
                 w2=sb("expert_w2", [P, 2, 2, D], f32r), wr=sb("router_w", [P, 2, KD, NE], f32r),
                 b2=sb("expert_b2", [NE, 2, D], f32r), ks=sb("ksum_by_head", [P, KD, NE]), bias=sb("bias_rep", [P, D]),
                 br=sb("router_b_rep", [P, GT, NE]), b1=sb("expert_b1_c", [P, 2]), sel=sb("expert_rows", [NE, 2 * P], f32r), head=sb("head_rows", [NE, D], f32r),
                 tri=sb("earlier_b", [P, P], bf16), one=sb("ones_bf", [P, P], bf16), i8=sb("iota_8", [P, NE]))
        with ExitStack() as prep:
            tail_weights(nc, K, prep, T, bfc, out_w, out_b, Wr, br, fW1, fb1, fW2, fb2)
        tail_groups(nc, K, st, T, wq, x, out, dram)


def tail_weights(nc, K, st, T, bfc, out_w, out_b, Wr, br, fW1, fb1, fW2, fb2):
    def sb(name, shape, dt=f32):
        return st.enter_context(nc.sbuf_tensor(name, shape, dt))

    sem = semaphores(nc, st)

    ow = sb("out_w_rows", [P, KD, D])
    owt = sb("out_w_t", [P, KD, D])
    w1s, w2s, wrs, b2s = sb("ew1_stage", [P, KD, 2 * P]), sb("ew2_stage", [P, 2, D]), sb("wr_stage", [P, KD, NE]), sb("eb2_stage", [NE, D])
    ob = sb("out_b_rep", [P, D])
    brs = sb("br_stage", [P, NE])
    bm = sb("head_mask", [P, P])
    sels = sb("rows_stage", [NE, 2 * P + D])
    kvm = sb("kv_masked", [P, KD, P])
    pst = [st.enter_context(nc.psum_tensor(f"ps_owt{i}", [P, D], f32)) for i in range(2)]
    psm = [st.enter_context(nc.psum_tensor(f"ps_mw{i}", [P, D], f32)) for i in range(2)]
    ow_in, rest_in, act_in, mask, turned, taken, kv_masked, products, p_taken, dv, pool = (sem(n) for n in (
        "ow_loaded", "tail_loaded", "tail_small_loaded", "mask_ready", "ow_turned", "ow_taken", "kv_masked_ready", "mix_products",
        "mix_taken", "tail_dve", "tail_pool"))
    block = st.enter_context(nc.Block())

    @block.sync
    def _(e):
        e.dma_start(ow[:, :, :], out_w.rearrange("(b p) c -> p b c", p=P)).then_inc(ow_in, 16)
        for k in range(KD):
            e.dma_start(w1s[:, k, :].rearrange("p (e f) -> p e f", e=NE),
                        fW1[:, k * P:(k + 1) * P, :].rearrange("e p f -> p e f")).then_inc(rest_in, 16)
        e.dma_start(w2s[:, :, :], fW2.rearrange("e f d -> (e f) d").rearrange("(k p) d -> p k d", p=P)).then_inc(rest_in, 16)
        e.dma_start(wrs[:, :, :], Wr.rearrange("(k p) e -> p k e", p=P)).then_inc(rest_in, 16)
        e.dma_start(b2s[:, :], fb2).then_inc(rest_in, 16)
        e.wait_ge(rest_in, 112)

    @block.scalar
    def _(e):
        e.dma_start(T["bias"][:, :], bfc.rearrange("(o c) -> o c", o=1).to_broadcast([P, D])).then_inc(act_in, 16)
        e.dma_start(ob[:, :], out_b.rearrange("(o c) -> o c", o=1).to_broadcast([P, D])).then_inc(act_in, 16)
        e.dma_start(brs[:, :], br.rearrange("(o c) -> o c", o=1).to_broadcast([P, NE])).then_inc(act_in, 16)
        e.dma_start(T["b1"][:, :], fb1.rearrange("e f -> (e f)").rearrange("(k p) -> p k", p=P), allow_slow_non_contiguous=True)\
         .then_inc(act_in, 16)
        for k in range(KD):
            e.wait_ge(turned, k + 1)
            e.activation(owt[:, k, :], pst[k % 2][:, :], ACT.Copy).then_inc(taken, 1)
        e.wait_ge(act_in, 64)

    @block.gpsimd
    def _(e):
        c = Chain(e, pool)
        c.mark(e.memset(bm[:, :], 0.0))
        c.mark(e.memset(sels[:, :], 1.0))
        c.mark(e.memset(T["one"][:, :], 1.0))
        c.mark(e.iota(T["i8"][:, :], pattern=[[1, NE]], base=0, channel_multiplier=0, allow_small_or_imprecise_dtypes=True))
        c.sync()
        c.link(e.tensor_copy(T["tri"][:, :], K["incl"][:, :]))
        c.link(e.memset(bm[0:64, 0:64], 1.0))
        c.link(e.memset(bm[64:P, 64:P], 1.0))
        for lo, hi, width in ((0, 2 * P, 32), (2 * P, 2 * P + D, 64)):
            c.link(e.affine_select(out=sels[:, lo:hi], in_=sels[:, lo:hi], compare_op=ALU.is_ge, fill=0.0, base=0,
                                   pattern=[[1, hi - lo]], channel_multiplier=-width))
            c.link(e.affine_select(out=sels[:, lo:hi], in_=sels[:, lo:hi], compare_op=ALU.is_ge, fill=0.0, base=width - 1,
                                   pattern=[[-1, hi - lo]], channel_multiplier=width))
        e.engine_nop().then_inc(mask, 1)

    @block.tensor
    def _(e):
        e.wait_ge(ow_in, 16)
        for k in range(KD):
            if k >= 2:
                e.wait_ge(taken, k - 1)
            for j in range(4):
                last = e.transpose(pst[k % 2][:, j * P:(j + 1) * P], ow[:, j, k * P:(k + 1) * P], K["ident"][:, :])
            last.then_inc(turned, 1)
        e.wait_ge(kv_masked, 1)
        e.wait_ge(taken, KD)
        for k in range(KD):
            if k >= 2:
                e.wait_ge(p_taken, k - 1)
            e.matmul(psm[k % 2][:, :], kvm[:, k, :], owt[:, k, :], start=True, stop=True).then_inc(products, 1)

    @block.vector
    def _(e):
        c = Chain(e, dv)
        e.wait_ge(mask, 1)
        c.link(e.memset(T["ks"][:, :, :], 0.0))
        for k in range(KD):
            c.mark(e.tensor_scalar(T["ks"][:, k, 2 * k:2 * k + 2], bm[:, 0:P:64], K["ksum"][:, k:k + 1], None, ALU.mult))
        c.mark(e.tensor_copy(T["sel"][:, :], sels[:, 0:2 * P]))
        c.mark(e.tensor_copy(T["head"][:, :], sels[:, 2 * P:2 * P + D]))
        e.tensor_tensor(kvm[:, :, :], K["kvT"][:, :].rearrange("p (k d) -> p k d", k=KD),
                        bm[:, :].unsqueeze(1).to_broadcast([P, KD, P]), ALU.mult).then_inc(kv_masked, 1)
        e.wait_ge(rest_in, 112)
        e.wait_ge(act_in, 64)
        pairs = ((T["w1"], w1s), (T["w2"], w2s), (T["wr"], wrs))
        for w, s in pairs:
            c.mark(e.tensor_copy(w[:, 0, :, :], s[:, :, :]))
        c.mark(e.tensor_copy(T["b2"][:, 0, :], b2s[:, :]))
        c.sync()
        for w, s in pairs:
            c.mark(e.tensor_tensor(w[:, 1, :, :], s[:, :, :], w[:, 0, :, :].bitcast(f32), ALU.subtract))
        c.mark(e.tensor_tensor(T["b2"][:, 1, :], b2s[:, :], T["b2"][:, 0, :].bitcast(f32), ALU.subtract))
        c.mark(e.tensor_tensor(T["bias"][:, :], T["bias"][:, :], ob[:, :], ALU.add))
        c.mark(e.tensor_copy(T["br"][:, :, :], brs[:, :].unsqueeze(1).to_broadcast([P, GT, NE])))
        for k in range(KD):
            e.wait_ge(products, k + 1)
            c.link(e.tensor_copy(T["mw"][:, 0, k, :], psm[k % 2][:, :]))
            e.tensor_tensor(T["mw"][:, 1, k, :], psm[k % 2][:, :], T["mw"][:, 0, k, :].bitcast(f32), ALU.subtract).then_inc(p_taken, 1)
        e.wait_ge(p_taken, KD)


def tail_groups(nc, K, st, T, wq, x, out, dram):
    def sb(name, shape, dt=f32):
        return st.enter_context(nc.sbuf_tensor(name, shape, dt))

    sem = semaphores(nc, st)

    GN = GT * P
    xb, yb, xn, t1, z, xn3, ob = (sb(n, [P, GT, D]) for n in (
        "g_x", "g_y", "g_xn", "g_sum", "g_z", "g_zn", "g_out"))
    xt, qp, zt = (sb(n, [P, 2, KD, GN], f32r) for n in ("g_xn_t", "g_q_parts", "g_zn_t"))
    qf = sb("g_q", [P, KD, GN])
    qz, qe = sb("g_q_relu", [P, 2, GN]), sb("g_q_exp", [P, GN])
    rn = K["kvT"]
    rs = sb("g_norm_parts", [NE, 2, GN], f32r)
    hg = sb("g_hidden", [P, 2, GN])
    hs = sb("g_hidden_parts", [P, 2, 2, GN], f32r)
    bn = sb("g_bn", [P, 6])
    mv = sb("g_mean_var", [P, GT, 2])
    va, sd, r3, n3 = sb("g_var", [P, GT]), sb("g_sd", [P, GT]), sb("g_rs", [P, GT]), sb("g_shift", [P, GT])
    lg, pe, pr, s0, s1, tw, po, ga = (sb(n, [P, GT, NE]) for n in (
        "r_logits", "r_exp", "r_probs", "r_first", "r_second", "r_top", "r_pos", "r_gate"))
    m8 = sb("r_max8", [P, GT, NE])
    i8u = sb("r_index8", [P, GT, NE], mybir.dt.uint32)
    i8f = sb("r_index8_f", [P, GT, NE])
    sl = sb("r_chosen", [P, GT, NE], bf16)
    t4 = sb("r_small", [P, 4, GT])
    run = sb("r_running", [P, NE])
    lt = hg[0:NE, 1, :]
    gs = sb("g_gate_t_parts", [NE, 2, GN], f32r)
    rot = [st.enter_context(nc.psum_tensor(f"ps_rot{i}", [P, D], f32)) for i in range(4)]
    pst = [st.enter_context(nc.psum_tensor(f"ps_turn{i}", [P, D], f32)) for i in range(2)]
    pss = st.enter_context(nc.psum_tensor("ps_small", [P, D], f32))
    psc = st.enter_context(nc.psum_tensor("ps_counts", [P, D], f32))
    names = ("xn_ready dve_apart chain_b xt_hi xt_lo t_turned sum_a sum_b sum_ready q_done q_taken qrelu_ready q_ready m_done m_taken rs_ready "
             "n_done qn_ready qp_hi qp_lo o_done z_ready var_ready sd_ready zs_ready zn_ready z_turned zt_hi zt_lo "
             "rt_done lt_ready r_done lg_ready re_ready sel_ready c_done c_taken gate_ready gt_done gs_lo h_done h_taken g_done "
             "hg_ready hs_hi hs_lo w_done out_ready tail_chain pe_apart_t pool_apart_t r_taken").split()
    S = {n: sem("t_" + n) for n in names}
    x_in, x_in2, y_in, stored = sem("t_x_in"), sem("t_x_in2"), sem("t_y_in"), sem("t_stored")
    USES = ([("q", j) for j in range(4)] + [("h", j) for j in range(2)] + [("n", j) for j in range(4)]
            + [("g", j) for j in range(2)] + [(s, j) for j in range(4) for s in "ow"])
    PER = dict(q=4, h=2, n=4, g=2, w=4, o=4)
    TAKEN = dict(q="q_taken", h="h_taken", n="qn_ready", g="hg_ready", w="out_ready", o="z_ready")
    assert len(USES) % 4 == 0

    def bank(kind, j):
        return rot[USES.index((kind, j)) % 4]

    FIRST_HALF = "qno"
    ORDER = (((0, 1), (0, 1)), ((2,), (2, 3)), ((3,), ()))

    def wait_bank(e, r, kind, j, a=True, b=True):
        u = USES.index((kind, j)) - 4
        while u >= 0 and not (a if USES[u][0] in FIRST_HALF else b):
            u -= 4
        before = u < 0
        k, m = USES[u % 4 + len(USES) - 4 if before else u]
        e.wait_ge(S[TAKEN[k]], (r if before else r + 1) * PER[k] + m + 1)

    FULL = NG - 1
    REST = NT - FULL * GT
    block = st.enter_context(nc.Block())

    def first(n):
        return isinstance(n, int) and n == 0

    def rounds(e, body):
        body(0, True, False, True)
        with e.Fori(1, NG - 1) as t:
            body(e.snap(t), True, True, True)
        body(NG - 1, True, True, False)
        body(NG, False, True, False)

    @block.sync
    def _(e):
        HALF = REST - 1

        def tiles(a, g, j0, j1):
            return a[bass.ds(g * GN + j0 * P, (j1 - j0) * P), :].rearrange("(j p) d -> p j d", p=P)

        y = dram["yt"].ap()
        def load(g):
            e.wait_ge(S["sum_ready"], g * GT + GT)
            e.dma_start(xb[:, 0:HALF, :], tiles(x, g, 0, HALF)).then_inc(x_in, 16)
            if isinstance(g, int) and g == FULL:
                e.dma_start(xb[0:LAST, HALF, :], x[(NT - 1) * P:N, :]).then_inc(x_in2, 16)
                e.dma_start(yb[:, 0:REST, :], tiles(y, g, 0, REST)).then_inc(y_in, 16)
            else:
                e.dma_start(xb[:, HALF:GT, :], tiles(x, g, HALF, GT)).then_inc(x_in2, 16)
                e.dma_start(yb[:, :, :], tiles(y, g, 0, GT)).then_inc(y_in, 16)

        load(0)
        with e.Fori(1, FULL) as t:
            load(e.snap(t))
        load(FULL)
        for s in (x_in, x_in2, y_in):
            e.wait_ge(s, 16 * NG)

    @block.gpsimd
    def _(e):
        apart = S["pool_apart_t"]
        e.sem_inc(S["sum_ready"], GT)
        e.sem_inc(S["qp_lo"], KD)
        e.sem_inc(S["hs_lo"], 2)

        def body(r, a, b, ahead):
            if a:
                for j in range(GT):
                    wait_apart(e, S["sum_a"], r * GT + j + 1, apart)
                    e.tensor_tensor(t1[:, j, :], t1[:, j, :], yb[:, j, :], ALU.add).then_inc(S["sum_b"], 1)
                    e.wait_ge(S["sum_b"], r * GT + j + 1)
                    e.tensor_tensor(t1[:, j, :], t1[:, j, :], T["bias"][:, :], ALU.add).then_inc(S["sum_ready"], 1)
                for j in range(KD):
                    n = r * KD + j
                    e.wait_ge(S["qp_hi"], n + 1)
                    e.tensor_tensor(qp[:, 1, j, :], qf[:, j, :], qp[:, 0, j, :].bitcast(f32), ALU.subtract).then_inc(S["qp_lo"], 1)
            if b:
                for j in range(2):
                    e.wait_ge(S["hs_hi"], (r - 1) * 2 + j + 1)
                    e.tensor_tensor(hs[:, 1, j, :], hg[:, j, :], hs[:, 0, j, :].bitcast(f32), ALU.subtract).then_inc(S["hs_lo"], 1)
                g = r - 1
                wait_apart(e, S["out_ready"], g * GT + 3 * GT, apart)
                if not (isinstance(g, int) and g == NG - 1):
                    e.dma_start(out[bass.ds(g * GN, GN), :].rearrange("(j p) d -> p j d", p=P), ob[:, :, :]).then_inc(stored, 16)
                else:
                    lo = FULL * GN
                    e.dma_start(out[lo:lo + (REST - 1) * P, :].rearrange("(j p) d -> p j d", p=P), ob[:, 0:REST - 1, :]).then_inc(stored, 16)
                    e.dma_start(out[(NT - 1) * P:N, :], ob[0:LAST, REST - 1, :]).then_inc(stored, 16)

        rounds(e, body)
        e.wait_ge(stored, 16 * (NG + 1))

    @block.scalar
    def _(e):
        e.sem_inc(S["q_taken"], KD)
        e.sem_inc(S["h_taken"], 4)

        def turn_hi(r0, j, turned, hi, dst):
            e.wait_ge(S[turned], r0 * GT + j + 1)
            e.activation(dst[:, 0, :, j * P:(j + 1) * P], pst[j % 2][:, :].rearrange("p (k n) -> p k n", k=KD), ACT.Copy)\
             .then_inc(S[hi], 1)

        def normed(g, n_x, tiles):
            e.wait_ge(x_in, n_x)
            e.wait_ge(x_in2, n_x)
            for j in tiles:
                e.wait_ge(S["sum_ready"], g * GT + GT)
                s = K["stat"]
                e.activation(xn[:, j, :], xb[:, j, :], ACT.Identity, bias=s[:, bass.ds(g * GT + j, 1), 1],
                             scale=s[:, bass.ds(g * GT + j, 1), 0]).then_inc(S["xn_ready"], 1)

        def query(r, j):
            n = r * KD + j
            e.wait_ge(S["q_done"], n + 1)
            if j >= 2 or not first(r):
                e.wait_ge(S["q_ready"], n - 1)
            e.activation(qz[:, j % 2, :], bank("q", j)[:, :], ACT.Relu, bias=K["bq"][:, j:j + 1]).then_inc(S["qrelu_ready"], 1)
            if j >= 1 or not first(r):
                e.wait_ge(S["q_ready"], n)
            e.activation(qe[:, :], bank("q", j)[:, :], ACT.Exp, bias=K["bq"][:, j:j + 1]).then_inc(S["q_taken"], 1)

        def body(r, a, b, ahead):
            g = r - 1
            for qs, zs in ORDER:
                if a:
                    for j in qs:
                        query(r, j)
                if b:
                    for j in zs:
                        turn_hi(g, j, "z_turned", "zt_hi", zt)
            if b:
                e.wait_ge(S["rt_done"], g + 1)
                e.wait_ge(S["hs_lo"], g * 2 + 2)
                e.activation(lt, pss[0:NE, :], ACT.Copy).then_inc(S["lt_ready"], 1)
                e.wait_ge(S["lg_ready"], g + 1)
                e.activation(pe[:, :, :], lg[:, :, :], ACT.Exp).then_inc(S["re_ready"], 1)
                for j in range(2):
                    e.wait_ge(S["h_done"], g * 2 + j + 1)
                    e.wait_ge(S["hs_lo"], g * 2 + j + 1)
                    e.activation(hg[:, j, :], bank("h", j)[:, :], ACT.Gelu, bias=T["b1"][:, j:j + 1]).then_inc(S["h_taken"], 1)
            if ahead:
                normed(r + 1, (r + 2) * 16, (0, 1))
            if a:
                for j in range(KD):
                    n = r * KD + j
                    e.wait_ge(S["qn_ready"], n + 1 + KD)
                    if not first(r):
                        e.wait_ge(S["o_done"], r * GT)
                    e.activation(qp[:, 0, j, :], qf[:, j, :], ACT.Copy).then_inc(S["qp_hi"], 1)
            if ahead:
                normed(r + 1, (r + 2) * 16, (2, 3))
                for j in range(2):
                    turn_hi(r + 1, j, "t_turned", "xt_hi", xt)
            if b:
                for j in range(2):
                    e.wait_ge(S["hg_ready"], g * 2 + j + 1 + 4)
                    if not first(g):
                        e.wait_ge(S["w_done"], g * GT)
                    e.activation(hs[:, 0, j, :], hg[:, j, :], ACT.Copy).then_inc(S["hs_hi"], 1)
            if ahead:
                for j in range(2, GT):
                    turn_hi(r + 1, j, "t_turned", "xt_hi", xt)
            if a:
                e.wait_ge(S["var_ready"], r + 1)
                e.activation(sd[:, :], va[:, :], ACT.Sqrt).then_inc(S["sd_ready"], 1)
                e.wait_ge(S["zs_ready"], r + 1)
                for j in range(GT):
                    e.activation(xn3[:, j, :], z[:, j, :], ACT.Identity, bias=n3[:, j:j + 1], scale=r3[:, j:j + 1])\
                     .then_inc(S["zn_ready"], 1)

        normed(0, 16, range(GT))
        for j in range(GT):
            turn_hi(0, j, "t_turned", "xt_hi", xt)
        rounds(e, body)

    @block.vector
    def _(e):
        ca, cb = Chain(e, S["tail_chain"]), Chain(e, S["chain_b"])
        e.sem_inc(S["xt_lo"], GT)
        e.sem_inc(S["zt_lo"], GT)
        e.sem_inc(S["qn_ready"], KD)
        e.sem_inc(S["hg_ready"], 4)
        e.sem_inc(S["z_ready"], GT)
        e.sem_inc(S["r_taken"], 1)
        e.sem_inc(S["c_taken"], 1)
        e.sem_inc(S["gs_lo"], 1)
        cb.link(e.memset(run[:, :], 0.0))
        e.sem_inc(S["out_ready"], 2 * GT)

        def turn_lo(g, j, hi, lo, dst):
            e.wait_ge(S[hi], g * GT + j + 1)
            e.tensor_tensor(dst[:, 1, :, j * P:(j + 1) * P], pst[j % 2][:, :].rearrange("p (k n) -> p k n", k=KD),
                            dst[:, 0, :, j * P:(j + 1) * P].bitcast(f32), ALU.subtract).then_inc(S[lo], 1)

        def body(r, a, b, ahead):
            if isinstance(r, int):
                ca.base, cb.base = r * STEPS_A, (r - 1) * STEPS_B + 1
            else:
                ca.base, cb.base = e.snap(r * STEPS_A), e.snap((r - 1) * STEPS_B + 1)
            ca.n = cb.n = 0
            g = r - 1
            s = K["stat"]
            if a:
                for j in range(GT):
                    n = r * KD + j
                    if j == 0:
                        e.wait_ge(y_in, (r + 1) * 16)
                        e.wait_ge(S["xn_ready"], r * GT + GT)
                        e.wait_ge(S["z_ready"], r * GT + GT)
                    e.scalar_tensor_tensor(t1[:, j, :], xn[:, j, :], s[:, bass.ds(r * GT + j, 1), 2], xb[:, j, :], ALU.mult, ALU.add)\
                     .then_inc(S["sum_a"], 1)
            for qs, zs in ORDER:
                if a:
                    for j in qs:
                        feature(r, j)
                if b:
                    for j in zs:
                        turn_lo(g, j, "zt_hi", "zt_lo", zt)
            if a:
                e.wait_ge(S["m_done"], r + 1)
                e.tensor_scalar(rn[0:NE, :], psc[0:NE, :], 1e-8, None, ALU.add).then_inc(S["m_taken"], 1)
                e.wait_ge(S["m_taken"], r + 1)
                ca.link(e.reciprocal(rn[0:NE, :], rn[0:NE, :]))
                ca.link(e.tensor_copy(rs[:, 0, :], rn[0:NE, :]))
                e.tensor_tensor(rs[:, 1, :], rn[0:NE, :], rs[:, 0, :].bitcast(f32), ALU.subtract).then_inc(S["rs_ready"], 1)
            if b:
                choose(g)
                gates(g)
            if a:
                for j in range(KD):
                    e.wait_ge(S["n_done"], r * KD + j + 1)
                    e.tensor_tensor(qf[:, j, :], qf[:, j, :], bank("n", j)[:, :], ALU.mult).then_inc(S["qn_ready"], 1)
            if b:
                e.wait_ge(S["gt_done"], g + 1)
                cb.link(e.tensor_copy(gs[:, 0, :], pss[0:NE, 0:GN]))
                e.tensor_tensor(gs[:, 1, :], pss[0:NE, 0:GN], gs[:, 0, :].bitcast(f32), ALU.subtract).then_inc(S["gs_lo"], 1)
            if ahead:
                for j in range(2):
                    turn_lo(r + 1, j, "xt_hi", "xt_lo", xt)
            if b:
                for j in range(2):
                    e.wait_ge(S["g_done"], g * 2 + j + 1)
                    e.wait_ge(S["h_taken"], g * 2 + j + 1 + 4)
                    e.tensor_tensor(hg[:, j, :], hg[:, j, :], bank("g", j)[:, :], ALU.mult).then_inc(S["hg_ready"], 1)
            if ahead:
                for j in range(2, GT):
                    turn_lo(r + 1, j, "xt_hi", "xt_lo", xt)
            for j in range(GT):
                if b:
                    e.wait_ge(S["w_done"], g * GT + j + 1)
                    if j == 0 and not first(g):
                        e.wait_ge(stored, g * 16)
                    e.tensor_tensor(ob[:, j, :], bank("w", j)[:, :], z[:, j, :], ALU.add).then_inc(S["out_ready"], 1)
                if a:
                    e.wait_ge(S["o_done"], r * GT + j + 1)
                    e.wait_ge(S["sum_ready"], r * GT + j + 1 + GT)
                    if b:
                        e.wait_ge(S["out_ready"], g * GT + 2 * GT + j + 1)
                    e.tensor_tensor(z[:, j, :], bank("o", j)[:, :], t1[:, j, :], ALU.add).then_inc(S["z_ready"], 1)
                    e.wait_ge(S["z_ready"], r * GT + j + 1 + GT)
                    ca.link(e.bn_stats(bn[:, :], z[:, j, :]))
                    e.sem_inc(S["dve_apart"], 1)
                    ca.link(e.bn_aggr(mv[:, j, :], bn[:, :]))
            if a:
                e.tensor_scalar(va[:, :], mv[:, :, 1], LN_EPS, None, ALU.add).then_inc(S["var_ready"], 1)
                e.wait_ge(S["sd_ready"], r + 1)
                ca.link(e.reciprocal(r3[:, :], sd[:, :]))
                e.scalar_tensor_tensor(n3[:, :], mv[:, :, 0], -1.0, r3[:, :], ALU.mult, ALU.mult).then_inc(S["zs_ready"], 1)
            assert ca.n == (STEPS_A if a else 0) and cb.n == (STEPS_B if b else 0), (ca.n, cb.n)

        def feature(r, j):
            n = r * KD + j
            e.wait_ge(S["qrelu_ready"], n + 1)
            e.wait_ge(S["q_taken"], n + 1 + KD)
            if j == 0:
                e.wait_ge(S["qp_lo"], r * KD + KD)
            e.scalar_tensor_tensor(qf[:, j, :], qe[:, :], 1.0, qz[:, j % 2, :], ALU.min, ALU.add).then_inc(S["q_ready"], 1)

        v = lambda i: t4[:, i, :]
        wide = lambda i: t4[:, i, :].unsqueeze(2).to_broadcast([P, GT, NE])

        def choose(g):
            e.wait_ge(S["r_done"], g + 1)
            e.tensor_tensor(lg[:, :, :], pss[:, 0:GT * NE].rearrange("p (j e) -> p j e", j=GT), T["br"][:, :, :], ALU.add)\
             .then_inc(S["r_taken"], 1)
            e.wait_ge(S["r_taken"], g + 2)
            cb.link(e.tensor_reduce(v(0), lg[:, :, :], axis=AX.X, op=ALU.max))
            e.tensor_tensor(lg[:, :, :], lg[:, :, :], wide(0), ALU.subtract).then_inc(S["lg_ready"], 1)
            e.wait_ge(S["re_ready"], g + 1)
            cb.link(e.reduce_sum(v(1), pe[:, :, :], axis=AX.X))
            cb.link(e.reciprocal(v(1), v(1)))
            cb.link(e.tensor_tensor(pr[:, :, :], pe[:, :, :], wide(1), ALU.mult))
            e.sem_inc(S["dve_apart"], 1)
            for j in range(GT):
                cb.mark(e.max(m8[:, j, :], pr[:, j, :]))
            cb.sync()
            e.sem_inc(S["dve_apart"], 1)
            for j in range(GT):
                cb.mark(e.max_index(i8u[:, j, :], m8[:, j, :], pr[:, j, :]))
            cb.mark(e.tensor_tensor(v(2), m8[:, :, 0], m8[:, :, 1], ALU.add))
            cb.sync()
            cb.mark(e.tensor_copy(i8f[:, :, :], i8u[:, :, :]))
            cb.link(e.tensor_scalar(v(2), v(2), 1e-9, None, ALU.add))
            it8 = T["i8"][:, :].unsqueeze(1).to_broadcast([P, GT, NE])
            cb.mark(e.tensor_tensor(s0[:, :, :], it8, i8f[:, :, 0:1].to_broadcast([P, GT, NE]), ALU.is_equal))
            cb.mark(e.tensor_tensor(s1[:, :, :], it8, i8f[:, :, 1:2].to_broadcast([P, GT, NE]), ALU.is_equal))
            cb.link(e.reciprocal(v(2), v(2)))
            cb.link(e.tensor_tensor(s0[:, :, :], s0[:, :, :], s1[:, :, :], ALU.add))
            e.tensor_copy(sl[:, :, :], s0[:, :, :]).then_inc(S["sel_ready"], 1)
            cb.link(e.tensor_tensor(tw[:, :, :], pr[:, :, :], wide(2), ALU.mult))
            cb.link(e.tensor_tensor(tw[:, :, :], tw[:, :, :], s0[:, :, :], ALU.mult))

        def gates(g):
            e.wait_ge(S["c_done"], g + 1)
            e.wait_ge(S["c_taken"], g + 1)
            cb.link(e.tensor_tensor(po[:, :, :], psc[:, 0:GT * NE].rearrange("p (j e) -> p j e", j=GT),
                                   run[:, :].unsqueeze(1).to_broadcast([P, GT, NE]), ALU.add))
            e.tensor_tensor(run[:, :], run[:, :], psc[:, GT * NE:(GT + 1) * NE], ALU.add).then_inc(S["c_taken"], 1)
            cb.link(e.tensor_scalar(po[:, :, :], po[:, :, :], float(CAP), None, ALU.is_lt))
            cb.link(e.tensor_tensor(tw[:, :, :], tw[:, :, :], po[:, :, :], ALU.mult))
            cb.link(e.reduce_sum(v(3), tw[:, :, :], axis=AX.X))
            cb.link(e.tensor_scalar(v(3), v(3), 1e-9, None, ALU.add))
            cb.link(e.reciprocal(v(3), v(3)))
            e.tensor_tensor(ga[:, :, :], tw[:, :, :], wide(3), ALU.mult).then_inc(S["gate_ready"], 1)

        for j in range(GT):
            turn_lo(0, j, "xt_hi", "xt_lo", xt)
        rounds(e, body)

    @block.tensor
    def _(e):
        PARTS = ((0, 0), (0, 1), (1, 0))

        def turn_x(g, tiles):
            for j in tiles:
                e.wait_ge(S["xn_ready"], g * GT + j + 1)
                if j < 2 and isinstance(g, int) and g == 1:
                    e.wait_ge(S["xt_lo"], GT + j + 3)
                elif j < 2 and not first(g):
                    e.wait_ge(S["zt_lo"], (g - 1) * GT + j + 3)
                elif j >= 2:
                    e.wait_ge(S["xt_lo"], g * GT + j - 1 + GT)
                for k in range(KD):
                    last = e.transpose(pst[j % 2][:, k * P:(k + 1) * P], xn[:, j, k * P:(k + 1) * P], K["ident"][:, :])
                last.then_inc(S["t_turned"], 1)

        def turn_z(g, tiles):
            for j in tiles:
                e.wait_ge(S["zn_ready"], g * GT + j + 1)
                if j < 2 and isinstance(g, int) and g == NG - 1:
                    e.wait_ge(S["zt_lo"], g * GT + j + 3)
                elif j < 2:
                    e.wait_ge(S["xt_lo"], (g + 2) * GT + j + 3)
                else:
                    e.wait_ge(S["zt_lo"], g * GT + j - 1 + GT)
                for k in range(KD):
                    last = e.transpose(pst[j % 2][:, k * P:(k + 1) * P], xn3[:, j, k * P:(k + 1) * P], K["ident"][:, :])
                last.then_inc(S["z_turned"], 1)

        def query(r, j, a, b):
            wait_bank(e, r, "q", j, a, b)
            for k in range(KD):
                for n, (m, w) in enumerate(PARTS):
                    last = e.matmul(bank("q", j)[:, :], wq[:, w, k, j * P:(j + 1) * P], xt[:, m, k, :],
                                    start=(k == 0 and n == 0), stop=(k == KD - 1 and n == 2))
            last.then_inc(S["q_done"], 1)

        def hidden(r, j, a, b):
            wait_bank(e, r, "h", j, a, b)
            for k in range(KD):
                for n, (m, w) in enumerate(PARTS):
                    last = e.matmul(bank("h", j)[:, :], T["w1"][:, w, k, j * P:(j + 1) * P], zt[:, m, k, :],
                                    start=(k == 0 and n == 0), stop=(k == KD - 1 and n == 2))
            last.then_inc(S["h_done"], 1)

        def normaliser(r, ks):
            for k in ks:
                e.wait_ge(S["q_ready"], r * KD + k + 1)
                last = e.matmul(psc[0:NE, :], T["ks"][:, k, :], qf[:, k, :], start=(k == 0), stop=(k == KD - 1))
            return last

        def spread_norm(r, j, a, b):
            wait_bank(e, r, "n", j, a, b)
            e.wait_ge(S["rs_ready"], r + 1)
            for n in range(2):
                last = e.matmul(bank("n", j)[:, :], T["head"][:, j * P:(j + 1) * P], rs[:, n, :], start=(n == 0), stop=(n == 1))
            last.then_inc(S["n_done"], 1)

        def body(r, a, b, ahead):
            g = r - 1
            if a:
                e.wait_ge(S["xt_lo"], r * GT + 2 * GT)
                for j in range(3):
                    query(r, j, a, b)
            if b:
                turn_z(g, (0, 1))
            if a:
                query(r, 3, a, b)
            if a:
                if not first(r):
                    e.wait_ge(S["c_taken"], r)
                normaliser(r, (0, 1))
            if b:
                turn_z(g, (2, 3))
            if a:
                normaliser(r, (2, 3)).then_inc(S["m_done"], 1)
            if b:
                e.wait_ge(S["gs_lo"], g + 1)
                e.wait_ge(S["zt_lo"], g * GT + 2 * GT)
                for k in range(KD):
                    for n, (m, w) in enumerate(PARTS):
                        last = e.matmul(pss[0:NE, :], T["wr"][:, w, k, :], zt[:, m, k, :],
                                        start=(k == 0 and n == 0), stop=(k == KD - 1 and n == 2))
                last.then_inc(S["rt_done"], 1)
                hidden(r, 0, a, b)
                wait_apart(e, S["lt_ready"], g + 1, S["pe_apart_t"])
                for j in range(GT):
                    last = e.transpose(pss[:, j * NE:(j + 1) * NE], lt[:, j * P:(j + 1) * P], K["ident"][0:NE, 0:NE])
                last.then_inc(S["r_done"], 1)
                hidden(r, 1, a, b)
            if a:
                for j in (0, 1):
                    spread_norm(r, j, a, b)
            if b:
                e.wait_ge(S["sel_ready"], g + 1)
                if a:
                    e.wait_ge(S["m_taken"], r + 1)
                for j in range(GT + 1):
                    before = range(j)
                    o = psc[:, j * NE:(j + 1) * NE]
                    for i in before:
                        last = e.matmul(o, T["one"][:, :], sl[:, i, :], start=(i == 0), stop=(j == GT and i == GT - 1))
                    if j < GT:
                        last = e.matmul(o, T["tri"][:, :], sl[:, j, :], start=(j == 0), stop=True)
                last.then_inc(S["c_done"], 1)
            if a:
                for j in (2, 3):
                    spread_norm(r, j, a, b)
            if ahead:
                turn_x(r + 1, (0, 1))
            if b:
                e.wait_ge(S["gate_ready"], g + 1)
                e.wait_ge(S["r_taken"], g + 2)
                for j in range(GT):
                    last = e.transpose(pss[0:NE, j * P:(j + 1) * P], ga[:, j, :], K["ident"][:, :])
                last.then_inc(S["gt_done"], 1)
                for j in range(2):
                    wait_bank(e, r, "g", j, a, b)
                    e.wait_ge(S["gs_lo"], g + 2)
                    for n in range(2):
                        last = e.matmul(bank("g", j)[:, :], T["sel"][:, j * P:(j + 1) * P], gs[:, n, :], start=(n == 0), stop=(n == 1))
                    last.then_inc(S["g_done"], 1)
            if ahead:
                turn_x(r + 1, (2, 3))
            for j in range(GT):
                if a:
                    e.wait_ge(S["qp_lo"], r * KD + 2 * KD)
                    wait_bank(e, r, "o", j, a, b)
                    for k in range(KD):
                        for n, (m, w) in enumerate(PARTS):
                            last = e.matmul(bank("o", j)[:, :], qp[:, m, k, j * P:(j + 1) * P], T["mw"][:, w, k, :],
                                            start=(k == 0 and n == 0), stop=(k == KD - 1 and n == 2))
                    last.then_inc(S["o_done"], 1)
                if b:
                    wait_bank(e, r, "w", j, a, b)
                    wait_apart(e, S["hs_lo"], g * 2 + 4, S["pe_apart_t"])
                    t = slice(j * P, (j + 1) * P)
                    for n, (m, w) in enumerate(PARTS):
                        e.matmul(bank("w", j)[:, :], gs[:, m, t], T["b2"][:, w, :], start=(n == 0), stop=False)
                    for k in range(2):
                        for n, (m, w) in enumerate(PARTS):
                            last = e.matmul(bank("w", j)[:, :], hs[:, m, k, t], T["w2"][:, w, k, :],
                                            start=False, stop=(k == 1 and n == 2))
                    last.then_inc(S["w_done"], 1)

        turn_x(0, range(GT))
        rounds(e, body)


STEPS_A, STEPS_B = 11, 28


_INS = ['x', 'src', 'dst', 'L0_gnn_W1', 'L0_gnn_a_src1', 'L0_gnn_a_dst1', 'L0_gnn_b1', 'L0_gnn_W2', 'L0_gnn_a_src2',
        'L0_gnn_a_dst2', 'L0_gnn_b2', 'L0_gnn_Wfc', 'L0_gnn_bfc', 'L0_mix_qkv_w', 'L0_mix_qkv_b', 'L0_mix_out_w',
        'L0_mix_out_b', 'L0_mix_ln_gamma', 'L0_mix_ln_beta', 'L0_ffn_Wr', 'L0_ffn_br', 'L0_ffn_W1', 'L0_ffn_b1',
        'L0_ffn_W2', 'L0_ffn_b2']


def kernel(**inputs):
    import numpy as _np
    import concourse.bacc as _bacc
    from concourse import mybir as _mybir
    from concourse.bass_utils import run_bass_kernel_spmd as _run

    nc = _bacc.Bacc("TRN2", target_bir_lowering=False, num_devices=1)
    arrays, args = {}, []
    for name in _INS:
        a = _np.ascontiguousarray(inputs[name])
        arrays[f"in_{name}_dram"] = a
        args.append(nc.dram_tensor(f"in_{name}_dram", a.shape, _mybir.dt.from_np(a.dtype), kind="ExternalInput").ap())
    args.append(nc.dram_tensor("out_0_dram", (N, D), f32, kind="ExternalOutput").ap())
    build(nc, *args)
    r = _run(nc, [arrays], core_ids=[0])
    return r.results[0]["out_0_dram"]
```

```python
import concourse.bass as bass
from concourse import mybir
from contextlib import ExitStack

f32 = mybir.dt.float32
f32r = mybir.dt.float32r
bf16 = mybir.dt.bfloat16
i32 = mybir.dt.int32
ALU = mybir.AluOpType
ACT = mybir.ActivationFunctionType
AX = mybir.AxisListType

P = 128
N = 10000
D = 512
HC = 1024
HEADS = 4
C = HC // HEADS
NT = -(-N // P)
LAST = N - (NT - 1) * P
NPAD = NT * P
ALS, ALD, DEN = HC, HC + HEADS, HC + 2 * HEADS
ROW = HC + 3 * HEADS
WEXT = HC + 2 * HEADS
EP, EK = 125, 100
SLOTS = 64
NITEMS = -(-(NT + (EP * EK) // SLOTS + 4) // 4) * 4
IG = NITEMS // 4
PADSLOT = 16384 * 256 + 255
NEG = -1.0e30
LN_EPS = 1e-5
NE = 8
CAP = 3125
KD = D // P
KH = HC // P
GT = 4
NG = -(-NT // GT)
assert NITEMS % 4 == 0 and IG <= P


class Chain:

    def __init__(self, eng, sem):
        self.eng, self.sem, self.n, self.base = eng, sem, 0, 0

    def mark(self, ins):
        ins.then_inc(self.sem, 1)
        self.n += 1

    def sync(self):
        self.eng.wait_ge(self.sem, self.base + self.n)

    def link(self, ins):
        self.mark(ins)
        self.sync()


def semaphores(nc, stack, suffix=""):
    taken = []

    def clear():
        nc.clear_and_free_semaphores(taken)
        nc.all_engine_barrier()

    def sem(name):
        taken.append(nc.alloc_semaphore(name + suffix))
        return taken[-1]

    stack.callback(clear)
    return sem


def wait_apart(e, sem, value, carrier):
    e.wait_ge(sem, value)
    e.sem_inc(carrier, 1)


def build(nc, x, src, dst, W1, as1, ad1, b1, W2, as2, ad2, b2, Wfc, bfc, qkv_w, qkv_b, out_w, out_b,
          gamma, beta, Wr, br, fW1, fb1, fW2, fb2, out):
    h1t = nc.dram_tensor("h1_table", (NPAD, ROW), f32)
    h2t = nc.dram_tensor("h2_table", (NPAD, ROW), f32)
    yt = nc.dram_tensor("gnn_out", (NPAD, D), f32)
    slots = nc.dram_tensor("slot_table", (NITEMS * SLOTS, 1), i32)
    keep = ExitStack()
    with keep:
        def ksb(name, shape, dt=f32):
            return keep.enter_context(nc.sbuf_tensor(name, shape, dt))

        K = {}
        K["ident"] = ksb("ident", [P, P])
        K["stat"] = ksb("stat", [P, NG * GT, 3])
        K["den0"] = ksb("den0", [P, NT])
        K["pos"] = ksb("pos", [P, EK], i32)
        K["val"] = ksb("val", [P, EK], i32)
        K["items"] = ksb("items", [1, 2 * NITEMS], i32)
        K["nitems"] = ksb("nitems", [1, 2], i32)
        K["iota"] = ksb("iota_node", [P, P])
        K["slot_src"] = ksb("slot_src", [SLOTS, NITEMS], i32)
        K["slot_dst"] = ksb("slot_dst", [SLOTS, NITEMS])
        K["bq"] = ksb("bq", [P, KD])
        K["kv"] = ksb("kv", [P, KD, P + 1])
        K["incl"] = ksb("incl", [P, P])
        dram = dict(h1t=h1t, h2t=h2t, yt=yt, slots=slots)
        with ExitStack() as st:
            wq = st.enter_context(nc.sbuf_tensor("wq", [P, 2, KD, D], f32r))
            with ExitStack() as first:
                sem = semaphores(nc, first)
                pre = dict(w1=first.enter_context(nc.sbuf_tensor("w1_stage", [P, KD, WEXT], f32)),
                           qkv=first.enter_context(nc.sbuf_tensor("qkv_stage", [P, 12, D], f32)),
                           att=first.enter_context(nc.sbuf_tensor("att_rep", [P, 2, HC], f32)),
                           loaded=sem("weights_loaded"), src=dict(w1=W1, qkv=qkv_w, att=(as1, ad1)))
                edges(nc, K, pre, src, dst, dram)
                dense_in(nc, K, pre, wq, x, qkv_b, gamma, beta, dram)
            gat(nc, K, 1, b1, W2, as2, ad2, dram["h1t"], dram["h2t"], dram)
            gat(nc, K, 2, b2, Wfc, None, None, dram["h2t"], dram["yt"], dram)
            tail(nc, K, wq, x, bfc, out_w, out_b, Wr, br, fW1, fb1, fW2, fb2, out, dram)


def edges(nc, K, pre, src, dst, dram):
    with ExitStack() as st:
        def sb(name, shape, dt=f32):
            return st.enter_context(nc.sbuf_tensor(name, shape, dt))

        sem = semaphores(nc, st)

        se = sb("src_i", [EP, EK], i32)
        de = sb("dst_i", [EP, EK], i32)
        ti = sb("tile_i", [EP, EK], i32)
        li = sb("local_i", [EP, EK], i32)
        sf, tf, lf, ed, te, tl, vf, pf = (sb(n, [EP, EK]) for n in (
            "src_f", "tile_f", "local_f", "is_edge", "tile_edge", "tile_loop", "val_f", "pos_f"))
        iot = sb("iota_tile", [P, NT])
        iop = K["iota"]
        oh = sb("edge_in_tile", [EP, NT, EK], bf16)
        ol = sb("loop_in_tile", [EP, NT, EK], bf16)
        on = sb("at_node", [EP, EK, P], bf16)
        rk = sb("rank", [P, NT, EK])
        low = sb("earlier", [P, P], bf16)
        one = sb("ones_b", [P, P], bf16)
        wrap = sb("not_first_col", [P, 5, EK])
        cnt = sb("tile_count", [P, NT])
        cnti = sb("tile_count_i", [P, NT], i32)
        end = sb("tile_end", [P, NT])
        base = sb("tile_base", [P, NT])
        itp = sb("item_number", [P, 4])
        tlt = sb("item_tile", [P, 4])
        cmp_ = sb("item_after", [P, NT])
        row = sb("item_row", [1, NITEMS])
        first = sb("item_first", [1, NITEMS])
        par = sb("item_parity", [1, NITEMS])
        offl = sb("item_base", [1, NITEMS])
        nn = sb("n_items_f", [1, 2])
        ni = sb("n_items_i", [1, 2], i32)
        pad = sb("pad_slots", [P, NITEMS * SLOTS // P], i32)
        zr = sb("zero_row", [P, NT])
        psa = [st.enter_context(nc.psum_tensor(f"ps_rank{i}", [P, 5 * EK], f32)) for i in range(2)]
        psb = [st.enter_context(nc.psum_tensor(f"ps_total{i}", [P, 5 * EK], f32)) for i in range(2)]
        psl = st.enter_context(nc.psum_tensor("ps_loops", [P, NT], f32))
        psi = st.enter_context(nc.psum_tensor("ps_items", [1, NITEMS], f32))

        loaded, consts, onehots, mm_done, evac, dv, loops_done, items_in, items_row, pads, padded = (sem(n) for n in (
            "edges_loaded", "edge_consts", "onehots_ready", "ranks_ready", "ranks_taken", "edges_dve", "loops_counted",
            "item_tiles_ready", "item_rows_ready", "pads_ready", "pads_stored"))
        pool = sem("edges_pool")
        chunks = [(a, min(a + 5, NT)) for a in range(0, NT, 5)]
        block = st.enter_context(nc.Block())

        @block.sync
        def _(e):
            e.dma_start(se[:, :], src.rearrange("(p k) -> p k", p=EP)).then_inc(loaded, 16)
            e.dma_start(de[:, :], dst.rearrange("(p k) -> p k", p=EP)).then_inc(loaded, 16)
            e.dma_start(pre["qkv"][:, :, :], pre["src"]["qkv"].rearrange("(b p) c -> p b c", p=P)).then_inc(pre["loaded"], 16)
            e.dma_start(pre["w1"][:, :, 0:HC], pre["src"]["w1"].rearrange("(k p) n -> p k n", p=P)).then_inc(pre["loaded"], 16)
            for j, a in enumerate(pre["src"]["att"]):
                e.dma_start(pre["att"][:, j, :], a.rearrange("(o h) c -> o (h c)", o=1).to_broadcast([P, HC])).then_inc(pre["loaded"], 16)
            e.wait_ge(pads, 1)
            e.dma_start(dram["slots"].ap().rearrange("(p n) o -> p (n o)", p=P), pad[:, :]).then_inc(padded, 16)
            e.wait_ge(padded, 16)
            e.wait_ge(pre["loaded"], 64)

        @block.gpsimd
        def _(e):
            pc = Chain(e, pool)
            e.memset(pad[:, :], PADSLOT).then_inc(pads, 1)
            pc.mark(e.memset(K["ident"][:, :], 0.0))
            pc.mark(e.memset(K["incl"][:, :], 1.0))
            pc.mark(e.memset(low[:, :], 0.0))
            pc.mark(e.memset(wrap[:, :, :], 1.0))
            pc.mark(e.memset(K["stat"][:, :, :], 0.0))
            pc.sync()
            pc.mark(e.affine_select(out=K["ident"][:, :], in_=K["ident"][:, :], compare_op=ALU.not_equal,
                                    fill=1.0, base=0, pattern=[[-1, P]], channel_multiplier=1))
            pc.mark(e.affine_select(out=K["incl"][:, :], in_=K["incl"][:, :], compare_op=ALU.is_gt,
                                    fill=0.0, base=0, pattern=[[1, P]], channel_multiplier=-1))
            pc.mark(e.affine_select(out=low[:, :], in_=low[:, :], compare_op=ALU.is_gt,
                                    fill=-1.0, base=0, pattern=[[1, P]], channel_multiplier=-1))
            pc.mark(e.memset(wrap[:, :, 0:1], 0.0))
            pc.mark(e.memset(one[:, :], 1.0))
            pc.mark(e.memset(zr[:, :], 1.0))
            pc.mark(e.iota(iot[:, :], pattern=[[1, NT]], base=0, channel_multiplier=0,
                           allow_small_or_imprecise_dtypes=True))
            pc.mark(e.iota(iop[:, :], pattern=[[1, P]], base=0, channel_multiplier=0,
                           allow_small_or_imprecise_dtypes=True))
            pc.mark(e.iota(itp[:, :], pattern=[[IG, 4]], base=0, channel_multiplier=1,
                           allow_small_or_imprecise_dtypes=True))
            pc.mark(e.iota(par[:, :].rearrange("p (a b) -> p a b", b=2), pattern=[[0, NITEMS // 2], [1, 2]],
                           base=0, channel_multiplier=0, allow_small_or_imprecise_dtypes=True))
            pc.sync()
            e.engine_nop().then_inc(consts, 1)

        @block.vector
        def _(e):
            c = Chain(e, dv)
            e.wait_ge(loaded, 32)
            e.wait_ge(consts, 1)
            c.mark(e.tensor_scalar(ti[:, :], de[:, :], 7, None, ALU.arith_shift_right))
            c.mark(e.tensor_scalar(li[:, :], de[:, :], 127, None, ALU.bitwise_and))
            c.mark(e.tensor_copy(sf[:, :], se[:, :]))
            c.mark(e.tensor_tensor(ed[:, :], se[:, :], de[:, :], ALU.not_equal))
            c.sync()
            c.mark(e.tensor_copy(tf[:, :], ti[:, :]))
            c.mark(e.tensor_copy(lf[:, :], li[:, :]))
            c.sync()
            c.mark(e.scalar_tensor_tensor(vf[:, :], sf[:, :], 256.0, lf[:, :], ALU.mult, ALU.add))
            c.mark(e.scalar_tensor_tensor(tl[:, :], ed[:, :], 1000.0, tf[:, :], ALU.mult, ALU.add))
            c.mark(e.tensor_scalar(te[:, :], ed[:, :], -1000.0, 1000.0, ALU.mult, ALU.add))
            c.sync()
            c.mark(e.tensor_copy(K["val"][0:EP, :], vf[:, :]))
            c.mark(e.tensor_tensor(te[:, :], te[:, :], tf[:, :], ALU.add))
            c.sync()
            e.tensor_tensor(oh[:, :, :], iot[0:EP, :].unsqueeze(2).to_broadcast([EP, NT, EK]),
                            te[:, :].unsqueeze(1).to_broadcast([EP, NT, EK]), ALU.is_equal).then_inc(onehots, 1)
            e.tensor_tensor(ol[:, :, :], iot[0:EP, :].unsqueeze(2).to_broadcast([EP, NT, EK]),
                            tl[:, :].unsqueeze(1).to_broadcast([EP, NT, EK]), ALU.is_equal).then_inc(onehots, 1)
            e.tensor_tensor(on[:, :, :], iop[0:EP, :].unsqueeze(1).to_broadcast([EP, EK, P]),
                            lf[:, :].unsqueeze(2).to_broadcast([EP, EK, P]), ALU.is_equal).then_inc(onehots, 1)
            for j, (a, b) in enumerate(chunks):
                w = (b - a) * EK
                e.wait_ge(mm_done, j + 1)
                c.link(e.tensor_tensor_scan(rk[:, a:b, :].rearrange("p a b -> p (a b)"),
                                            wrap[:, 0:b - a, :].rearrange("p a b -> p (a b)"),
                                            psb[j % 2][:, 0:w], 0.0, ALU.mult, ALU.add))
                c.link(e.tensor_copy(cnt[:, a:b], rk[:, a:b, EK - 1:EK].rearrange("p a b -> p (a b)")))
                e.tensor_tensor(rk[0:EP, a:b, :].rearrange("p a b -> p (a b)"),
                                rk[0:EP, a:b, :].rearrange("p a b -> p (a b)"),
                                psa[j % 2][0:EP, 0:w], ALU.add).then_inc(evac, 1)
            e.wait_ge(evac, len(chunks))
            c.link(e.tensor_scalar(cnt[:, :], cnt[:, :], float(SLOTS - 1), None, ALU.add))
            c.link(e.tensor_copy(cnti[:, :], cnt[:, :]))
            c.link(e.tensor_scalar(cnti[:, :], cnti[:, :], 6, None, ALU.arith_shift_right))
            c.link(e.tensor_copy(cnt[:, :], cnti[:, :]))
            c.link(e.tensor_scalar(cnt[:, :], cnt[:, :], 1.0, None, ALU.max))
            c.link(e.tensor_tensor_scan(end[:, :], zr[:, :], cnt[:, :], 0.0, ALU.mult, ALU.add))
            c.link(e.tensor_tensor(base[:, :], end[:, :], cnt[:, :], ALU.subtract))
            c.link(e.tensor_scalar(base[:, :], base[:, :], float(SLOTS), None, ALU.mult))
            c.link(e.tensor_tensor(rk[0:EP, :, :], rk[0:EP, :, :],
                                   base[0:EP, :].unsqueeze(2).to_broadcast([EP, NT, EK]), ALU.add))
            c.link(e.tensor_tensor(rk[0:EP, :, :], rk[0:EP, :, :], oh[:, :, :], ALU.mult))
            c.link(e.tensor_reduce(pf[:, :], rk[0:EP, :, :].rearrange("p t k -> p k t"), axis=AX.X, op=ALU.add))
            c.link(e.tensor_scalar(vf[:, :], ed[:, :], -1048576.0, 1048576.0, ALU.mult, ALU.add))
            c.link(e.tensor_tensor(pf[:, :], pf[:, :], vf[:, :], ALU.add))
            c.link(e.tensor_copy(K["pos"][0:EP, :], pf[:, :]))
            for g in range(4):
                c.link(e.tensor_scalar(cmp_[:, :], end[:, :], itp[:, g:g + 1], None, ALU.is_le))
                c.link(e.reduce_sum(tlt[:, g:g + 1], cmp_[:, :], axis=AX.X))
            e.tensor_scalar(tlt[:, :], tlt[:, :], float(NT - 1), None, ALU.min).then_inc(items_in, 1)
            e.wait_ge(items_row, 1)
            c.link(e.tensor_copy(row[:, :], psi[:, :]))
            c.mark(e.tensor_copy(K["items"][:, 0:NITEMS], row[:, :]))
            c.link(e.memset(first[:, :], 1.0))
            c.link(e.tensor_tensor(first[:, 1:NITEMS], row[:, 1:NITEMS], row[:, 0:NITEMS - 1], ALU.not_equal))
            c.link(e.tensor_scalar(offl[:, :], par[:, :], 2.0, -3.0, ALU.mult, ALU.add))
            c.link(e.tensor_tensor(offl[:, :], offl[:, :], first[:, :], ALU.mult))
            c.link(e.tensor_tensor(offl[:, :], offl[:, :], par[:, :], ALU.subtract))
            c.link(e.tensor_scalar(offl[:, :], offl[:, :], 3.0, float(ROW), ALU.add, ALU.mult))
            c.link(e.tensor_copy(K["items"][:, NITEMS:2 * NITEMS], offl[:, :]))
            c.link(e.tensor_scalar(nn[:, 0:1], end[0:1, NT - 1:NT], 1.0, None, ALU.add))
            c.link(e.tensor_copy(ni[:, 0:1], nn[:, 0:1]))
            c.link(e.tensor_scalar(K["nitems"][:, 0:1], ni[:, 0:1], 1, None, ALU.arith_shift_right))
            e.wait_ge(loops_done, 1)
            c.link(e.tensor_scalar(K["den0"][:, :], psl[:, :], 1.0, None, ALU.add))

        @block.tensor
        def _(e):
            e.wait_ge(consts, 1)
            e.wait_ge(onehots, 1)
            for j, (a, b) in enumerate(chunks):
                w = (b - a) * EK
                if j >= 2:
                    e.wait_ge(evac, j - 1)
                m = oh[:, a:b, :].rearrange("p a b -> p (a b)")
                e.matmul(psb[j % 2][:, 0:w], one[0:EP, :], m, start=True, stop=True)
                e.matmul(psa[j % 2][:, 0:w], low[0:EP, :], m, start=True, stop=True).then_inc(mm_done, 1)
            e.wait_ge(onehots, 3)
            for k in range(EK):
                last = e.matmul(psl[:, :], on[:, k, :], ol[:, :, k], start=(k == 0), stop=(k == EK - 1))
            last.then_inc(loops_done, 1)
            e.wait_ge(items_in, 1)
            for g in range(4):
                last = e.matmul(psi[:, g * IG:(g + 1) * IG], tlt[0:IG, g:g + 1], K["ident"][0:IG, 0:IG],
                                start=True, stop=True)
            last.then_inc(items_row, 1)


def dense_in(nc, K, pre, wq, x, qkv_b, gamma, beta, dram):
    with ExitStack() as st:
        def sb(name, shape, dt=f32):
            return st.enter_context(nc.sbuf_tensor(name, shape, dt))

        w1 = sb("w1", [P, 2, KD, WEXT], f32r)
        wkv = sb("wkv", [P, 2, KD, 2 * D], f32r)
        bkv = sb("bkv", [P, 2 * D])
        with ExitStack() as prep:
            weights_in(nc, K, pre, prep, w1, wkv, bkv, wq, qkv_b, gamma, beta)
        tiles_in(nc, K, st, w1, wkv, bkv, x, dram)


def weights_in(nc, K, pre, st, w1, wkv, bkv, wq, qkv_b, gamma, beta):
    def sb(name, shape, dt=f32):
        return st.enter_context(nc.sbuf_tensor(name, shape, dt))

    sem = semaphores(nc, st)

    w1s, qs, arep = pre["w1"], pre["qkv"], pre["att"]
    raw = sb("qkv_t", [P, KD, 3 * D])
    tmp = sb("att_prod", [P, 2, 2, HC])
    gc, bc, qb = sb("gamma_c", [P, KD]), sb("beta_c", [P, KD]), sb("qb_c", [P, KD])
    brep = sb("beta_rep", [P, KD, P])
    kvb = sb("kv_bias_rep", [P, 2 * D])
    pst = [st.enter_context(nc.psum_tensor(f"ps_wt{i}", [P, D], f32)) for i in range(2)]
    psb = [st.enter_context(nc.psum_tensor(f"ps_wb{i}", [P, D], f32)) for i in range(2)]
    psq = st.enter_context(nc.psum_tensor("ps_qb", [P, KD], f32))
    small_in, turned, taken, q_hi, w_hi, pool_prod, folded, pool_lo, rep_ready, bias_mm, dv = (sem(n) for n in (
        "small_loaded", "qkv_turned", "qkv_taken", "qkv_hi", "w1_hi", "att_products", "att_folded", "w1_lo_pool",
        "beta_rep_ready", "bias_products", "weights_dve"))
    block = st.enter_context(nc.Block())
    BLOCKS = [(b, k) for b in range(3) for k in range(KD)]

    def part(b, i, k):
        return wq[:, i, k, :] if b == 0 else wkv[:, i, k, (b - 1) * D:b * D]

    @block.scalar
    def _(e):
        for t, s in ((gc, gamma), (bc, beta), (qb, qkv_b[0:D])):
            e.dma_start(t[:, :], s.rearrange("(k p) -> p k", p=P), allow_slow_non_contiguous=True).then_inc(small_in, 16)
        e.dma_start(kvb[:, :], qkv_b[D:3 * D].rearrange("(o c) -> o c", o=1).to_broadcast([P, 2 * D])).then_inc(small_in, 16)
        for k in range(KD):
            e.activation(w1[:, 0, k, 0:HC], w1s[:, k, 0:HC], ACT.Copy).then_inc(w_hi, 1)
        e.wait_ge(small_in, 64)
        for n, (b, k) in enumerate(BLOCKS):
            e.wait_ge(turned, n + 1)
            e.activation(raw[:, k, b * D:(b + 1) * D], pst[n % 2][:, :], ACT.Copy).then_inc(taken, 1)
            e.wait_ge(taken, n + 1)
            e.activation(part(b, 0, k), raw[:, k, b * D:(b + 1) * D], ACT.Copy, scale=gc[:, k:k + 1]).then_inc(q_hi, 1)

    @block.gpsimd
    def _(e):
        for k in range(KD):
            if k >= 2:
                e.wait_ge(folded, k - 1)
            e.tensor_tensor(tmp[:, 0, k % 2, :], w1s[:, k, 0:HC], arep[:, 0, :], ALU.mult).then_inc(pool_prod, 1)
            if k % 2 == 0:
                e.wait_ge(w_hi, k + 1)
                e.tensor_tensor(w1[:, 1, k, 0:HC], w1s[:, k, 0:HC], w1[:, 0, k, 0:HC].bitcast(f32), ALU.subtract).then_inc(pool_lo, 1)
        e.wait_ge(pool_lo, KD // 2)

    @block.tensor
    def _(e):
        for n, (b, k) in enumerate(BLOCKS):
            if n >= 2:
                e.wait_ge(taken, n - 1)
            for j in range(4):
                last = e.transpose(pst[n % 2][:, j * P:(j + 1) * P], qs[:, 4 * b + j, k * P:(k + 1) * P], K["ident"][:, :])
            last.then_inc(turned, 1)
        e.wait_ge(taken, 12)
        e.wait_ge(rep_ready, 1)
        for b in range(2):
            for k in range(KD):
                e.matmul(psb[b][:, :], brep[:, k, :], raw[:, k, (b + 1) * D:(b + 2) * D], start=(k == 0), stop=(k == KD - 1))
        for b in range(KD):
            for k in range(KD):
                last = e.matmul(psq[:, b:b + 1], raw[:, k, b * P:(b + 1) * P], bc[:, k:k + 1], start=(k == 0), stop=(k == KD - 1))
        last.then_inc(bias_mm, 1)

    @block.vector
    def _(e):
        c = Chain(e, dv)
        for k in range(KD):
            c.link(e.tensor_tensor(tmp[:, 1, k % 2, :], w1s[:, k, 0:HC], arep[:, 1, :], ALU.mult))
            c.mark(e.reduce_sum(w1s[:, k, HC + 4:WEXT], tmp[:, 1, k % 2, :].rearrange("p (h c) -> p h c", h=HEADS), axis=AX.X))
            e.wait_ge(pool_prod, k + 1)
            e.reduce_sum(w1s[:, k, HC:HC + 4], tmp[:, 0, k % 2, :].rearrange("p (h c) -> p h c", h=HEADS), axis=AX.X).then_inc(folded, 1)
            if k % 2:
                e.wait_ge(w_hi, k + 1)
                c.mark(e.tensor_tensor(w1[:, 1, k, 0:HC], w1s[:, k, 0:HC], w1[:, 0, k, 0:HC].bitcast(f32), ALU.subtract))
        e.wait_ge(folded, KD)
        c.sync()
        c.link(e.tensor_copy(w1[:, 0, :, HC:WEXT], w1s[:, :, HC:WEXT]))
        c.mark(e.tensor_tensor(w1[:, 1, :, HC:WEXT], w1s[:, :, HC:WEXT], w1[:, 0, :, HC:WEXT].bitcast(f32), ALU.subtract))
        e.wait_ge(small_in, 64)
        e.tensor_copy(brep[:, :, :], bc[:, :].unsqueeze(2).to_broadcast([P, KD, P])).then_inc(rep_ready, 1)
        for n, (b, k) in enumerate(BLOCKS):
            e.wait_ge(q_hi, n + 1)
            c.mark(e.scalar_tensor_tensor(part(b, 1, k), raw[:, k, b * D:(b + 1) * D], gc[:, k:k + 1], part(b, 0, k).bitcast(f32),
                                          ALU.mult, ALU.subtract))
        e.wait_ge(bias_mm, 1)
        for b in range(2):
            c.mark(e.tensor_tensor(bkv[:, b * D:(b + 1) * D], kvb[:, b * D:(b + 1) * D], psb[b][:, :], ALU.add))
        c.link(e.tensor_tensor(K["bq"][:, :], qb[:, :], psq[:, :], ALU.add))


def tiles_in(nc, K, st, w1, wkv, bkv, x, dram):
    def sb(name, shape, dt=f32):
        return st.enter_context(nc.sbuf_tensor(name, shape, dt))

    sem = semaphores(nc, st)

    ps = lambda name, w=D: st.enter_context(nc.psum_tensor(name, [P, w], f32))
    xb = sb("x_rows", [P, 2, D])
    bn = sb("bn", [P, 6])
    mv = sb("mean_var", [P, 2])
    sc = sb("norm_vars", [P, 3])
    sq = sb("norm_roots", [P, 2])
    xn = sb("x_norm", [P, D])
    xt = sb("x_norm_t", [P, 2, 2, D], f32r)
    ho = sb("h_rows", [P, 2, ROW])
    kz, km, ke = sb("k_pre", [P, D]), sb("k_relu", [P, D]), sb("k_exp", [P, D])
    kf = sb("k_feat", [P, 2, D])
    vf = sb("v_rows", [P, 2, KD, P + 1])
    lt = sb("logits_t", [2 * HEADS, P])
    idx = sb("slot_of", [EP, 2, 2], i32)
    pst, psh0, psh1, psk, psv, pss, pskv0, pskv1 = (
        ps(n, w) for n, w in (("ps_t", D), ("ps_h0", D), ("ps_h1", D), ("ps_k", D), ("ps_v", D), ("ps_al", D),
                              ("ps_kv0", D), ("ps_kv1", D)))
    x_in = [sem("x_in0"), sem("x_in1")]
    h_out = [sem("h_out0"), sem("h_out1")]
    names = ("var_ready roots_ready scales_ready xn_ready x_turned hi_ready lo_ready h_done h_taken al_taken alt_done lt_ready al_done "
             "k_done v_done k_taken v_taken kexp_ready kv_ready kvt_done kvt_taken "
             "a_dve bn_seen slot_free slot_copied pe_apart").split()
    S = {n: sem(n) for n in names}
    slotdma = [sem(f"slot_dma{i}") for i in range(2)]
    TRIPS = NT // 2
    assert NT == 2 * TRIPS + 1
    block = st.enter_context(nc.Block())

    @block.sync
    def _(e):
        with e.Fori(0, TRIPS) as t:
            it = e.snap(t)
            for p in range(2):
                i = it * 2 + p
                e.wait_ge(S["xn_ready"], i + 1)
                e.dma_start(xb[:, p, :], x[bass.ds(i * P, P), :]).then_inc(x_in[p], 16)
        e.wait_ge(S["xn_ready"], NT)
        e.dma_start(xb[0:LAST, 0, :], x[(NT - 1) * P:N, :]).then_inc(x_in[0], 16)
        e.wait_ge(x_in[0], 16 * (TRIPS + 1))

    @block.gpsimd
    def _(e):
        with e.Fori(0, EK // 2) as t:
            it = e.snap(t)
            for p in range(2):
                k = it * 2 + p
                e.tensor_copy(idx[:, p, 0:1], K["pos"][0:EP, bass.ds(k, 1)]).then_inc(S["slot_copied"], 1)
                e.tensor_copy(idx[:, p, 1:2], K["val"][0:EP, bass.ds(k, 1)]).then_inc(S["slot_copied"], 1)
                wait_apart(e, S["slot_copied"], k * 2 + 2, S["slot_free"])
                e.indirect_dma_start(out=dram["slots"].ap(), out_offset=bass.IndirectOffsetOnAxis(ap=idx[:, p, 0:1], axis=0),
                                     in_=idx[:, p, 1:2], in_offset=None, bounds_check=NITEMS * SLOTS - 1,
                                     oob_is_err=False).then_inc(slotdma[p], 16)
                wait_apart(e, slotdma[p], it * 16 + 16, S["slot_free"])

    @block.scalar
    def _(e):
        e.sem_inc(S["xn_ready"], 2)
        e.sem_inc(S["h_taken"], 1)
        e.sem_inc(S["kexp_ready"], 1)
        for p in range(2):
            e.sem_inc(h_out[p], 16)

        def normalise(i, p):
            e.wait_ge(S["var_ready"], i + 1)
            e.activation(sq[:, :], sc[:, 0:2], ACT.Sqrt).then_inc(S["roots_ready"], 1)
            e.wait_ge(S["x_turned"], i + 1)
            e.wait_ge(S["scales_ready"], i + 1)
            e.activation(xn[:, :], xb[:, p, :], ACT.Identity, bias=K["stat"][:, bass.ds(i, 1), 1],
                         scale=K["stat"][:, bass.ds(i, 1), 0]).then_inc(S["xn_ready"], 1)

        def high(i, p):
            e.wait_ge(S["x_turned"], i + 2)
            e.wait_ge(S["v_done"], i + 1)
            e.activation(xt[:, p, 0, :], pst[:, :], ACT.Copy).then_inc(S["hi_ready"], 1)

        def body(i, it, p, ahead=True):
            if ahead:
                normalise(i + 1, 1 - p)
            e.wait_ge(S["h_done"], i + 1)
            e.wait_ge(h_out[p], it * 16 + 16)
            q = K["stat"][:, bass.ds(i, 1), 2]
            e.activation(ho[:, p, 0:D], psh0[:, :], ACT.Copy, scale=q)
            e.activation(ho[:, p, D:HC], psh1[:, :], ACT.Copy, scale=q).then_inc(S["h_taken"], 1)
            e.wait_ge(S["alt_done"], i + 1)
            e.activation(lt[:, :], pss[0:2 * HEADS, 0:P], ACT.Copy).then_inc(S["lt_ready"], 1)
            if ahead:
                high(i + 1, 1 - p)
            e.wait_ge(S["k_taken"], i + 2)
            e.activation(ke[:, :], kz[:, :], ACT.Exp)
            e.activation(km[:, :], kz[:, :], ACT.Relu).then_inc(S["kexp_ready"], 1)
            e.wait_ge(S["h_taken"], i + 2)
            e.wait_ge(S["al_taken"], i + 2)
            e.dma_start(dram["h1t"].ap()[bass.ds(i * P, P), :], ho[:, p, :]).then_inc(h_out[p], 16)

        normalise(0, 0)
        high(0, 0)
        with e.Fori(0, TRIPS) as t:
            it = e.snap(t)
            for p in range(2):
                body(e.snap(it * 2 + p), it, p)
        body(NT - 1, TRIPS, 0, ahead=False)
        e.wait_ge(h_out[0], 16 * (TRIPS + 2))
        e.wait_ge(h_out[1], 16 * (TRIPS + 1))

    @block.vector
    def _(e):
        c = Chain(e, S["a_dve"])

        def stats(i, it, p):
            e.wait_ge(x_in[p], it * 16 + 16)
            c.link(e.bn_stats(bn[:, :], xb[:, p, :]))
            e.sem_inc(S["bn_seen"], 1)
            c.link(e.bn_aggr(mv[:, :], bn[:, :]))
            c.mark(e.tensor_scalar(sc[:, 2:3], mv[:, 1:2], LN_EPS, None, ALU.add))
            c.link(e.tensor_scalar(sc[:, 0:1], mv[:, 1:2], 1.0 + LN_EPS, LN_EPS * LN_EPS, ALU.mult, ALU.add))
            c.link(e.reciprocal(sc[:, 2:3], sc[:, 2:3]))
            e.tensor_tensor(sc[:, 1:2], sc[:, 0:1], sc[:, 2:3], ALU.mult).then_inc(S["var_ready"], 1)
            e.wait_ge(S["roots_ready"], i + 1)
            s = K["stat"][:, bass.ds(i, 1), :]
            c.mark(e.tensor_copy(K["stat"][:, bass.ds(i, 1), 2], sq[:, 1:2]))
            c.link(e.reciprocal(K["stat"][:, bass.ds(i, 1), 0], sq[:, 0:1]))
            e.scalar_tensor_tensor(K["stat"][:, bass.ds(i, 1), 1], mv[:, 0:1], -1.0, K["stat"][:, bass.ds(i, 1), 0],
                                   ALU.mult, ALU.mult).then_inc(S["scales_ready"], 1)

        def low(i, p):
            e.wait_ge(S["hi_ready"], i + 1)
            e.tensor_tensor(xt[:, p, 1, :], pst[:, :], xt[:, p, 0, :].bitcast(f32), ALU.subtract).then_inc(S["lo_ready"], 1)

        def body(i, it, p, ahead=True):
            if ahead:
                stats(i + 1, it if p == 0 else it + 1, 1 - p)
            e.wait_ge(S["al_done"], i + 1)
            e.wait_ge(h_out[p], it * 16 + 16)
            c.mark(e.tensor_scalar(ho[:, p, HC:DEN], pss[:, P:P + 2 * HEADS], K["stat"][:, bass.ds(i, 1), 2], None, ALU.mult))
            e.tensor_copy(ho[:, p, DEN:ROW], K["den0"][:, bass.ds(i, 1)].to_broadcast([P, HEADS])).then_inc(S["al_taken"], 1)
            if ahead:
                low(i + 1, 1 - p)
            accumulate(i)
            e.wait_ge(S["k_done"], i + 1)
            e.wait_ge(S["kexp_ready"], i + 1)
            e.tensor_tensor(kz[:, :], psk[:, :], bkv[:, 0:D], ALU.add).then_inc(S["k_taken"], 1)
            e.wait_ge(S["v_done"], i + 3)
            e.wait_ge(S["kvt_done"], i + 1)
            e.tensor_tensor(vf[:, p, :, 0:P], psv[:, :].rearrange("p (k d) -> p k d", k=KD),
                            bkv[:, D:2 * D].rearrange("p (k d) -> p k d", k=KD), ALU.add).then_inc(S["v_taken"], 1)
            e.wait_ge(S["kexp_ready"], i + 2)
            e.scalar_tensor_tensor(kf[:, p, :], ke[:, :], 1.0, km[:, :], ALU.min, ALU.add).then_inc(S["kv_ready"], 1)

        def accumulate(n):
            e.wait_ge(S["kvt_done"], n + 2)
            for b, o in enumerate((pskv0, pskv1)):
                a = K["kv"][:, 2 * b:2 * b + 2, :]
                last = e.tensor_tensor(a, a, o[:, 0:2 * (P + 1)].rearrange("p (k d) -> p k d", k=2), ALU.add)
            last.then_inc(S["kvt_taken"], 1)

        e.sem_inc(S["al_taken"], 1)
        e.sem_inc(S["lo_ready"], 1)
        e.sem_inc(S["k_taken"], 1)
        e.sem_inc(S["v_taken"], 1)
        e.sem_inc(S["kvt_taken"], 1)
        c.mark(e.memset(kf[:, 1, :], 0.0))
        c.mark(e.memset(vf[:, 1, :, :], 0.0))
        c.mark(e.memset(K["kv"][:, :, :], 0.0))
        c.mark(e.memset(vf[:, 0, :, P:P + 1], 1.0))
        c.sync()
        c.link(e.memset(vf[:, 1, :, P:P + 1], 1.0))
        e.engine_nop().then_inc(S["kv_ready"], 1)
        stats(0, 0, 0)
        low(0, 0)
        assert c.n == A_START, c.n
        with e.Fori(0, TRIPS) as t:
            it = e.snap(t)
            c.base, c.n = e.snap(it * A_STEPS + A_START), 0
            for p in range(2):
                body(e.snap(it * 2 + p), it, p)
            assert c.n == A_STEPS, c.n
        c.base, c.n = 0, A_STEPS * TRIPS + A_START
        body(NT - 1, TRIPS, 0, ahead=False)
        accumulate(NT)

    @block.tensor
    def _(e):
        e.sem_inc(S["x_turned"], 1)
        e.sem_inc(S["v_done"], 2)
        e.sem_inc(S["kvt_done"], 1)

        def turn(i):
            e.wait_ge(S["xn_ready"], i + 3)
            e.wait_ge(S["lo_ready"], i + 1)
            for k in range(KD):
                last = e.transpose(pst[:, k * P:(k + 1) * P], xn[:, k * P:(k + 1) * P], K["ident"][:, :])
            last.then_inc(S["x_turned"], 1)

        def product(p, w, outs):
            for k in range(KD):
                for n, (a, b) in enumerate(((0, 0), (0, 1), (1, 0))):
                    for o, c0, c1 in outs:
                        last = e.matmul(o, xt[:, p, a, k * P:(k + 1) * P], w[:, b, k, c0:c1],
                                        start=(k == 0 and n == 0), stop=(k == KD - 1 and n == 2))
            return last

        def kv(n, p, rows=P):
            e.wait_ge(S["kv_ready"], n + 1)
            e.wait_ge(S["kvt_taken"], n + 1)
            for b in range(KD):
                o = (pskv0, pskv1)[b // 2][:, (b % 2) * (P + 1):(b % 2 + 1) * (P + 1)]
                last = e.matmul(o, kf[0:rows, p, b * P:(b + 1) * P], vf[0:rows, p, b, :], start=True, stop=True)
            last.then_inc(S["kvt_done"], 1)

        def logits(p):
            for k in range(KD):
                for n, (a, b) in enumerate(((0, 0), (0, 1), (1, 0))):
                    last = e.matmul(pss[0:2 * HEADS, 0:P], w1[:, b, k, HC:WEXT], xt[:, p, a, k * P:(k + 1) * P],
                                    start=(k == 0 and n == 0), stop=(k == KD - 1 and n == 2))
            last.then_inc(S["alt_done"], 1)

        def body(i, p, ahead=True):
            e.wait_ge(S["lo_ready"], i + 2)
            e.wait_ge(S["h_taken"], i + 1)
            e.wait_ge(S["al_taken"], i + 1)
            product(p, w1, ((psh0[:, :], 0, D), (psh1[:, :], D, HC))).then_inc(S["h_done"], 1)
            logits(p)
            if ahead:
                turn(i + 1)
            kv(i, 1 - p)
            wait_apart(e, S["lt_ready"], i + 1, S["pe_apart"])
            e.transpose(pss[:, P:P + 2 * HEADS], lt[:, :], K["ident"][0:2 * HEADS, 0:2 * HEADS]).then_inc(S["al_done"], 1)
            e.wait_ge(S["k_taken"], i + 1)
            product(p, wkv, ((psk[:, :], 0, D),)).then_inc(S["k_done"], 1)
            e.wait_ge(S["v_taken"], i + 1)
            product(p, wkv, ((psv[:, :], D, 2 * D),)).then_inc(S["v_done"], 1)

        turn(0)
        with e.Fori(0, TRIPS) as t:
            it = e.snap(t)
            for p in range(2):
                body(e.snap(it * 2 + p), p)
        body(NT - 1, 0, ahead=False)
        kv(NT, 0, LAST)


A_STEPS = 16
A_START = 12


def gat(nc, K, layer, bias, W, att_s, att_d, table, result, dram):
    WO = WEXT if layer == 1 else D
    with ExitStack() as st:
        w = st.enter_context(nc.sbuf_tensor(f"w_next{layer}", [P, 2, KH, WO], f32r))
        bcol = st.enter_context(nc.sbuf_tensor(f"bias_c{layer}", [P, KH], f32))
        with ExitStack() as prep:
            gat_weights(nc, K, prep, layer, w, bcol, bias, W, att_s, att_d, dram)
        gat_items(nc, K, st, layer, w, bcol, table, result)


def gat_weights(nc, K, st, layer, w, bcol, bias, W, att_s, att_d, dram):
    def sb(name, shape, dt=f32):
        return st.enter_context(nc.sbuf_tensor(f"{name}{layer}", shape, dt))

    sem = semaphores(nc, st, str(layer))

    WO = WEXT if layer == 1 else D
    WS = min(WO, HC)
    ws = sb("w_stage", [P, KH, WO])
    arep = sb("att_rep", [P, 2, HC])
    tmp = sb("att_prod", [P, 2, 2, HC])
    raw = sb("slots_raw", [IG, 4, SLOTS], i32)
    si, di = sb("slots_src_i", [IG, 4, SLOTS], i32), sb("slots_dst_i", [IG, 4, SLOTS], i32)
    sf = sb("slots_f", [IG, 2, 4, SLOTS])
    ps = [st.enter_context(nc.psum_tensor(f"ps_slots{layer}{i}", [SLOTS, NITEMS], f32)) for i in range(2)]
    s_in, a_in, b_in, parts, turned, w_hi, pool_prod, folded, pool_lo, dv = (sem(n) for n in (
        "slots_loaded", "att_loaded", "bias_loaded", "slots_parts", "slots_turned", "gw_hi", "gw_products", "gw_folded",
        "gw_lo_pool", "gw_dve"))
    w_in = [sem(f"gw_loaded{k}_") for k in range(KH)]
    block = st.enter_context(nc.Block())

    @block.sync
    def _(e):
        if layer == 1:
            e.dma_start(raw[:, :, :], dram["slots"].ap().rearrange("(g i s) o -> i g (s o)", i=IG, s=SLOTS)).then_inc(s_in, 16)
            for j, a in enumerate((att_s, att_d)):
                e.dma_start(arep[:, j, :], a.rearrange("(o h) c -> o (h c)", o=1).to_broadcast([P, HC])).then_inc(a_in, 16)
        for k in range(KH):
            e.dma_start(ws[:, k, 0:WS], W[k * P:(k + 1) * P, :]).then_inc(w_in[k], 16)
        e.dma_start(bcol[:, :], bias.rearrange("(k p) -> p k", p=P), allow_slow_non_contiguous=True).then_inc(b_in, 16)
        e.wait_ge(b_in, 16)

    @block.scalar
    def _(e):
        for k in range(KH):
            e.wait_ge(w_in[k], 16)
            e.activation(w[:, 0, k, 0:WS], ws[:, k, 0:WS], ACT.Copy).then_inc(w_hi, 1)

    def low(e, k):
        return e.tensor_tensor(w[:, 1, k, 0:WS], ws[:, k, 0:WS], w[:, 0, k, 0:WS].bitcast(f32), ALU.subtract)

    @block.gpsimd
    def _(e):
        if layer == 1:
            e.wait_ge(a_in, 32)
        for k in range(KH):
            if layer == 1:
                e.wait_ge(w_in[k], 16)
                if k >= 2:
                    e.wait_ge(folded, k - 1)
                e.tensor_tensor(tmp[:, 0, k % 2, :], ws[:, k, 0:HC], arep[:, 0, :], ALU.mult).then_inc(pool_prod, 1)
            if k % 2 == 0:
                e.wait_ge(w_hi, k + 1)
                low(e, k).then_inc(pool_lo, 1)
        e.wait_ge(pool_lo, KH // 2)

    @block.vector
    def _(e):
        c = Chain(e, dv)
        if layer == 1:
            e.wait_ge(s_in, 16)
            c.mark(e.tensor_scalar(si[:, :, :], raw[:, :, :], 8, None, ALU.arith_shift_right))
            c.mark(e.tensor_scalar(di[:, :, :], raw[:, :, :], 255, None, ALU.bitwise_and))
            c.sync()
            c.mark(e.tensor_copy(sf[:, 0, :, :], si[:, :, :]))
            e.tensor_copy(sf[:, 1, :, :], di[:, :, :]).then_inc(parts, 1)
            e.wait_ge(turned, 1)
            c.mark(e.tensor_copy(K["slot_src"][:, :], ps[0][:, :]))
            c.mark(e.tensor_copy(K["slot_dst"][:, :], ps[1][:, :]))
            e.wait_ge(a_in, 32)
        for k in range(KH):
            if layer == 1:
                e.wait_ge(w_in[k], 16)
                c.link(e.tensor_tensor(tmp[:, 1, k % 2, :], ws[:, k, 0:HC], arep[:, 1, :], ALU.mult))
                c.mark(e.reduce_sum(ws[:, k, HC + 4:WEXT], tmp[:, 1, k % 2, :].rearrange("p (h c) -> p h c", h=HEADS), axis=AX.X))
                e.wait_ge(pool_prod, k + 1)
                e.reduce_sum(ws[:, k, HC:HC + 4], tmp[:, 0, k % 2, :].rearrange("p (h c) -> p h c", h=HEADS), axis=AX.X)\
                 .then_inc(folded, 1)
            if k % 2:
                e.wait_ge(w_hi, k + 1)
                c.mark(low(e, k))
        if layer == 1:
            e.wait_ge(folded, KH)
            c.sync()
            c.link(e.tensor_copy(w[:, 0, :, HC:WEXT], ws[:, :, HC:WEXT]))
            c.mark(e.tensor_tensor(w[:, 1, :, HC:WEXT], ws[:, :, HC:WEXT], w[:, 0, :, HC:WEXT].bitcast(f32), ALU.subtract))
        c.sync()

    @block.tensor
    def _(e):
        if layer == 1:
            e.wait_ge(parts, 1)
            for j in range(2):
                for g in range(4):
                    last = e.matmul(ps[j][:, g * IG:(g + 1) * IG], sf[:, j, g, :], K["ident"][0:IG, 0:IG], start=True, stop=True)
            last.then_inc(turned, 1)


def gat_items(nc, K, st, layer, w, bcol, table, result):
    def sb(name, shape, dt=f32):
        return st.enter_context(nc.sbuf_tensor(f"{name}{layer}", shape, dt))

    sem = semaphores(nc, st, str(layer))

    def ps(name, rows=P):
        return st.enter_context(nc.psum_tensor(f"{name}{layer}", [rows, D], f32))

    first = layer == 1
    OW = ROW if first else D
    SH = HEADS * SLOTS
    state = sb("state", [P, 4, ROW])
    flat = state[:, :, :].rearrange("p a b -> p (a b)")
    gr = sb("edge_rows", [SLOTS, 2, ROW])
    ix = sb("edge_index", [SLOTS, 2], i32)
    dm = sb("edge_node", [SLOTS, P])
    y = sb("edge_logit_diag", [SLOTS, 5, SLOTS])
    pen = sb("mask", [P, SLOTS])
    s = sb("logits", [P, HEADS, SLOTS])
    mx = sb("edge_max", [P, HEADS])
    z2 = sb("new_old_max", [P, 2 * HEADS])
    ee = sb("exponents", [P, SH + HEADS])
    ex = sb("weights", [P, SH + HEADS])
    dn = sb("den_part", [P, 3, HEADS])
    cs = sb("base_scale", [P, HEADS])
    pr = sb("alpha", [P, HEADS, SLOTS])
    pt = sb("alpha_t", [SLOTS, HEADS * P])
    ff = sb("features_t", [P, 2, D])
    ft = sb("features_t_parts", [P, 2, 2, HC], f32r)
    ho = sb("next_rows", [P, 2, OW])
    lt = sb("next_logits_t", [2 * HEADS, P])
    psb, psp, psa0, psa1, pst, psal, psh0, psh1 = (ps("ps_b"), ps("ps_p", SLOTS), ps("ps_a0"), ps("ps_a1"), ps("ps_t"), ps("ps_al"),
                                                  ps("ps_h0"), ps("ps_h1"))
    names = ("d_ready a_done s_taken e_ready x_ready p_ready b_done pt_ready c_done combined turned f_ready first_hi second_hi "
             "first_ready second_ready h0_done h1_done h0_taken h1_taken al_done lt_ready alt_done al_taken "
             "index_ready b_dve ended pool_apart pe_apart").split()
    S = {n: sem(n) for n in names}
    last_done = S["h1_done" if first else "h0_done"]
    gathered, loaded, h_out = ([sem(f"{n}{p}_") for p in range(2)] for n in ("gathered", "loaded", "rows_out"))
    tab, res = table.ap(), result.ap()
    block = st.enter_context(nc.Block())

    def pairs(e):
        return e.value_load(K["nitems"][0:1, 0:1], min_val=1, max_val=NITEMS // 2 - 2)

    def base_of(e, i):
        return e.value_load(K["items"][0:1, bass.ds(i + NITEMS, 1)], min_val=0, max_val=3 * ROW)

    def tile_of(e, i):
        return e.value_load(K["items"][0:1, bass.ds(i, 1)], min_val=0, max_val=NT - 1)

    @block.sync
    def _(e):
        for p in range(2):
            e.sem_inc(h_out[p], 16)

        def load(i, p):
            t = tile_of(e, i)
            e.dma_start(state[:, p, :], tab[bass.ds(t * P, P), :]).then_inc(loaded[p], 16)

        load(0, 0)
        load(1, 1)
        e.wait_ge(S["combined"], 2)
        load(2, 0)
        n = pairs(e)
        with e.Fori(0, n) as tt:
            it = e.snap(tt)
            for p in range(2):
                i = e.snap(it * 2 + p)
                e.wait_ge(S["combined"], i + 3)
                load(i + 3, 1 - p)
                t = tile_of(e, i)
                if first:
                    e.wait_ge(S["h1_taken"], i + 2)
                    e.wait_ge(S["al_taken"], i + 2)
                else:
                    e.wait_ge(S["h0_taken"], i + 3)
                e.sem_inc(S["ended"], 1)
                wait_apart(e, h_out[1 - p], it * 16 + (16, 32)[p], S["ended"])
                e.dma_start(res[bass.ds(t * P, P), :], ho[:, p, :]).then_inc(h_out[p], 16)
        for p in range(2):
            wait_apart(e, h_out[p], n * 16 + 16, S["ended"])
            wait_apart(e, loaded[p], n * 16 + (32, 16)[p], S["ended"])

    @block.gpsimd
    def _(e):
        e.sem_inc(S["second_ready"], 1)

        def index(i, p):
            e.tensor_copy(ix[:, p:p + 1], K["slot_src"][:, bass.ds(i, 1)]).then_inc(S["index_ready"], 1)

        def gather(i, p):
            wait_apart(e, S["index_ready"], i + 1, S["pool_apart"])
            e.indirect_dma_start(out=gr[:, p, :], out_offset=None, in_=tab,
                                 in_offset=bass.IndirectOffsetOnAxis(ap=ix[:, p:p + 1], axis=0),
                                 bounds_check=N - 1, oob_is_err=False).then_inc(gathered[p], 16)

        def second_low(i, p):
            wait_apart(e, S["second_hi"], i + 1, S["pool_apart"])
            e.tensor_tensor(ft[:, p, 1, D:HC], ff[:, 1, :], ft[:, p, 0, D:HC].bitcast(f32), ALU.subtract).then_inc(S["second_ready"], 1)

        e.memset(gr[:, :, :], 0.0)
        index(0, 0)
        index(1, 1)
        gather(0, 0)
        gather(1, 1)
        e.wait_ge(S["c_done"], 1)
        index(2, 0)
        gather(2, 0)
        n = pairs(e)
        with e.Fori(0, n) as tt:
            it = e.snap(tt)
            for p in range(2):
                i = e.snap(it * 2 + p)
                second_low(i, p)
                wait_apart(e, S["c_done"], i + 2, S["pool_apart"])
                index(i + 3, 1 - p)
                gather(i + 3, 1 - p)
        for p in range(2):
            wait_apart(e, gathered[p], n * 16 + (32, 16)[p], S["pool_apart"])

    @block.scalar
    def _(e):
        e.sem_inc(S["pt_ready"], 1)
        e.sem_inc(S["f_ready"], 1)
        e.sem_inc(S["h0_taken"], 1 if first else 2)
        e.sem_inc(S["h1_taken"], 1)

        def exps(i):
            e.wait_ge(S["e_ready"], i + 1)
            e.activation(ex[:, :], ee[:, :], ACT.Exp).then_inc(S["x_ready"], 1)

        def alphas(i):
            e.wait_ge(S["b_done"], i + 2)
            e.activation(pt[:, :], psp[:, :], ACT.Copy).then_inc(S["pt_ready"], 1)

        def features(i, j):
            n = i * 2 + j
            e.wait_ge(S["turned"], n + 1)
            e.wait_ge(S[("first_ready", "second_ready")[j]], i + 1)
            for b in range(4):
                last = e.activation(ff[:, j, b * P:(b + 1) * P], pst[:, b * P:(b + 1) * P], ACT.Relu,
                                    bias=bcol[:, 4 * j + b:4 * j + b + 1])
            last.then_inc(S["f_ready"], 1)

        def high(i, p, j):
            e.wait_ge(S["f_ready"], i * 2 + j + 2)
            e.wait_ge(last_done, i + 1)
            e.activation(ft[:, p, 0, j * D:(j + 1) * D], ff[:, j, :], ACT.Copy).then_inc(S[("first_hi", "second_hi")[j]], 1)

        exps(0)
        alphas(0)
        exps(1)
        features(0, 0)
        high(0, 0, 0)
        features(0, 1)
        n = pairs(e)
        with e.Fori(0, n) as tt:
            it = e.snap(tt)
            for p in range(2):
                i = e.snap(it * 2 + p)
                alphas(i + 1)
                high(i, p, 1)
                exps(i + 2)
                if first:
                    e.wait_ge(S["h0_done"], i + 1)
                    e.wait_ge(h_out[p], it * 16 + 16)
                    e.activation(ho[:, p, 0:D], psh0[:, :], ACT.Copy).then_inc(S["h0_taken"], 1)
                    e.wait_ge(S["alt_done"], i + 1)
                    e.activation(lt[:, :], psal[0:2 * HEADS, 0:P], ACT.Copy).then_inc(S["lt_ready"], 1)
                features(i + 1, 0)
                high(i + 1, 1 - p, 0)
                features(i + 1, 1)
                if first:
                    e.wait_ge(S["h1_done"], i + 3)
                    e.activation(ho[:, p, D:HC], psh1[:, :], ACT.Copy).then_inc(S["h1_taken"], 1)
                else:
                    e.wait_ge(S["h0_done"], i + 3)
                    e.wait_ge(h_out[p], it * 16 + 16)
                    e.activation(ho[:, p, :], (psh0, psh1)[p][:, :], ACT.Copy).then_inc(S["h0_taken"], 1)

    @block.vector
    def _(e):
        c = Chain(e, S["b_dve"])
        e.sem_inc(S["s_taken"], 1)
        e.sem_inc(S["combined"], 1)
        e.sem_inc(S["first_ready"], 1)
        e.sem_inc(S["al_taken"], 1)
        e.tensor_copy(y[:, 4, :], K["ident"][0:SLOTS, 0:SLOTS])

        def prepare(i, it, p):
            e.wait_ge(gathered[p], it * 16 + 16)
            e.wait_ge(S["a_done"], i + 1)
            e.tensor_scalar(dm[:, :], K["iota"][0:SLOTS, :], K["slot_dst"][:, bass.ds(i, 1)], None, ALU.is_equal)
            e.tensor_tensor(y[:, 0:HEADS, :], K["ident"][0:SLOTS, 0:SLOTS].unsqueeze(1).to_broadcast([SLOTS, HEADS, SLOTS]),
                            gr[:, p, ALS:ALD].unsqueeze(2).to_broadcast([SLOTS, HEADS, SLOTS]), ALU.mult)\
             .then_inc(S["d_ready"], 1)

        def first_low(i, p):
            e.wait_ge(S["first_hi"], i + 1)
            e.tensor_tensor(ft[:, p, 1, 0:D], ff[:, 0, :], ft[:, p, 0, 0:D].bitcast(f32), ALU.subtract).then_inc(S["first_ready"], 1)

        def softmax_exponents(i, it, p, o):
            new = state[:, 2 + p, :]
            e.wait_ge(S["a_done"], i + 2)
            c.link(e.tensor_scalar(pen[:, :], psb[:, SH:SH + SLOTS], -1.0, -NEG, ALU.add, ALU.mult))
            e.tensor_tensor(s[:, :, :], psb[:, 0:SH].rearrange("p (h s) -> p h s", h=HEADS),
                            pen[:, :].unsqueeze(1).to_broadcast([P, HEADS, SLOTS]), ALU.add).then_inc(S["s_taken"], 1)
            e.wait_ge(S["s_taken"], i + 2)
            c.link(e.tensor_reduce(mx[:, :], s[:, :, :], axis=AX.X, op=ALU.max))
            e.wait_ge(loaded[p], it * 16 + 16)
            bm, ba = (flat[:, bass.ds(o + k, HEADS)] for k in (ALS, ALD))
            c.mark(e.tensor_copy(new[:, ALD:DEN], ba))
            c.link(e.tensor_tensor(new[:, ALS:ALD], mx[:, :], bm, ALU.max))
            c.mark(e.tensor_tensor(z2[:, HEADS:2 * HEADS], bm, new[:, ALD:DEN], ALU.add))
            c.mark(e.tensor_tensor(z2[:, 0:HEADS], new[:, ALS:ALD], new[:, ALD:DEN], ALU.add))
            c.link(e.tensor_tensor(s[:, :, :], s[:, :, :], new[:, ALD:DEN].unsqueeze(2).to_broadcast([P, HEADS, SLOTS]), ALU.add))
            c.mark(e.scalar_tensor_tensor(z2[:, :], z2[:, :], 0.2, z2[:, :], ALU.mult, ALU.max))
            c.link(e.scalar_tensor_tensor(s[:, :, :], s[:, :, :], 0.2, s[:, :, :], ALU.mult, ALU.max))
            e.tensor_tensor(ee[:, SH:SH + HEADS], z2[:, HEADS:2 * HEADS], z2[:, 0:HEADS], ALU.subtract)
            e.tensor_tensor(ee[:, 0:SH].rearrange("p (h s) -> p h s", h=HEADS), s[:, :, :],
                            z2[:, 0:HEADS].unsqueeze(2).to_broadcast([P, HEADS, SLOTS]), ALU.subtract).then_inc(S["e_ready"], 1)

        def softmax_weights(i, p, o):
            new = state[:, 2 + p, :]
            bd = flat[:, bass.ds(o + DEN, HEADS)]
            e.wait_ge(S["x_ready"], i + 1)
            xe = ex[:, 0:SH].rearrange("p (h s) -> p h s", h=HEADS)
            c.mark(e.tensor_tensor(dn[:, 1, :], ex[:, SH:SH + HEADS], bd, ALU.mult))
            c.link(e.reduce_sum(dn[:, 0, :], xe, axis=AX.X))
            c.link(e.tensor_tensor(new[:, DEN:ROW], dn[:, 0, :], dn[:, 1, :], ALU.add))
            c.link(e.reciprocal(dn[:, 2, :], new[:, DEN:ROW]))
            e.wait_ge(S["combined"], i + 1)
            e.wait_ge(S["b_done"], i + 1)
            c.mark(e.tensor_tensor(cs[:, :], dn[:, 1, :], dn[:, 2, :], ALU.mult))
            e.tensor_tensor(pr[:, :, :], xe, dn[:, 2, :].unsqueeze(2).to_broadcast([P, HEADS, SLOTS]), ALU.mult)\
             .then_inc(S["p_ready"], 1)

        def combine(i, p, o):
            e.wait_ge(S["c_done"], i + 1)
            e.wait_ge(S["p_ready"], i + 1)
            e.wait_ge(S["combined"], i + 1)
            for h in range(HEADS):
                a = (psa0, psa1)[h // 2][:, (h % 2) * C:(h % 2 + 1) * C]
                last = e.scalar_tensor_tensor(state[:, 2 + p, h * C:(h + 1) * C], flat[:, bass.ds(o + h * C, C)],
                                              cs[:, h:h + 1], a, ALU.mult, ALU.add)
            last.then_inc(S["combined"], 1)

        prepare(0, 0, 0)
        base = [base_of(e, i) for i in range(2)]
        softmax_exponents(0, 0, 0, base[0])
        softmax_weights(0, 0, base[0])
        prepare(1, 0, 1)
        softmax_exponents(1, 0, 1, base[1])
        combine(0, 0, base[0])
        softmax_weights(1, 1, base[1])
        start = c.n
        n = pairs(e)
        with e.Fori(0, n) as tt:
            it = e.snap(tt)
            c.base, c.n = e.snap(it * start + start), 0
            for p in range(2):
                i = e.snap(it * 2 + p)
                prepare(i + 2, it + 1, p)
                base = [base[1] if p else base_of(e, i + 1), base_of(e, i + 2)]
                first_low(i, p)
                softmax_exponents(i + 2, it + 1, p, base[1])
                combine(i + 1, 1 - p, base[0])
                softmax_weights(i + 2, p, base[1])
                if first:
                    t = tile_of(e, i)
                    e.wait_ge(S["al_done"], i + 1)
                    e.wait_ge(h_out[p], it * 16 + 16)
                    e.tensor_copy(ho[:, p, DEN:ROW], K["den0"][:, bass.ds(t, 1)].to_broadcast([P, HEADS]))
                    e.tensor_copy(ho[:, p, HC:DEN], psal[:, P:P + 2 * HEADS]).then_inc(S["al_taken"], 1)
            assert c.n == start, (c.n, start)

    @block.tensor
    def _(e):
        e.sem_inc(S["a_done"], 1)
        e.sem_inc(S["b_done"], 1)
        e.sem_inc(last_done, 2)

        def spread(i):
            e.wait_ge(S["d_ready"], i + 1)
            e.wait_ge(S["s_taken"], i + 1)
            e.matmul(psb[:, 0:SH + SLOTS], dm[:, :], y[:, :, :].rearrange("p a b -> p (a b)"), start=True, stop=True)\
             .then_inc(S["a_done"], 1)

        def turn_alpha(i):
            e.wait_ge(S["p_ready"], i + 1)
            wait_apart(e, S["pt_ready"], i + 1, S["pe_apart"])
            for h in range(HEADS):
                last = e.transpose(psp[:, h * P:(h + 1) * P], pr[:, h, :], K["ident"][:, :])
            last.then_inc(S["b_done"], 1)

        def aggregate(i, p):
            e.wait_ge(S["pt_ready"], i + 2)
            e.wait_ge(S["combined"], i + 1)
            for h in range(HEADS):
                a = (psa0, psa1)[h // 2][:, (h % 2) * C:(h % 2 + 1) * C]
                last = e.matmul(a, pt[:, h * P:(h + 1) * P], gr[:, p, h * C:(h + 1) * C], start=True, stop=True)
            last.then_inc(S["c_done"], 1)

        def turn(i, p, j):
            e.wait_ge(S["combined"], i + 2)
            e.wait_ge(S["f_ready"], i * 2 + j + 1)
            for b in range(4):
                k = 4 * j + b
                last = e.transpose(pst[:, b * P:(b + 1) * P], state[:, 2 + p, k * P:(k + 1) * P], K["ident"][:, :])
            last.then_inc(S["turned"], 1)

        def product(out, p, ks, c0, c1):
            for k in ks:
                for n, (a, b) in enumerate(((0, 0), (0, 1), (1, 0))):
                    last = e.matmul(out, ft[:, p, a, k * P:(k + 1) * P], w[:, b, k, c0:c1],
                                    start=(k == 0 and n == 0), stop=(k == KH - 1 and n == 2))
            return last

        def next_logits(i, p):
            e.wait_ge(S["al_taken"], i + 1)
            for k in range(KH):
                for n, (a, b) in enumerate(((0, 0), (0, 1), (1, 0))):
                    last = e.matmul(psal[0:2 * HEADS, 0:P], w[:, b, k, HC:WEXT], ft[:, p, a, k * P:(k + 1) * P],
                                    start=(k == 0 and n == 0), stop=(k == KH - 1 and n == 2))
            last.then_inc(S["alt_done"], 1)

        def turn_logits(i):
            wait_apart(e, S["lt_ready"], i + 1, S["pe_apart"])
            e.transpose(psal[:, P:P + 2 * HEADS], lt[:, :], K["ident"][0:2 * HEADS, 0:2 * HEADS]).then_inc(S["al_done"], 1)

        spread(0)
        turn_alpha(0)
        spread(1)
        aggregate(0, 0)
        turn(0, 0, 0)
        turn(0, 0, 1)
        n = pairs(e)
        with e.Fori(0, n) as tt:
            it = e.snap(tt)
            for p in range(2):
                i = e.snap(it * 2 + p)
                h0 = psh0 if first or p == 0 else psh1
                turn_alpha(i + 1)
                spread(i + 2)
                e.wait_ge(S["first_ready"], i + 2)
                e.wait_ge(S["h0_taken"], i + 1)
                product(h0[:, :], p, (0, 1), 0, D)
                aggregate(i + 1, 1 - p)
                product(h0[:, :], p, (2, 3), 0, D)
                e.wait_ge(S["second_ready"], i + 2)
                if first:
                    product(h0[:, :], p, (4, 5, 6, 7), 0, D).then_inc(S["h0_done"], 1)
                    next_logits(i, p)
                    turn(i + 1, 1 - p, 0)
                    e.wait_ge(S["h1_taken"], i + 1)
                    product(psh1[:, :], p, (0, 1, 2, 3), D, HC)
                    turn_logits(i)
                    turn(i + 1, 1 - p, 1)
                    product(psh1[:, :], p, (4, 5, 6, 7), D, HC).then_inc(S["h1_done"], 1)
                else:
                    product(h0[:, :], p, (4,), 0, D)
                    turn(i + 1, 1 - p, 0)
                    product(h0[:, :], p, (5, 6), 0, D)
                    turn(i + 1, 1 - p, 1)
                    product(h0[:, :], p, (7,), 0, D).then_inc(S["h0_done"], 1)


def tail(nc, K, wq, x, bfc, out_w, out_b, Wr, br, fW1, fb1, fW2, fb2, out, dram):
    with ExitStack() as st:
        def sb(name, shape, dt=f32):
            return st.enter_context(nc.sbuf_tensor(name, shape, dt))

        T = dict(mw=sb("mix_out_w", [P, 2, KD, D], f32r), w1=sb("expert_w1", [P, 2, KD, 2 * P], f32r),
                 w2=sb("expert_w2", [P, 2, 2, D], f32r), wr=sb("router_w", [P, 2, KD, NE], f32r),
                 b2=sb("expert_b2", [NE, 2, D], f32r), ks=sb("ksum_by_head", [P, KD, NE]), bias=sb("bias_rep", [P, D]),
                 br=sb("router_b_rep", [P, GT, NE]), b1=sb("expert_b1_c", [P, 2]), sel=sb("expert_rows", [NE, 2 * P], f32r),
                 head=sb("head_rows", [NE, D], f32r),
                 tri=sb("earlier_b", [P, P], bf16), one=sb("ones_bf", [P, P], bf16), i8=sb("iota_8", [P, NE]))
        with ExitStack() as prep:
            tail_weights(nc, K, prep, T, bfc, out_w, out_b, Wr, br, fW1, fb1, fW2, fb2)
        tail_groups(nc, K, st, T, wq, x, out, dram)


def tail_weights(nc, K, st, T, bfc, out_w, out_b, Wr, br, fW1, fb1, fW2, fb2):
    def sb(name, shape, dt=f32):
        return st.enter_context(nc.sbuf_tensor(name, shape, dt))

    sem = semaphores(nc, st)

    ow = sb("out_w_rows", [P, KD, D])
    owt = sb("out_w_t", [P, KD, D])
    w1s, w2s, wrs, b2s = sb("ew1_stage", [P, KD, 2 * P]), sb("ew2_stage", [P, 2, D]), sb("wr_stage", [P, KD, NE]), sb("eb2_stage", [NE, D])
    ob = sb("out_b_rep", [P, D])
    brs = sb("br_stage", [P, NE])
    bm = sb("head_mask", [P, P])
    sels = sb("rows_stage", [NE, 2 * P + D])
    kvm = sb("kv_masked", [P, KD, P])
    kvt = sb("kv_turned", [P, KD, P])
    pst = [st.enter_context(nc.psum_tensor(f"ps_owt{i}", [P, D], f32)) for i in range(2)]
    psm = [st.enter_context(nc.psum_tensor(f"ps_mw{i}", [P, D], f32)) for i in range(2)]
    ow_in, rest_in, act_in, mask, turned, taken, kv_masked, products, p_taken, dv, pool = (sem(n) for n in (
        "ow_loaded", "tail_loaded", "tail_small_loaded", "mask_ready", "ow_turned", "ow_taken", "kv_masked_ready", "mix_products",
        "mix_taken", "tail_dve", "tail_pool"))
    block = st.enter_context(nc.Block())

    @block.sync
    def _(e):
        e.dma_start(ow[:, :, :], out_w.rearrange("(b p) c -> p b c", p=P)).then_inc(ow_in, 16)
        for k in range(KD):
            e.dma_start(w1s[:, k, :].rearrange("p (e f) -> p e f", e=NE),
                        fW1[:, k * P:(k + 1) * P, :].rearrange("e p f -> p e f")).then_inc(rest_in, 16)
        e.dma_start(w2s[:, :, :], fW2.rearrange("e f d -> (e f) d").rearrange("(k p) d -> p k d", p=P)).then_inc(rest_in, 16)
        e.dma_start(wrs[:, :, :], Wr.rearrange("(k p) e -> p k e", p=P)).then_inc(rest_in, 16)
        e.dma_start(b2s[:, :], fb2).then_inc(rest_in, 16)
        e.wait_ge(rest_in, 112)

    @block.scalar
    def _(e):
        e.dma_start(T["bias"][:, :], bfc.rearrange("(o c) -> o c", o=1).to_broadcast([P, D])).then_inc(act_in, 16)
        e.dma_start(ob[:, :], out_b.rearrange("(o c) -> o c", o=1).to_broadcast([P, D])).then_inc(act_in, 16)
        e.dma_start(brs[:, :], br.rearrange("(o c) -> o c", o=1).to_broadcast([P, NE])).then_inc(act_in, 16)
        e.dma_start(T["b1"][:, :], fb1.rearrange("e f -> (e f)").rearrange("(k p) -> p k", p=P), allow_slow_non_contiguous=True)\
         .then_inc(act_in, 16)
        for k in range(KD):
            e.wait_ge(turned, k + 1)
            e.activation(owt[:, k, :], pst[k % 2][:, :], ACT.Copy).then_inc(taken, 1)
        e.wait_ge(turned, KD + 1)
        e.activation(kvt[:, :, :], pst[0][:, :].rearrange("p (k d) -> p k d", k=KD), ACT.Copy).then_inc(taken, 1)
        e.wait_ge(act_in, 64)

    @block.gpsimd
    def _(e):
        c = Chain(e, pool)
        c.mark(e.memset(bm[:, :], 0.0))
        c.mark(e.memset(sels[:, :], 1.0))
        c.mark(e.memset(T["one"][:, :], 1.0))
        c.mark(e.iota(T["i8"][:, :], pattern=[[1, NE]], base=0, channel_multiplier=0, allow_small_or_imprecise_dtypes=True))
        c.sync()
        c.link(e.tensor_copy(T["tri"][:, :], K["incl"][:, :]))
        c.link(e.memset(bm[0:64, 0:64], 1.0))
        c.link(e.memset(bm[64:P, 64:P], 1.0))
        for lo, hi, width in ((0, 2 * P, 32), (2 * P, 2 * P + D, 64)):
            c.link(e.affine_select(out=sels[:, lo:hi], in_=sels[:, lo:hi], compare_op=ALU.is_ge, fill=0.0, base=0,
                                   pattern=[[1, hi - lo]], channel_multiplier=-width))
            c.link(e.affine_select(out=sels[:, lo:hi], in_=sels[:, lo:hi], compare_op=ALU.is_ge, fill=0.0, base=width - 1,
                                   pattern=[[-1, hi - lo]], channel_multiplier=width))
        e.engine_nop().then_inc(mask, 1)

    @block.tensor
    def _(e):
        e.wait_ge(ow_in, 16)
        for k in range(KD):
            if k >= 2:
                e.wait_ge(taken, k - 1)
            for j in range(4):
                last = e.transpose(pst[k % 2][:, j * P:(j + 1) * P], ow[:, j, k * P:(k + 1) * P], K["ident"][:, :])
            last.then_inc(turned, 1)
        e.wait_ge(kv_masked, 1)
        e.wait_ge(taken, KD)
        for k in range(KD):
            last = e.transpose(pst[0][:, k * P:(k + 1) * P], kvm[:, k, :], K["ident"][:, :])
        last.then_inc(turned, 1)
        e.wait_ge(taken, KD + 1)
        for k in range(KD):
            if k >= 2:
                e.wait_ge(p_taken, k - 1)
            e.matmul(psm[k % 2][:, :], kvt[:, k, :], owt[:, k, :], start=True, stop=True).then_inc(products, 1)

    @block.vector
    def _(e):
        c = Chain(e, dv)
        e.wait_ge(mask, 1)
        c.link(e.memset(T["ks"][:, :, :], 0.0))
        for k in range(KD):
            c.mark(e.tensor_scalar(T["ks"][:, k, 2 * k:2 * k + 2], bm[:, 0:P:64], K["kv"][:, k, P:P + 1], None, ALU.mult))
        c.mark(e.tensor_copy(T["sel"][:, :], sels[:, 0:2 * P]))
        c.mark(e.tensor_copy(T["head"][:, :], sels[:, 2 * P:2 * P + D]))
        e.tensor_tensor(kvm[:, :, :], K["kv"][:, :, 0:P], bm[:, :].unsqueeze(1).to_broadcast([P, KD, P]), ALU.mult)\
         .then_inc(kv_masked, 1)
        e.wait_ge(rest_in, 112)
        e.wait_ge(act_in, 64)
        pairs = ((T["w1"], w1s), (T["w2"], w2s), (T["wr"], wrs))
        for w, s in pairs:
            c.mark(e.tensor_copy(w[:, 0, :, :], s[:, :, :]))
        c.mark(e.tensor_copy(T["b2"][:, 0, :], b2s[:, :]))
        c.sync()
        for w, s in pairs:
            c.mark(e.tensor_tensor(w[:, 1, :, :], s[:, :, :], w[:, 0, :, :].bitcast(f32), ALU.subtract))
        c.mark(e.tensor_tensor(T["b2"][:, 1, :], b2s[:, :], T["b2"][:, 0, :].bitcast(f32), ALU.subtract))
        c.mark(e.tensor_tensor(T["bias"][:, :], T["bias"][:, :], ob[:, :], ALU.add))
        c.mark(e.tensor_copy(T["br"][:, :, :], brs[:, :].unsqueeze(1).to_broadcast([P, GT, NE])))
        for k in range(KD):
            e.wait_ge(products, k + 1)
            c.link(e.tensor_copy(T["mw"][:, 0, k, :], psm[k % 2][:, :]))
            e.tensor_tensor(T["mw"][:, 1, k, :], psm[k % 2][:, :], T["mw"][:, 0, k, :].bitcast(f32), ALU.subtract).then_inc(p_taken, 1)
        e.wait_ge(p_taken, KD)


def tail_groups(nc, K, st, T, wq, x, out, dram):
    def sb(name, shape, dt=f32):
        return st.enter_context(nc.sbuf_tensor(name, shape, dt))

    sem = semaphores(nc, st)

    GN = GT * P
    xb, yb, xn, t1, z, xn3, ob = (sb(n, [P, GT, D]) for n in (
        "g_x", "g_y", "g_xn", "g_sum", "g_z", "g_zn", "g_out"))
    xt, qp, zt = (sb(n, [P, 2, KD, GN], f32r) for n in ("g_xn_t", "g_q_parts", "g_zn_t"))
    qf = sb("g_q", [P, KD, GN])
    qz, qe = sb("g_q_relu", [P, 2, GN]), sb("g_q_exp", [P, GN])
    rn = K["kv"][:, :, :].rearrange("p k d -> p (k d)")[:, 0:D]
    rs = sb("g_norm_parts", [NE, 2, GN], f32r)
    hg = sb("g_hidden", [P, 2, GN])
    hs = sb("g_hidden_parts", [P, 2, 2, GN], f32r)
    bn = sb("g_bn", [P, 6])
    mv = sb("g_mean_var", [P, GT, 2])
    va, sd, r3, n3 = sb("g_var", [P, GT]), sb("g_sd", [P, GT]), sb("g_rs", [P, GT]), sb("g_shift", [P, GT])
    lg, pe, pr, s0, s1, tw, po, ga = (sb(n, [P, GT, NE]) for n in (
        "r_logits", "r_exp", "r_probs", "r_first", "r_second", "r_top", "r_pos", "r_gate"))
    m8 = sb("r_max8", [P, GT, NE])
    i8u = sb("r_index8", [P, GT, NE], mybir.dt.uint32)
    i8f = sb("r_index8_f", [P, GT, NE])
    sl = sb("r_chosen", [P, GT, NE], bf16)
    t4 = sb("r_small", [P, 4, GT])
    run = sb("r_running", [P, NE])
    lt = hg[0:NE, 1, :]
    gs = sb("g_gate_t_parts", [NE, 2, GN], f32r)
    rot = [st.enter_context(nc.psum_tensor(f"ps_rot{i}", [P, D], f32)) for i in range(4)]
    pst = [st.enter_context(nc.psum_tensor(f"ps_turn{i}", [P, D], f32)) for i in range(2)]
    pss = st.enter_context(nc.psum_tensor("ps_small", [P, D], f32))
    psc = st.enter_context(nc.psum_tensor("ps_counts", [P, D], f32))
    names = ("xn_ready dve_apart chain_b xt_hi xt_lo t_turned sum_a sum_b sum_ready q_done q_taken qrelu_ready q_ready m_done m_taken rs_ready "
             "n_done qn_ready qp_hi qp_lo o_done z_ready var_ready sd_ready zs_ready zn_ready zn_ready_pool z_turned zt_hi zt_lo "
             "rt_done lt_ready r_done lg_ready re_ready sel_ready c_done c_taken gate_ready gt_done gs_hi gs_lo h_done h_taken g_done "
             "hg_ready hs_hi hs_lo w_done out_ready tail_chain pe_apart_t pool_apart_t r_taken").split()
    S = {n: sem("t_" + n) for n in names}
    x_in, x_in2, y_in, stored = sem("t_x_in"), sem("t_x_in2"), sem("t_y_in"), sem("t_stored")
    MIXED = [(s, j) for h in (0, 2) for s in "ow" for j in (h, h + 1)]
    USES = ([("q", j) for j in range(4)] + [("h", j) for j in range(2)] + [("n", j) for j in range(4)]
            + [("g", j) for j in range(2)] + MIXED)
    PER = dict(q=4, h=2, n=4, g=2, w=4, o=4)
    TAKEN = dict(q="q_taken", h="h_taken", n="qn_ready", g="hg_ready", w="out_ready", o="z_ready")
    assert len(USES) % 4 == 0

    def bank(kind, j):
        return rot[USES.index((kind, j)) % 4]

    FIRST_HALF = "qno"
    ORDER = (((0, 1), (0, 1)), ((2, 3), (2, 3)))

    def wait_bank(e, r, kind, j, a=True, b=True):
        u = USES.index((kind, j)) - 4
        while u >= 0 and not (a if USES[u][0] in FIRST_HALF else b):
            u -= 4
        before = u < 0
        k, m = USES[u % 4 + len(USES) - 4 if before else u]
        e.wait_ge(S[TAKEN[k]], (r if before else r + 1) * PER[k] + m + 1)

    FULL = NG - 1
    REST = NT - FULL * GT
    block = st.enter_context(nc.Block())

    def first(n):
        return isinstance(n, int) and n == 0

    def rounds(e, body):
        body(0, True, False, True)
        with e.Fori(1, NG - 1) as t:
            body(e.snap(t), True, True, True)
        body(NG - 1, True, True, False)
        body(NG, False, True, False)

    @block.sync
    def _(e):
        HALF = REST - 1

        def tiles(a, g, j0, j1):
            return a[bass.ds(g * GN + j0 * P, (j1 - j0) * P), :].rearrange("(j p) d -> p j d", p=P)

        y = dram["yt"].ap()
        def load(g):
            e.wait_ge(S["sum_ready"], g * GT + GT)
            e.dma_start(xb[:, 0:HALF, :], tiles(x, g, 0, HALF)).then_inc(x_in, 16)
            if isinstance(g, int) and g == FULL:
                e.dma_start(xb[0:LAST, HALF, :], x[(NT - 1) * P:N, :]).then_inc(x_in2, 16)
                e.dma_start(yb[:, 0:REST, :], tiles(y, g, 0, REST)).then_inc(y_in, 16)
            else:
                e.dma_start(xb[:, HALF:GT, :], tiles(x, g, HALF, GT)).then_inc(x_in2, 16)
                e.dma_start(yb[:, :, :], tiles(y, g, 0, GT)).then_inc(y_in, 16)

        load(0)
        with e.Fori(1, FULL) as t:
            load(e.snap(t))
        load(FULL)
        for s in (x_in, x_in2, y_in):
            e.wait_ge(s, 16 * NG)

    @block.gpsimd
    def _(e):
        apart = S["pool_apart_t"]
        e.sem_inc(S["sum_ready"], GT)
        e.sem_inc(S["qp_lo"], KD)
        e.sem_inc(S["hs_lo"], 2)

        def body(r, a, b, ahead):
            if b:
                for j in (2, 3):
                    wait_apart(e, S["zs_ready"], r, apart)
                    e.tensor_scalar(xn3[:, j, :], z[:, j, :], r3[:, j:j + 1], n3[:, j:j + 1], ALU.mult, ALU.add)\
                     .then_inc(S["zn_ready_pool"], 1)
            if a:
                for j in range(GT):
                    wait_apart(e, S["sum_a"], r * GT + j + 1, apart)
                    e.tensor_tensor(t1[:, j, :], t1[:, j, :], yb[:, j, :], ALU.add).then_inc(S["sum_b"], 1)
                    e.wait_ge(S["sum_b"], r * GT + j + 1)
                    e.tensor_tensor(t1[:, j, :], t1[:, j, :], T["bias"][:, :], ALU.add).then_inc(S["sum_ready"], 1)
                for j in range(KD):
                    n = r * KD + j
                    e.wait_ge(S["qp_hi"], n + 1)
                    e.tensor_tensor(qp[:, 1, j, :], qf[:, j, :], qp[:, 0, j, :].bitcast(f32), ALU.subtract).then_inc(S["qp_lo"], 1)
            if b:
                for j in range(2):
                    e.wait_ge(S["hs_hi"], (r - 1) * 2 + j + 1)
                    e.tensor_tensor(hs[:, 1, j, :], hg[:, j, :], hs[:, 0, j, :].bitcast(f32), ALU.subtract).then_inc(S["hs_lo"], 1)
                g = r - 1
                wait_apart(e, S["out_ready"], g * GT + 3 * GT, apart)
                if not (isinstance(g, int) and g == NG - 1):
                    e.dma_start(out[bass.ds(g * GN, GN), :].rearrange("(j p) d -> p j d", p=P), ob[:, :, :]).then_inc(stored, 16)
                else:
                    lo = FULL * GN
                    e.dma_start(out[lo:lo + (REST - 1) * P, :].rearrange("(j p) d -> p j d", p=P), ob[:, 0:REST - 1, :]).then_inc(stored, 16)
                    e.dma_start(out[(NT - 1) * P:N, :], ob[0:LAST, REST - 1, :]).then_inc(stored, 16)

        rounds(e, body)
        e.wait_ge(stored, 16 * (NG + 1))

    @block.scalar
    def _(e):
        e.sem_inc(S["q_taken"], KD)
        e.sem_inc(S["h_taken"], 4)

        def turn_hi(r0, j, turned, hi, dst):
            e.wait_ge(S[turned], r0 * GT + j + 1)
            e.activation(dst[:, 0, :, j * P:(j + 1) * P], pst[j % 2][:, :].rearrange("p (k n) -> p k n", k=KD), ACT.Copy)\
             .then_inc(S[hi], 1)

        def query_hi(r, j):
            n = r * KD + j
            e.wait_ge(S["qn_ready"], n + 1 + KD)
            if not first(r):
                e.wait_ge(S["o_done"], r * GT)
            e.activation(qp[:, 0, j, :], qf[:, j, :], ACT.Copy).then_inc(S["qp_hi"], 1)

        def normed(g, n_x):
            e.wait_ge(x_in, n_x)
            e.wait_ge(x_in2, n_x)
            for j in range(GT):
                e.wait_ge(S["sum_ready"], g * GT + GT)
                s = K["stat"]
                e.activation(xn[:, j, :], xb[:, j, :], ACT.Identity, bias=s[:, bass.ds(g * GT + j, 1), 1],
                             scale=s[:, bass.ds(g * GT + j, 1), 0]).then_inc(S["xn_ready"], 1)

        def query(r, j):
            n = r * KD + j
            e.wait_ge(S["q_done"], n + 1)
            if j >= 2 or not first(r):
                e.wait_ge(S["q_ready"], n - 1)
            e.activation(qz[:, j % 2, :], bank("q", j)[:, :], ACT.Relu, bias=K["bq"][:, j:j + 1]).then_inc(S["qrelu_ready"], 1)
            if j >= 1 or not first(r):
                e.wait_ge(S["q_ready"], n)
            e.activation(qe[:, :], bank("q", j)[:, :], ACT.Exp, bias=K["bq"][:, j:j + 1]).then_inc(S["q_taken"], 1)

        def body(r, a, b, ahead):
            g = r - 1
            for qs, zs in ORDER:
                if a:
                    for j in qs:
                        query(r, j)
                if b:
                    for j in zs:
                        turn_hi(g, j, "z_turned", "zt_hi", zt)
            if b:
                e.wait_ge(S["rt_done"], g + 1)
                e.wait_ge(S["hs_lo"], g * 2 + 2)
                e.activation(lt, pss[0:NE, :], ACT.Copy).then_inc(S["lt_ready"], 1)
                e.wait_ge(S["lg_ready"], g + 1)
                e.activation(pe[:, :, :], lg[:, :, :], ACT.Exp).then_inc(S["re_ready"], 1)
                for j in range(2):
                    e.wait_ge(S["h_done"], g * 2 + j + 1)
                    e.wait_ge(S["hs_lo"], g * 2 + j + 1)
                    e.activation(hg[:, j, :], bank("h", j)[:, :], ACT.Gelu, bias=T["b1"][:, j:j + 1]).then_inc(S["h_taken"], 1)
            if ahead:
                normed(r + 1, (r + 2) * 16)
            if a:
                for j in (0, 1):
                    query_hi(r, j)
            if ahead:
                for j in (0, 1):
                    turn_hi(r + 1, j, "t_turned", "xt_hi", xt)
            if a:
                for j in (2, 3):
                    query_hi(r, j)
            if b:
                for j in range(2):
                    e.wait_ge(S["hg_ready"], g * 2 + j + 1 + 4)
                    if not first(g):
                        e.wait_ge(S["w_done"], g * GT)
                    e.activation(hs[:, 0, j, :], hg[:, j, :], ACT.Copy).then_inc(S["hs_hi"], 1)
            if ahead:
                for j in range(2, GT):
                    turn_hi(r + 1, j, "t_turned", "xt_hi", xt)
            if a:
                e.wait_ge(S["var_ready"], r + 1)
                e.activation(sd[:, :], va[:, :], ACT.Sqrt).then_inc(S["sd_ready"], 1)
                e.wait_ge(S["zs_ready"], r + 1)
                for j in (0, 1):
                    e.activation(xn3[:, j, :], z[:, j, :], ACT.Identity, bias=n3[:, j:j + 1], scale=r3[:, j:j + 1])\
                     .then_inc(S["zn_ready"], 1)

        normed(0, 16)
        for j in range(GT):
            turn_hi(0, j, "t_turned", "xt_hi", xt)
        rounds(e, body)

    @block.vector
    def _(e):
        ca, cb = Chain(e, S["tail_chain"]), Chain(e, S["chain_b"])
        e.sem_inc(S["xt_lo"], GT)
        e.sem_inc(S["zt_lo"], GT)
        e.sem_inc(S["qn_ready"], KD)
        e.sem_inc(S["hg_ready"], 4)
        e.sem_inc(S["z_ready"], GT)
        e.sem_inc(S["r_taken"], 1)
        e.sem_inc(S["c_taken"], 1)
        e.sem_inc(S["gs_lo"], 1)
        cb.link(e.memset(run[:, :], 0.0))
        e.sem_inc(S["out_ready"], 2 * GT)

        def turn_lo(g, j, hi, lo, dst):
            e.wait_ge(S[hi], g * GT + j + 1)
            e.tensor_tensor(dst[:, 1, :, j * P:(j + 1) * P], pst[j % 2][:, :].rearrange("p (k n) -> p k n", k=KD),
                            dst[:, 0, :, j * P:(j + 1) * P].bitcast(f32), ALU.subtract).then_inc(S[lo], 1)

        def body(r, a, b, ahead):
            if isinstance(r, int):
                ca.base, cb.base = r * STEPS_A, (r - 1) * STEPS_B + 1
            else:
                ca.base, cb.base = e.snap(r * STEPS_A), e.snap((r - 1) * STEPS_B + 1)
            ca.n = cb.n = 0
            g = r - 1
            s = K["stat"]
            if a:
                for j in range(GT):
                    n = r * KD + j
                    if j == 0:
                        e.wait_ge(y_in, (r + 1) * 16)
                        e.wait_ge(S["xn_ready"], r * GT + GT)
                        e.wait_ge(S["z_ready"], r * GT + GT)
                    e.scalar_tensor_tensor(t1[:, j, :], xn[:, j, :], s[:, bass.ds(r * GT + j, 1), 2], xb[:, j, :], ALU.mult, ALU.add)\
                     .then_inc(S["sum_a"], 1)
            for qs, zs in ORDER:
                if a:
                    for j in qs:
                        feature(r, j)
                if b:
                    for j in zs:
                        turn_lo(g, j, "zt_hi", "zt_lo", zt)
            if a:
                e.wait_ge(S["m_done"], r + 1)
                e.tensor_scalar(rn[0:NE, :], psc[0:NE, :], 1e-8, None, ALU.add).then_inc(S["m_taken"], 1)
                e.wait_ge(S["m_taken"], r + 1)
                ca.link(e.reciprocal(rn[0:NE, :], rn[0:NE, :]))
                ca.link(e.tensor_copy(rs[:, 0, :], rn[0:NE, :]))
                e.tensor_tensor(rs[:, 1, :], rn[0:NE, :], rs[:, 0, :].bitcast(f32), ALU.subtract).then_inc(S["rs_ready"], 1)
            if b:
                choose(g)
                gates(g)
            if a:
                for j in (0, 1):
                    divide(r, j)
            if b:
                e.wait_ge(S["gt_done"], g + 1)
                e.tensor_copy(gs[:, 0, :], pss[0:NE, 0:GN]).then_inc(S["gs_hi"], 1)
                e.wait_ge(S["gs_hi"], g + 1)
                e.tensor_tensor(gs[:, 1, :], pss[0:NE, 0:GN], gs[:, 0, :].bitcast(f32), ALU.subtract).then_inc(S["gs_lo"], 1)
            if ahead:
                for j in range(2):
                    turn_lo(r + 1, j, "xt_hi", "xt_lo", xt)
            if a:
                for j in (2, 3):
                    divide(r, j)
            if b:
                for j in range(2):
                    e.wait_ge(S["g_done"], g * 2 + j + 1)
                    e.wait_ge(S["h_taken"], g * 2 + j + 1 + 4)
                    e.tensor_tensor(hg[:, j, :], hg[:, j, :], bank("g", j)[:, :], ALU.mult).then_inc(S["hg_ready"], 1)
            if ahead:
                for j in range(2, GT):
                    turn_lo(r + 1, j, "xt_hi", "xt_lo", xt)
            for j in range(GT):
                if b:
                    e.wait_ge(S["w_done"], g * GT + j + 1)
                    if j == 0 and not first(g):
                        e.wait_ge(stored, g * 16)
                    e.tensor_tensor(ob[:, j, :], bank("w", j)[:, :], z[:, j, :], ALU.add).then_inc(S["out_ready"], 1)
                if a:
                    e.wait_ge(S["o_done"], r * GT + j + 1)
                    e.wait_ge(S["sum_ready"], r * GT + j + 1 + GT)
                    if b:
                        e.wait_ge(S["out_ready"], g * GT + 2 * GT + j + 1)
                    e.tensor_tensor(z[:, j, :], bank("o", j)[:, :], t1[:, j, :], ALU.add).then_inc(S["z_ready"], 1)
                    e.wait_ge(S["z_ready"], r * GT + j + 1 + GT)
                    ca.link(e.bn_stats(bn[:, :], z[:, j, :]))
                    e.sem_inc(S["dve_apart"], 1)
                    ca.link(e.bn_aggr(mv[:, j, :], bn[:, :]))
            if a:
                e.tensor_scalar(va[:, :], mv[:, :, 1], LN_EPS, None, ALU.add).then_inc(S["var_ready"], 1)
                e.wait_ge(S["sd_ready"], r + 1)
                ca.link(e.reciprocal(r3[:, :], sd[:, :]))
                e.scalar_tensor_tensor(n3[:, :], mv[:, :, 0], -1.0, r3[:, :], ALU.mult, ALU.mult).then_inc(S["zs_ready"], 1)
            assert ca.n == (STEPS_A if a else 0) and cb.n == (STEPS_B if b else 0), (ca.n, cb.n)

        def divide(r, j):
            e.wait_ge(S["n_done"], r * KD + j + 1)
            e.tensor_tensor(qf[:, j, :], qf[:, j, :], bank("n", j)[:, :], ALU.mult).then_inc(S["qn_ready"], 1)

        def feature(r, j):
            n = r * KD + j
            e.wait_ge(S["qrelu_ready"], n + 1)
            e.wait_ge(S["q_taken"], n + 1 + KD)
            if j == 0:
                e.wait_ge(S["qp_lo"], r * KD + KD)
            e.scalar_tensor_tensor(qf[:, j, :], qe[:, :], 1.0, qz[:, j % 2, :], ALU.min, ALU.add).then_inc(S["q_ready"], 1)

        v = lambda i: t4[:, i, :]
        wide = lambda i: t4[:, i, :].unsqueeze(2).to_broadcast([P, GT, NE])

        def choose(g):
            e.wait_ge(S["r_done"], g + 1)
            e.tensor_tensor(lg[:, :, :], pss[:, 0:GT * NE].rearrange("p (j e) -> p j e", j=GT), T["br"][:, :, :], ALU.add)\
             .then_inc(S["r_taken"], 1)
            e.wait_ge(S["r_taken"], g + 2)
            cb.link(e.tensor_reduce(v(0), lg[:, :, :], axis=AX.X, op=ALU.max))
            e.tensor_tensor(lg[:, :, :], lg[:, :, :], wide(0), ALU.subtract).then_inc(S["lg_ready"], 1)
            e.wait_ge(S["re_ready"], g + 1)
            cb.link(e.reduce_sum(v(1), pe[:, :, :], axis=AX.X))
            cb.link(e.reciprocal(v(1), v(1)))
            cb.link(e.tensor_tensor(pr[:, :, :], pe[:, :, :], wide(1), ALU.mult))
            e.sem_inc(S["dve_apart"], 1)
            for j in range(GT):
                cb.mark(e.max(m8[:, j, :], pr[:, j, :]))
            cb.sync()
            e.sem_inc(S["dve_apart"], 1)
            for j in range(GT):
                cb.mark(e.max_index(i8u[:, j, :], m8[:, j, :], pr[:, j, :]))
            cb.mark(e.tensor_tensor(v(2), m8[:, :, 0], m8[:, :, 1], ALU.add))
            cb.sync()
            cb.mark(e.tensor_copy(i8f[:, :, :], i8u[:, :, :]))
            cb.link(e.tensor_scalar(v(2), v(2), 1e-9, None, ALU.add))
            it8 = T["i8"][:, :].unsqueeze(1).to_broadcast([P, GT, NE])
            cb.mark(e.tensor_tensor(s0[:, :, :], it8, i8f[:, :, 0:1].to_broadcast([P, GT, NE]), ALU.is_equal))
            cb.mark(e.tensor_tensor(s1[:, :, :], it8, i8f[:, :, 1:2].to_broadcast([P, GT, NE]), ALU.is_equal))
            cb.link(e.reciprocal(v(2), v(2)))
            cb.link(e.tensor_tensor(s0[:, :, :], s0[:, :, :], s1[:, :, :], ALU.add))
            e.tensor_copy(sl[:, :, :], s0[:, :, :]).then_inc(S["sel_ready"], 1)
            cb.link(e.tensor_tensor(tw[:, :, :], pr[:, :, :], wide(2), ALU.mult))
            cb.link(e.tensor_tensor(tw[:, :, :], tw[:, :, :], s0[:, :, :], ALU.mult))

        def gates(g):
            e.wait_ge(S["c_done"], g + 1)
            e.wait_ge(S["c_taken"], g + 1)
            cb.link(e.tensor_tensor(po[:, :, :], psc[:, 0:GT * NE].rearrange("p (j e) -> p j e", j=GT),
                                   run[:, :].unsqueeze(1).to_broadcast([P, GT, NE]), ALU.add))
            e.tensor_tensor(run[:, :], run[:, :], psc[:, GT * NE:(GT + 1) * NE], ALU.add).then_inc(S["c_taken"], 1)
            cb.link(e.tensor_scalar(po[:, :, :], po[:, :, :], float(CAP), None, ALU.is_lt))
            cb.link(e.tensor_tensor(tw[:, :, :], tw[:, :, :], po[:, :, :], ALU.mult))
            cb.link(e.reduce_sum(v(3), tw[:, :, :], axis=AX.X))
            cb.link(e.tensor_scalar(v(3), v(3), 1e-9, None, ALU.add))
            cb.link(e.reciprocal(v(3), v(3)))
            e.tensor_tensor(ga[:, :, :], tw[:, :, :], wide(3), ALU.mult).then_inc(S["gate_ready"], 1)

        for j in range(GT):
            turn_lo(0, j, "xt_hi", "xt_lo", xt)
        rounds(e, body)

    @block.tensor
    def _(e):
        PARTS = ((0, 0), (0, 1), (1, 0))

        def turn_x(g, tiles):
            for j in tiles:
                e.wait_ge(S["xn_ready"], g * GT + j + 1)
                if j < 2 and isinstance(g, int) and g == 1:
                    e.wait_ge(S["xt_lo"], GT + j + 3)
                elif j < 2 and not first(g):
                    e.wait_ge(S["zt_lo"], (g - 1) * GT + j + 3)
                elif j >= 2:
                    e.wait_ge(S["xt_lo"], g * GT + j - 1 + GT)
                for k in range(KD):
                    last = e.transpose(pst[j % 2][:, k * P:(k + 1) * P], xn[:, j, k * P:(k + 1) * P], K["ident"][:, :])
                last.then_inc(S["t_turned"], 1)

        def turn_z(g, tiles):
            for j in tiles:
                if j < 2:
                    e.wait_ge(S["zn_ready"], g * 2 + j + 1)
                else:
                    e.wait_ge(S["zn_ready_pool"], g * 2 + j - 1)
                if j < 2 and isinstance(g, int) and g == NG - 1:
                    e.wait_ge(S["zt_lo"], g * GT + j + 3)
                elif j < 2:
                    e.wait_ge(S["xt_lo"], (g + 2) * GT + j + 3)
                else:
                    e.wait_ge(S["zt_lo"], g * GT + j - 1 + GT)
                for k in range(KD):
                    last = e.transpose(pst[j % 2][:, k * P:(k + 1) * P], xn3[:, j, k * P:(k + 1) * P], K["ident"][:, :])
                last.then_inc(S["z_turned"], 1)

        def query(r, j, a, b):
            wait_bank(e, r, "q", j, a, b)
            for k in range(KD):
                for n, (m, w) in enumerate(PARTS):
                    last = e.matmul(bank("q", j)[:, :], wq[:, w, k, j * P:(j + 1) * P], xt[:, m, k, :],
                                    start=(k == 0 and n == 0), stop=(k == KD - 1 and n == 2))
            last.then_inc(S["q_done"], 1)

        def hidden(r, j, a, b):
            wait_bank(e, r, "h", j, a, b)
            for k in range(KD):
                for n, (m, w) in enumerate(PARTS):
                    last = e.matmul(bank("h", j)[:, :], T["w1"][:, w, k, j * P:(j + 1) * P], zt[:, m, k, :],
                                    start=(k == 0 and n == 0), stop=(k == KD - 1 and n == 2))
            last.then_inc(S["h_done"], 1)

        def spread_norm(r, j, a, b):
            wait_bank(e, r, "n", j, a, b)
            e.wait_ge(S["rs_ready"], r + 1)
            for n in range(2):
                last = e.matmul(bank("n", j)[:, :], T["head"][:, j * P:(j + 1) * P], rs[:, n, :], start=(n == 0), stop=(n == 1))
            last.then_inc(S["n_done"], 1)

        def body(r, a, b, ahead):
            g = r - 1
            if a:
                e.wait_ge(S["xt_lo"], r * GT + 2 * GT)
                for j in range(3):
                    query(r, j, a, b)
            if b:
                turn_z(g, (0, 1))
            if a:
                query(r, 3, a, b)
            if b:
                turn_z(g, (2, 3))
            if a:
                if not first(r):
                    e.wait_ge(S["c_taken"], r)
                for k in range(KD):
                    e.wait_ge(S["q_ready"], r * KD + k + 1)
                    last = e.matmul(psc[0:NE, :], T["ks"][:, k, :], qf[:, k, :], start=(k == 0), stop=(k == KD - 1))
                last.then_inc(S["m_done"], 1)
            if b:
                e.wait_ge(S["gs_lo"], g + 1)
                e.wait_ge(S["zt_lo"], g * GT + 2 * GT)
                for k in range(KD):
                    for n, (m, w) in enumerate(PARTS):
                        last = e.matmul(pss[0:NE, :], T["wr"][:, w, k, :], zt[:, m, k, :],
                                        start=(k == 0 and n == 0), stop=(k == KD - 1 and n == 2))
                last.then_inc(S["rt_done"], 1)
                hidden(r, 0, a, b)
                wait_apart(e, S["lt_ready"], g + 1, S["pe_apart_t"])
                for j in range(GT):
                    last = e.transpose(pss[:, j * NE:(j + 1) * NE], lt[:, j * P:(j + 1) * P], K["ident"][0:NE, 0:NE])
                last.then_inc(S["r_done"], 1)
                hidden(r, 1, a, b)
            if a:
                for j in (0, 1):
                    spread_norm(r, j, a, b)
            if b:
                e.wait_ge(S["sel_ready"], g + 1)
                if a:
                    e.wait_ge(S["m_taken"], r + 1)
                for j in range(GT + 1):
                    before = range(j)
                    o = psc[:, j * NE:(j + 1) * NE]
                    for i in before:
                        last = e.matmul(o, T["one"][:, :], sl[:, i, :], start=(i == 0), stop=(j == GT and i == GT - 1))
                    if j < GT:
                        last = e.matmul(o, T["tri"][:, :], sl[:, j, :], start=(j == 0), stop=True)
                last.then_inc(S["c_done"], 1)
            if a:
                for j in (2, 3):
                    spread_norm(r, j, a, b)
            if ahead:
                turn_x(r + 1, (0, 1))
            if b:
                e.wait_ge(S["gate_ready"], g + 1)
                e.wait_ge(S["r_taken"], g + 2)
                for j in range(GT):
                    last = e.transpose(pss[0:NE, j * P:(j + 1) * P], ga[:, j, :], K["ident"][:, :])
                last.then_inc(S["gt_done"], 1)
                for j in range(2):
                    wait_bank(e, r, "g", j, a, b)
                    for n in range(2):
                        e.wait_ge(S[("gs_hi", "gs_lo")[n]], g + 1 + n)
                        last = e.matmul(bank("g", j)[:, :], T["sel"][:, j * P:(j + 1) * P], gs[:, n, :], start=(n == 0), stop=(n == 1))
                    last.then_inc(S["g_done"], 1)
            if ahead:
                turn_x(r + 1, (2, 3))
            for kind, j in MIXED:
                if a and kind == "o":
                    wait_bank(e, r, "o", j, a, b)
                    for k in range(KD):
                        if j == 0:
                            e.wait_ge(S["qp_lo"], r * KD + k + 1 + KD)
                        for n, (m, w) in enumerate(PARTS):
                            last = e.matmul(bank("o", j)[:, :], qp[:, m, k, j * P:(j + 1) * P], T["mw"][:, w, k, :],
                                            start=(k == 0 and n == 0), stop=(k == KD - 1 and n == 2))
                    last.then_inc(S["o_done"], 1)
                if b and kind == "w":
                    wait_bank(e, r, "w", j, a, b)
                    wait_apart(e, S["hs_lo"], g * 2 + 4, S["pe_apart_t"])
                    t = slice(j * P, (j + 1) * P)
                    for n, (m, w) in enumerate(PARTS):
                        e.matmul(bank("w", j)[:, :], gs[:, m, t], T["b2"][:, w, :], start=(n == 0), stop=False)
                    for k in range(2):
                        for n, (m, w) in enumerate(PARTS):
                            last = e.matmul(bank("w", j)[:, :], hs[:, m, k, t], T["w2"][:, w, k, :],
                                            start=False, stop=(k == 1 and n == 2))
                    last.then_inc(S["w_done"], 1)

        turn_x(0, range(GT))
        rounds(e, body)


STEPS_A, STEPS_B = 11, 27


_INS = ['x', 'src', 'dst', 'L0_gnn_W1', 'L0_gnn_a_src1', 'L0_gnn_a_dst1', 'L0_gnn_b1', 'L0_gnn_W2', 'L0_gnn_a_src2',
        'L0_gnn_a_dst2', 'L0_gnn_b2', 'L0_gnn_Wfc', 'L0_gnn_bfc', 'L0_mix_qkv_w', 'L0_mix_qkv_b', 'L0_mix_out_w',
        'L0_mix_out_b', 'L0_mix_ln_gamma', 'L0_mix_ln_beta', 'L0_ffn_Wr', 'L0_ffn_br', 'L0_ffn_W1', 'L0_ffn_b1',
        'L0_ffn_W2', 'L0_ffn_b2']


def kernel(**inputs):
    import numpy as _np
    import concourse.bacc as _bacc
    from concourse import mybir as _mybir
    from concourse.bass_utils import run_bass_kernel_spmd as _run

    nc = _bacc.Bacc("TRN2", target_bir_lowering=False, num_devices=1)
    arrays, args = {}, []
    for name in _INS:
        a = _np.ascontiguousarray(inputs[name])
        arrays[f"in_{name}_dram"] = a
        args.append(nc.dram_tensor(f"in_{name}_dram", a.shape, _mybir.dt.from_np(a.dtype), kind="ExternalInput").ap())
    args.append(nc.dram_tensor("out_0_dram", (N, D), f32, kind="ExternalOutput").ap())
    build(nc, *args)
    r = _run(nc, [arrays], core_ids=[0])
    return r.results[0]["out_0_dram"]
```
